# Optimizing a Trainium2 kernel written in Bass

```python
import numpy as np
import jax
import jax.numpy as jnp

def _softmax(x, axis=-1):
    return jax.nn.softmax(x, axis=axis)

def _gelu(x):
    return jax.nn.gelu(x, approximate=True)

def _silu(x):
    return jax.nn.silu(x)

def _sigmoid(x):
    return jax.nn.sigmoid(x)

def _layernorm(x, axis=-1, eps=1e-05):
    m = jnp.mean(x, axis=axis, keepdims=True)
    v = jnp.var(x, axis=axis, keepdims=True)
    return (x - m) / jnp.sqrt(v + eps)

def _scatter_add(tgt, idx, src, axis=0):
    return tgt.at[idx].add(src)

def _segment_sum(src, seg, n):
    return jax.ops.segment_sum(src, seg, n)
kernel_name = 'mk_prb_d2_jaxref_r8_8d9972'

def setup_inputs(seed: int=0):
    np.random.seed(seed)
    _w = jnp.asarray

    def _L0_attn_setup():
        import jax, jax.numpy as jnp
        import numpy as np
        N_EMBD = 128
        N_HEAD = 16
        HEAD_DIM = N_EMBD // N_HEAD
        BLOCK = 64
        SCALE = HEAD_DIM ** (-0.5)

        def _flash(q, k, v):
            BH, T, D = q.shape
            nb = T // BLOCK
            qb = q.reshape(BH, nb, BLOCK, D).transpose(1, 0, 2, 3)
            kb = k.reshape(BH, nb, BLOCK, D).transpose(1, 0, 2, 3)
            vb = v.reshape(BH, nb, BLOCK, D).transpose(1, 0, 2, 3)
            row = jnp.arange(BLOCK)

            def per_qblock(i, q_i):
                qpos = i * BLOCK + row[:, None]

                def step(carry, jkv):
                    m, l, o = carry
                    j, k_j, v_j = jkv
                    s = jnp.einsum('bqd,bkd->bqk', q_i, k_j) * SCALE
                    kpos = j * BLOCK + row[None, :]
                    s = jnp.where(kpos > qpos, -jnp.inf, s)
                    m_new = jnp.maximum(m, s.max(-1))
                    p = jnp.exp(s - m_new[..., None])
                    l_new = l * jnp.exp(m - m_new) + p.sum(-1)
                    ob = jnp.einsum('bqk,bkd->bqd', p, v_j)
                    o = o + (ob - o) * (l / l_new)[..., None]
                    return ((m_new, l_new, o), None)
                init = (jnp.full((BH, BLOCK), -jnp.inf, q.dtype), jnp.zeros((BH, BLOCK), q.dtype), jnp.zeros_like(q_i))
                (m, l, o), _ = jax.lax.scan(step, init, (jnp.arange(nb), kb, vb))
                return o / l[..., None]
            out = jax.vmap(per_qblock)(jnp.arange(nb), qb)
            return out.transpose(1, 0, 2, 3).reshape(BH, T, D)
        key = jax.random.key(seed)
        ks = jax.random.split(key, 4)
        x = jax.random.normal(ks[0], (4, 512, N_EMBD), jnp.float32)
        qkv_w = jax.random.normal(ks[1], (3 * N_EMBD, N_EMBD), jnp.float32) * 0.02
        qkv_b = jnp.zeros((3 * N_EMBD,), jnp.float32)
        proj_w = jax.random.normal(ks[2], (N_EMBD, N_EMBD), jnp.float32) * 0.02
        proj_b = jnp.zeros((N_EMBD,), jnp.float32)
        return {'x': x, 'qkv_w': qkv_w, 'qkv_b': qkv_b, 'proj_w': proj_w, 'proj_b': proj_b}
    _L0_attn_in = _L0_attn_setup()

    def _L0_ffn_setup():
        import jax, jax.numpy as jnp
        import numpy as np
        D_MODEL = 128
        D_FF = 512
        NUM_EXPERTS = 8
        B, N = (16, 128)
        key = jax.random.key(seed)
        ks = jax.random.split(key, 7)
        s_in = 1.0 / np.sqrt(D_MODEL)
        s_ff = 1.0 / np.sqrt(D_FF)
        return {'x': jax.random.normal(ks[0], (B, N, D_MODEL), dtype=jnp.float32), 'Wr': jax.random.uniform(ks[1], (D_MODEL, NUM_EXPERTS), jnp.float32, -s_in, s_in), 'br': jax.random.uniform(ks[2], (NUM_EXPERTS,), jnp.float32, -s_in, s_in), 'W1': jax.random.uniform(ks[3], (NUM_EXPERTS, D_MODEL, D_FF), jnp.float32, -s_in, s_in), 'b1': jax.random.uniform(ks[4], (NUM_EXPERTS, D_FF), jnp.float32, -s_in, s_in), 'W2': jax.random.uniform(ks[5], (NUM_EXPERTS, D_FF, D_MODEL), jnp.float32, -s_ff, s_ff), 'b2': jax.random.uniform(ks[6], (NUM_EXPERTS, D_MODEL), jnp.float32, -s_ff, s_ff)}
    _L0_ffn_in = _L0_ffn_setup()

    def _L1_attn_setup():
        import jax, jax.numpy as jnp
        import numpy as np
        D_MODEL, H, DK, DV, R, C, KW = (128, 16, 64, 64, 64, 64, 4)
        ALPHA_MIN, BETA_MAX, EPS = (0.1, 1.0, 1e-06)

        def _shortconv(x, w, b):
            y = jax.lax.conv_general_dilated(x.transpose(0, 2, 1), w, (1,), [(KW - 1, 0)], feature_group_count=w.shape[0], dimension_numbers=('NCH', 'OIH', 'NCH'))
            y = y + b[None, :, None]
            return jax.nn.silu(y).transpose(0, 2, 1)

        def _l2n(x):
            return x / jnp.sqrt(jnp.maximum(jnp.sum(x * x, -1, keepdims=True), EPS))

        def _forward(x, wq_conv, bq_conv, wk_conv, bk_conv, wv_conv, bv_conv, Wq, bq, Wk, bk, Wv, bv, Wad, bad, Wau, bau, Wbeta, bbeta, rms_w, Wgd, bgd, Wgu, bgu, Wo, bo):
            B, T, D = x.shape
            BH = B * H
            Q = (_shortconv(x, wq_conv, bq_conv) @ Wq.T + bq).reshape(B, T, H, DK).transpose(0, 2, 1, 3)
            K = (_shortconv(x, wk_conv, bk_conv) @ Wk.T + bk).reshape(B, T, H, DK).transpose(0, 2, 1, 3)
            V = (_shortconv(x, wv_conv, bv_conv) @ Wv.T + bv).reshape(B, T, H, DV).transpose(0, 2, 1, 3)
            Q, K = (_l2n(Q), _l2n(K))
            alpha = jax.nn.sigmoid(jax.nn.silu(x @ Wad.T + bad) @ Wau.T + bau)
            alpha = alpha.reshape(B, T, H, DK).transpose(0, 2, 1, 3).reshape(BH, T, DK)
            alpha = jnp.clip(alpha, ALPHA_MIN, 1.0)
            beta = jax.nn.sigmoid(x @ Wbeta.T + bbeta).transpose(0, 2, 1).reshape(BH, T, 1)
            beta = jnp.minimum(beta, BETA_MAX)
            Qf = Q.reshape(BH, T, DK)
            Kf = K.reshape(BH, T, DK)
            Vf = V.reshape(BH, T, DV)
            N = T // C
            Qc = Qf.reshape(BH, N, C, DK).transpose(1, 0, 2, 3)
            Kc = Kf.reshape(BH, N, C, DK).transpose(1, 0, 2, 3)
            Vc = Vf.reshape(BH, N, C, DV).transpose(1, 0, 2, 3)
            Ac = alpha.reshape(BH, N, C, DK).transpose(1, 0, 2, 3)
            Bc = beta.reshape(BH, N, C, 1).transpose(1, 0, 2, 3)
            mask = jnp.tril(jnp.ones((C, C), bool))

            def chunk_step(S, inp):
                qc, kc, vc, ac, bc = inp
                O_inter = jnp.einsum('bcd,bde->bce', qc, S)
                cl = jnp.cumsum(jnp.log(jnp.maximum(ac, 1e-07)), axis=1)
                cum = jnp.exp(cl[:, :, None, :] - cl[:, None, :, :]) * mask[None, :, :, None]
                A = jnp.einsum('bid,bijd,bjd->bij', qc, cum, kc * bc)
                O = O_inter + jnp.einsum('bij,bje->bie', A, vc)

                def step(S, t):
                    k_t, v_t, a_t, b_t = t
                    S = S * a_t[:, :, None]
                    kTS = jnp.einsum('bd,bde->be', k_t, S)
                    S = S + (b_t * k_t)[:, :, None] * (v_t - kTS)[:, None, :]
                    return (S, None)
                S, _ = jax.lax.scan(step, S, (kc.transpose(1, 0, 2), vc.transpose(1, 0, 2), ac.transpose(1, 0, 2), bc.transpose(1, 0, 2)))
                return (S, O)
            S0 = jnp.zeros((BH, DK, DV), x.dtype)
            _, Oc = jax.lax.scan(chunk_step, S0, (Qc, Kc, Vc, Ac, Bc))
            O = Oc.transpose(1, 0, 2, 3).reshape(B, H, T, DV)
            var = jnp.mean(O * O, -1, keepdims=True)
            O = O * jax.lax.rsqrt(var + EPS) * rms_w[None, :, None, :]
            g = jax.nn.sigmoid(jax.nn.silu(x @ Wgd.T + bgd) @ Wgu.T + bgu)
            O = O * g.transpose(0, 2, 1)[..., None]
            out = O.transpose(0, 2, 1, 3).reshape(B, T, H * DV) @ Wo.T + bo
            return out
        key = jax.random.key(seed)
        ks = iter(jax.random.split(key, 32))
        s = 0.02
        d = {'x': jax.random.normal(next(ks), (2, 256, D_MODEL), jnp.float32)}
        for p in ('q', 'k', 'v'):
            d[f'w{p}_conv'] = jax.random.normal(next(ks), (D_MODEL, 1, KW), jnp.float32) * s
            d[f'b{p}_conv'] = jnp.zeros((D_MODEL,), jnp.float32)
        d['Wq'] = jax.random.normal(next(ks), (H * DK, D_MODEL), jnp.float32) * s
        d['bq'] = jnp.zeros((H * DK,), jnp.float32)
        d['Wk'] = jax.random.normal(next(ks), (H * DK, D_MODEL), jnp.float32) * s
        d['bk'] = jnp.zeros((H * DK,), jnp.float32)
        d['Wv'] = jax.random.normal(next(ks), (H * DV, D_MODEL), jnp.float32) * s
        d['bv'] = jnp.zeros((H * DV,), jnp.float32)
        d['Wad'] = jax.random.normal(next(ks), (R, D_MODEL), jnp.float32) * s
        d['bad'] = jnp.zeros((R,), jnp.float32)
        d['Wau'] = jax.random.normal(next(ks), (H * DK, R), jnp.float32) * s
        d['bau'] = jnp.zeros((H * DK,), jnp.float32)
        d['Wbeta'] = jax.random.normal(next(ks), (H, D_MODEL), jnp.float32) * s
        d['bbeta'] = jnp.zeros((H,), jnp.float32)
        d['rms_w'] = jnp.ones((H, DV), jnp.float32)
        d['Wgd'] = jax.random.normal(next(ks), (R, D_MODEL), jnp.float32) * s
        d['bgd'] = jnp.zeros((R,), jnp.float32)
        d['Wgu'] = jax.random.normal(next(ks), (H, R), jnp.float32) * s
        d['bgu'] = jnp.zeros((H,), jnp.float32)
        d['Wo'] = jax.random.normal(next(ks), (D_MODEL, H * DV), jnp.float32) * s
        d['bo'] = jnp.zeros((D_MODEL,), jnp.float32)
        return d
    _L1_attn_in = _L1_attn_setup()

    def _L1_ffn_setup():
        import jax, jax.numpy as jnp
        import numpy as np
        E = 16
        K = 4
        G = 4
        TG = 2
        NS = 2
        H = 128
        I = 176
        SCALE = 1.0

        def _gate(x2d, gate_w, gate_bias):
            T = x2d.shape[0]
            logits = x2d.astype(jnp.float32) @ gate_w.astype(jnp.float32).T
            scores = jax.nn.sigmoid(logits)
            sfc = scores + gate_bias[None, :]
            grp = sfc.reshape(T, G, E // G)
            top2, _ = jax.lax.top_k(grp, 2)
            group_scores = top2.sum(-1)
            _, gidx = jax.lax.top_k(group_scores, TG)
            gmask = jnp.zeros((T, G), sfc.dtype).at[jnp.arange(T)[:, None], gidx].set(1.0)
            smask = jnp.repeat(gmask, E // G, axis=1) > 0
            tmp = jnp.where(smask, sfc, 0.0)
            _, topk_idx = jax.lax.top_k(tmp, K)
            topk_w = jnp.take_along_axis(scores, topk_idx, axis=1)
            topk_w = topk_w / (topk_w.sum(-1, keepdims=True) + 1e-20)
            return (topk_idx, topk_w * SCALE)
        key = jax.random.key(seed)
        ks = jax.random.split(key, 8)
        bound = 1.0 / np.sqrt(H)
        return {'hidden_states': jax.random.normal(ks[0], (1, 128, H), jnp.float32), 'gate_w': jax.random.uniform(ks[1], (E, H), jnp.float32, -bound, bound), 'gate_bias': jnp.zeros((E,), jnp.float32), 'gate_proj': jax.random.normal(ks[2], (E, I, H), jnp.float32) * 0.02, 'up_proj': jax.random.normal(ks[3], (E, I, H), jnp.float32) * 0.02, 'down_proj': jax.random.normal(ks[4], (E, H, I), jnp.float32) * 0.02, 'shared_gate_w': jax.random.normal(ks[5], (I * NS, H), jnp.float32) * 0.02, 'shared_up_w': jax.random.normal(ks[6], (I * NS, H), jnp.float32) * 0.02, 'shared_down_w': jax.random.normal(ks[7], (H, I * NS), jnp.float32) * 0.02}
    _L1_ffn_in = _L1_ffn_setup()
    _d = {'L0_attn_x': _L0_attn_in['x'], 'L0_attn_qkv_w': _L0_attn_in['qkv_w'], 'L0_attn_qkv_b': _L0_attn_in['qkv_b'], 'L0_attn_proj_w': _L0_attn_in['proj_w'], 'L0_attn_proj_b': _L0_attn_in['proj_b'], 'L0_ffn_Wr': _L0_ffn_in['Wr'], 'L0_ffn_br': _L0_ffn_in['br'], 'L0_ffn_W1': _L0_ffn_in['W1'], 'L0_ffn_b1': _L0_ffn_in['b1'], 'L0_ffn_W2': _L0_ffn_in['W2'], 'L0_ffn_b2': _L0_ffn_in['b2'], 'L1_attn_wq_conv': _L1_attn_in['wq_conv'], 'L1_attn_bq_conv': _L1_attn_in['bq_conv'], 'L1_attn_wk_conv': _L1_attn_in['wk_conv'], 'L1_attn_bk_conv': _L1_attn_in['bk_conv'], 'L1_attn_wv_conv': _L1_attn_in['wv_conv'], 'L1_attn_bv_conv': _L1_attn_in['bv_conv'], 'L1_attn_Wq': _L1_attn_in['Wq'], 'L1_attn_bq': _L1_attn_in['bq'], 'L1_attn_Wk': _L1_attn_in['Wk'], 'L1_attn_bk': _L1_attn_in['bk'], 'L1_attn_Wv': _L1_attn_in['Wv'], 'L1_attn_bv': _L1_attn_in['bv'], 'L1_attn_Wad': _L1_attn_in['Wad'], 'L1_attn_bad': _L1_attn_in['bad'], 'L1_attn_Wau': _L1_attn_in['Wau'], 'L1_attn_bau': _L1_attn_in['bau'], 'L1_attn_Wbeta': _L1_attn_in['Wbeta'], 'L1_attn_bbeta': _L1_attn_in['bbeta'], 'L1_attn_rms_w': _L1_attn_in['rms_w'], 'L1_attn_Wgd': _L1_attn_in['Wgd'], 'L1_attn_bgd': _L1_attn_in['bgd'], 'L1_attn_Wgu': _L1_attn_in['Wgu'], 'L1_attn_bgu': _L1_attn_in['bgu'], 'L1_attn_Wo': _L1_attn_in['Wo'], 'L1_attn_bo': _L1_attn_in['bo'], 'L1_ffn_gate_w': _L1_ffn_in['gate_w'], 'L1_ffn_gate_bias': _L1_ffn_in['gate_bias'], 'L1_ffn_gate_proj': _L1_ffn_in['gate_proj'], 'L1_ffn_up_proj': _L1_ffn_in['up_proj'], 'L1_ffn_down_proj': _L1_ffn_in['down_proj'], 'L1_ffn_shared_gate_w': _L1_ffn_in['shared_gate_w'], 'L1_ffn_shared_up_w': _L1_ffn_in['shared_up_w'], 'L1_ffn_shared_down_w': _L1_ffn_in['shared_down_w']}
    _x0 = _d['L0_attn_x']
    _d['L0_attn_x'] = jax.random.normal(jax.random.fold_in(jax.random.key(seed), 1), (4, 1024, 128), dtype=_x0.dtype)
    del _x0
    return _d

def reference(L0_attn_x, L0_attn_qkv_w, L0_attn_qkv_b, L0_attn_proj_w, L0_attn_proj_b, L0_ffn_Wr, L0_ffn_br, L0_ffn_W1, L0_ffn_b1, L0_ffn_W2, L0_ffn_b2, L1_attn_wq_conv, L1_attn_bq_conv, L1_attn_wk_conv, L1_attn_bk_conv, L1_attn_wv_conv, L1_attn_bv_conv, L1_attn_Wq, L1_attn_bq, L1_attn_Wk, L1_attn_bk, L1_attn_Wv, L1_attn_bv, L1_attn_Wad, L1_attn_bad, L1_attn_Wau, L1_attn_bau, L1_attn_Wbeta, L1_attn_bbeta, L1_attn_rms_w, L1_attn_Wgd, L1_attn_bgd, L1_attn_Wgu, L1_attn_bgu, L1_attn_Wo, L1_attn_bo, L1_ffn_gate_w, L1_ffn_gate_bias, L1_ffn_gate_proj, L1_ffn_up_proj, L1_ffn_down_proj, L1_ffn_shared_gate_w, L1_ffn_shared_up_w, L1_ffn_shared_down_w):

    def _L0_attn_ref(x, qkv_w, qkv_b, proj_w, proj_b):
        import jax, jax.numpy as jnp
        import numpy as np
        N_EMBD = 128
        N_HEAD = 16
        HEAD_DIM = N_EMBD // N_HEAD
        BLOCK = 64
        SCALE = HEAD_DIM ** (-0.5)

        def _flash(q, k, v):
            BH, T, D = q.shape
            nb = T // BLOCK
            qb = q.reshape(BH, nb, BLOCK, D).transpose(1, 0, 2, 3)
            kb = k.reshape(BH, nb, BLOCK, D).transpose(1, 0, 2, 3)
            vb = v.reshape(BH, nb, BLOCK, D).transpose(1, 0, 2, 3)
            row = jnp.arange(BLOCK)

            def per_qblock(i, q_i):
                qpos = i * BLOCK + row[:, None]

                def step(carry, jkv):
                    m, l, o = carry
                    j, k_j, v_j = jkv
                    s = jnp.einsum('bqd,bkd->bqk', q_i, k_j) * SCALE
                    kpos = j * BLOCK + row[None, :]
                    s = jnp.where(kpos > qpos, -jnp.inf, s)
                    m_new = jnp.maximum(m, s.max(-1))
                    p = jnp.exp(s - m_new[..., None])
                    l_new = l * jnp.exp(m - m_new) + p.sum(-1)
                    ob = jnp.einsum('bqk,bkd->bqd', p, v_j)
                    o = o + (ob - o) * (l / l_new)[..., None]
                    return ((m_new, l_new, o), None)
                init = (jnp.full((BH, BLOCK), -jnp.inf, q.dtype), jnp.zeros((BH, BLOCK), q.dtype), jnp.zeros_like(q_i))
                (m, l, o), _ = jax.lax.scan(step, init, (jnp.arange(nb), kb, vb))
                return o / l[..., None]
            out = jax.vmap(per_qblock)(jnp.arange(nb), qb)
            return out.transpose(1, 0, 2, 3).reshape(BH, T, D)
        b, t, c = x.shape
        qkv = (x @ qkv_w.T + qkv_b).reshape(b, t, 3, N_HEAD, HEAD_DIM)
        q, k, v = (qkv[:, :, 0], qkv[:, :, 1], qkv[:, :, 2])

        def to_bh(a):
            return a.transpose(0, 2, 1, 3).reshape(b * N_HEAD, t, HEAD_DIM)
        o = _flash(to_bh(q), to_bh(k), to_bh(v))
        o = o.reshape(b, N_HEAD, t, HEAD_DIM).transpose(0, 2, 1, 3).reshape(b, t, c)
        return o @ proj_w.T + proj_b

    def _L0_ffn_ref(x, Wr, br, W1, b1, W2, b2):
        import jax, jax.numpy as jnp
        import numpy as np
        D_MODEL = 128
        D_FF = 512
        NUM_EXPERTS = 8
        B, N = (16, 128)
        scores = jnp.einsum('bh,he->be', x.mean(axis=1), Wr) + br
        top1 = jnp.argmax(scores, axis=-1)
        w1 = W1[top1]
        c1 = b1[top1]
        w2 = W2[top1]
        c2 = b2[top1]
        h = jax.nn.relu(jnp.einsum('bnh,bhf->bnf', x, w1) + c1[:, None, :])
        out = jnp.einsum('bnf,bfh->bnh', h, w2) + c2[:, None, :]
        return out

    def _L1_attn_ref(x, wq_conv, bq_conv, wk_conv, bk_conv, wv_conv, bv_conv, Wq, bq, Wk, bk, Wv, bv, Wad, bad, Wau, bau, Wbeta, bbeta, rms_w, Wgd, bgd, Wgu, bgu, Wo, bo):
        import jax, jax.numpy as jnp
        import numpy as np
        D_MODEL, H, DK, DV, R, C, KW = (128, 16, 64, 64, 64, 64, 4)
        ALPHA_MIN, BETA_MAX, EPS = (0.1, 1.0, 1e-06)

        def _shortconv(x, w, b):
            y = jax.lax.conv_general_dilated(x.transpose(0, 2, 1), w, (1,), [(KW - 1, 0)], feature_group_count=w.shape[0], dimension_numbers=('NCH', 'OIH', 'NCH'))
            y = y + b[None, :, None]
            return jax.nn.silu(y).transpose(0, 2, 1)

        def _l2n(x):
            return x / jnp.sqrt(jnp.maximum(jnp.sum(x * x, -1, keepdims=True), EPS))

        def _forward(x, wq_conv, bq_conv, wk_conv, bk_conv, wv_conv, bv_conv, Wq, bq, Wk, bk, Wv, bv, Wad, bad, Wau, bau, Wbeta, bbeta, rms_w, Wgd, bgd, Wgu, bgu, Wo, bo):
            B, T, D = x.shape
            BH = B * H
            Q = (_shortconv(x, wq_conv, bq_conv) @ Wq.T + bq).reshape(B, T, H, DK).transpose(0, 2, 1, 3)
            K = (_shortconv(x, wk_conv, bk_conv) @ Wk.T + bk).reshape(B, T, H, DK).transpose(0, 2, 1, 3)
            V = (_shortconv(x, wv_conv, bv_conv) @ Wv.T + bv).reshape(B, T, H, DV).transpose(0, 2, 1, 3)
            Q, K = (_l2n(Q), _l2n(K))
            alpha = jax.nn.sigmoid(jax.nn.silu(x @ Wad.T + bad) @ Wau.T + bau)
            alpha = alpha.reshape(B, T, H, DK).transpose(0, 2, 1, 3).reshape(BH, T, DK)
            alpha = jnp.clip(alpha, ALPHA_MIN, 1.0)
            beta = jax.nn.sigmoid(x @ Wbeta.T + bbeta).transpose(0, 2, 1).reshape(BH, T, 1)
            beta = jnp.minimum(beta, BETA_MAX)
            Qf = Q.reshape(BH, T, DK)
            Kf = K.reshape(BH, T, DK)
            Vf = V.reshape(BH, T, DV)
            N = T // C
            Qc = Qf.reshape(BH, N, C, DK).transpose(1, 0, 2, 3)
            Kc = Kf.reshape(BH, N, C, DK).transpose(1, 0, 2, 3)
            Vc = Vf.reshape(BH, N, C, DV).transpose(1, 0, 2, 3)
            Ac = alpha.reshape(BH, N, C, DK).transpose(1, 0, 2, 3)
            Bc = beta.reshape(BH, N, C, 1).transpose(1, 0, 2, 3)
            mask = jnp.tril(jnp.ones((C, C), bool))

            def chunk_step(S, inp):
                qc, kc, vc, ac, bc = inp
                O_inter = jnp.einsum('bcd,bde->bce', qc, S)
                cl = jnp.cumsum(jnp.log(jnp.maximum(ac, 1e-07)), axis=1)
                cum = jnp.exp(cl[:, :, None, :] - cl[:, None, :, :]) * mask[None, :, :, None]
                A = jnp.einsum('bid,bijd,bjd->bij', qc, cum, kc * bc)
                O = O_inter + jnp.einsum('bij,bje->bie', A, vc)

                def step(S, t):
                    k_t, v_t, a_t, b_t = t
                    S = S * a_t[:, :, None]
                    kTS = jnp.einsum('bd,bde->be', k_t, S)
                    S = S + (b_t * k_t)[:, :, None] * (v_t - kTS)[:, None, :]
                    return (S, None)
                S, _ = jax.lax.scan(step, S, (kc.transpose(1, 0, 2), vc.transpose(1, 0, 2), ac.transpose(1, 0, 2), bc.transpose(1, 0, 2)))
                return (S, O)
            S0 = jnp.zeros((BH, DK, DV), x.dtype)
            _, Oc = jax.lax.scan(chunk_step, S0, (Qc, Kc, Vc, Ac, Bc))
            O = Oc.transpose(1, 0, 2, 3).reshape(B, H, T, DV)
            var = jnp.mean(O * O, -1, keepdims=True)
            O = O * jax.lax.rsqrt(var + EPS) * rms_w[None, :, None, :]
            g = jax.nn.sigmoid(jax.nn.silu(x @ Wgd.T + bgd) @ Wgu.T + bgu)
            O = O * g.transpose(0, 2, 1)[..., None]
            out = O.transpose(0, 2, 1, 3).reshape(B, T, H * DV) @ Wo.T + bo
            return out
        return _forward(x, wq_conv, bq_conv, wk_conv, bk_conv, wv_conv, bv_conv, Wq, bq, Wk, bk, Wv, bv, Wad, bad, Wau, bau, Wbeta, bbeta, rms_w, Wgd, bgd, Wgu, bgu, Wo, bo)

    def _L1_ffn_ref(hidden_states, gate_w, gate_bias, gate_proj, up_proj, down_proj, shared_gate_w, shared_up_w, shared_down_w):
        import jax, jax.numpy as jnp
        import numpy as np
        E = 16
        K = 4
        G = 4
        TG = 2
        NS = 2
        H = 128
        I = 176
        SCALE = 1.0

        def _gate(x2d, gate_w, gate_bias):
            T = x2d.shape[0]
            logits = x2d.astype(jnp.float32) @ gate_w.astype(jnp.float32).T
            scores = jax.nn.sigmoid(logits)
            sfc = scores + gate_bias[None, :]
            grp = sfc.reshape(T, G, E // G)
            top2, _ = jax.lax.top_k(grp, 2)
            group_scores = top2.sum(-1)
            _, gidx = jax.lax.top_k(group_scores, TG)
            gmask = jnp.zeros((T, G), sfc.dtype).at[jnp.arange(T)[:, None], gidx].set(1.0)
            smask = jnp.repeat(gmask, E // G, axis=1) > 0
            tmp = jnp.where(smask, sfc, 0.0)
            _, topk_idx = jax.lax.top_k(tmp, K)
            topk_w = jnp.take_along_axis(scores, topk_idx, axis=1)
            topk_w = topk_w / (topk_w.sum(-1, keepdims=True) + 1e-20)
            return (topk_idx, topk_w * SCALE)
        orig_shape = hidden_states.shape
        x = hidden_states.reshape(-1, H)
        topk_idx, topk_w = _gate(x, gate_w, gate_bias)
        combine_w = (jax.nn.one_hot(topk_idx, E, dtype=x.dtype) * topk_w[..., None]).sum(1)
        g = jnp.einsum('th,eih->tei', x, gate_proj)
        u = jnp.einsum('th,eih->tei', x, up_proj)
        act = jax.nn.silu(g) * u
        y = jnp.einsum('tei,ehi,te->th', act, down_proj, combine_w)
        sg = x @ shared_gate_w.T
        su = x @ shared_up_w.T
        y = y + jax.nn.silu(sg) * su @ shared_down_w.T
        return y.reshape(orig_shape)
    x = L0_attn_x
    xn = _layernorm(x, axis=-1)
    x = x + _L0_attn_ref(xn, L0_attn_qkv_w, L0_attn_qkv_b, L0_attn_proj_w, L0_attn_proj_b) + _L0_ffn_ref(xn, L0_ffn_Wr, L0_ffn_br, L0_ffn_W1, L0_ffn_b1, L0_ffn_W2, L0_ffn_b2)
    xn = _layernorm(x, axis=-1)
    x = x + _L1_attn_ref(xn, L1_attn_wq_conv, L1_attn_bq_conv, L1_attn_wk_conv, L1_attn_bk_conv, L1_attn_wv_conv, L1_attn_bv_conv, L1_attn_Wq, L1_attn_bq, L1_attn_Wk, L1_attn_bk, L1_attn_Wv, L1_attn_bv, L1_attn_Wad, L1_attn_bad, L1_attn_Wau, L1_attn_bau, L1_attn_Wbeta, L1_attn_bbeta, L1_attn_rms_w, L1_attn_Wgd, L1_attn_bgd, L1_attn_Wgu, L1_attn_bgu, L1_attn_Wo, L1_attn_bo) + _L1_ffn_ref(xn, L1_ffn_gate_w, L1_ffn_gate_bias, L1_ffn_gate_proj, L1_ffn_up_proj, L1_ffn_down_proj, L1_ffn_shared_gate_w, L1_ffn_shared_up_w, L1_ffn_shared_down_w)
    return x

_drawn_inputs = setup_inputs


def setup_inputs(seed=0):
    import zlib

    import numpy as np

    out = dict(_drawn_inputs(seed))
    spreads = {'L0_attn_qkv_b': (0.0, 0.1),
     'L0_attn_proj_b': (0.0, 0.1),
     'L1_attn_bq_conv': (0.0, 0.1),
     'L1_attn_bk_conv': (0.0, 0.1),
     'L1_attn_bv_conv': (0.0, 0.1),
     'L1_attn_bq': (0.0, 0.1),
     'L1_attn_bk': (0.0, 0.1),
     'L1_attn_bv': (0.0, 0.1),
     'L1_attn_bad': (0.0, 0.1),
     'L1_attn_bau': (0.0, 0.1),
     'L1_attn_bbeta': (0.0, 0.1),
     'L1_attn_rms_w': (1.0, 0.2),
     'L1_attn_bgd': (0.0, 0.1),
     'L1_attn_bgu': (0.0, 0.1),
     'L1_attn_bo': (0.0, 0.1),
     'L1_ffn_gate_bias': (0.0, 0.1)}
    factors = {}
    for name, (base, spread) in spreads.items():
        noise = np.random.default_rng([zlib.crc32(name.encode()), seed]).standard_normal(out[name].shape)
        drawn = base * np.exp(spread * noise) if base else spread * noise
        out[name] = jnp.asarray(drawn.astype(out[name].dtype))
    for name, factor in factors.items():
        out[name] = (out[name] * factor).astype(out[name].dtype)
    return out
```

```python
from contextlib import ExitStack

import numpy as np

import concourse.bass as bass
from concourse import mybir

F32 = mybir.dt.float32
I32 = mybir.dt.int32
U32 = mybir.dt.uint32
ALU = mybir.AluOpType
ACT = mybir.ActivationFunctionType
AX = mybir.AxisListType.X

P = 128
B, T, D = 4, 1024, 128
TT = T // P
NT = B * TT
BLK = 64
H0, D0 = 16, 8
HP = 8
F0, E0 = 512, 8
H1, DK = 16, 64
R1 = 64
E1, I1, NS1, K1 = 16, 176, 2, 4
IT = -(-(E1 + NS1) * I1 // P)
IW = IT * P
EPS_LN, EPS1 = 1e-05, 1e-06
NEG = -1e30
KW = 4


def constants():
    i = np.arange(P)
    parts = {}
    parts["ident"] = np.eye(P)
    c, r = i // BLK, i % BLK
    same = (c[:, None] == c[None, :])
    upto = same & (r[:, None] <= r[None, :])
    tomid = same & (r[:, None] < BLK // 2)
    parts["cum_mid"] = upto.astype(float) - tomid
    parts["cum_end"] = same & (r[:, None] > r[None, :])
    parts["cum"] = upto
    parts["chunk_of"] = c[:, None] == np.arange(2)[None, :]
    ii = np.arange(BLK)[None, :]
    parts["mask_a"] = (r[:, None] <= ii)
    parts["mask_l"] = (r[:, None] < ii)
    for s in (2, 4, 8, 16, 32, 64):
        parts[f"lev{s}"] = (r[:, None] // s == ii // s) & (r[:, None] % s < s // 2) & (ii % s >= s // 2)
    parts["eye_chunk"] = r[:, None] == ii
    parts["head_of"] = (i[:, None] // D0 == np.arange(H0)[None, :])
    parts["causal_q"] = np.where(r[:, None] < ii, NEG, 0.0)
    parts["causal_k"] = np.where(ii < r[:, None], NEG, 0.0)
    parts["two_eyes"] = (i[:, None] == np.arange(P)[None, :] % BLK) & (i[:, None] < BLK)
    parts["eye_hi"] = (i[:, None] + BLK == np.arange(P)[None, :])
    blk = np.arange(T) // BLK
    parts["blk_of"] = (i[:, None] == blk[None, :])
    parts["iota8"] = np.broadcast_to(np.arange(E0), (P, E0))
    parts["rowid"] = i[:, None]
    e = np.arange(E1)
    parts["before16"] = np.broadcast_to((e[None, :] < e[:, None]).reshape(1, -1), (P, 256))
    g = np.arange(4)
    parts["before4"] = np.broadcast_to((g[None, :] < g[:, None]).reshape(1, -1), (P, 16))
    only0 = ("head_of", "causal_q", "causal_k", "two_eyes", "eye_hi", "blk_of", "iota8", "rowid")
    at, cols, n = {}, ([], []), [0, 0]
    for k, v in parts.items():
        v = np.asarray(v, np.float32)
        z = int(k in only0)
        at[k] = (z, n[z], v.shape[1])
        n[z] += v.shape[1]
        cols[z].append(v)
    own = np.zeros((P, IW), np.float32)
    for x in range(E1 + NS1):
        own[x, x * I1:(x + 1) * I1] = 1
    return np.concatenate(cols[0], 1), np.concatenate(cols[1], 1), at, own


class Engine:

    def __init__(self, name, eng, semaphore):
        self.name, self.eng, self.semaphore = name, eng, semaphore
        self.counts, self.waited, self.pending, self.last = {}, {}, [], None

    def do(self, issue, *waits, sig="done", inc=1):
        own = [self.last] if self.name in ("dve", "act", "pool") else []
        for w in list(waits) + self.pending + own:
            if w and self.waited.get(w[0], 0) < w[1]:
                self.waited[w[0]] = w[1]
                if self.eng is not None:
                    self.eng.wait_ge(self.semaphore(w[0]), w[1])
        self.pending = []
        ins = issue(self.eng) if self.eng is not None else None
        if not sig:
            return None
        key = f"{self.name}_{sig}"
        self.counts[key] = self.counts.get(key, 0) + inc
        self.last = (key, self.counts[key])
        if ins is not None:
            ins.then_inc(self.semaphore(key), inc)
        else:
            self.semaphore(key)
        return self.last


def bc(ap, axis, n):
    a = ap.unsqueeze(axis)
    shape = list(a.shape)
    shape[axis] = n
    return a.broadcast_to(shape)


def program(nc, ins, out):
    with ExitStack() as ctx:
        made = {}

        def sbuf(name, shape):
            if name not in made:
                made[name] = ctx.enter_context(nc.sbuf_tensor(name, shape, F32))
            return made[name][:]

        def psum(name, shape):
            if name not in made:
                made[name] = ctx.enter_context(nc.psum_tensor(name, shape, F32))
            return made[name][:]

        def semaphore(name):
            if name not in made:
                made[name] = ctx.enter_context(nc.semaphore(name))
            return made[name]

        def write(name, eng):
            engines = [Engine(n, eng if n == name else None, semaphore) for n in ("pe", "dve", "act", "pool", "sp")]
            describe(engines, sbuf, psum, ins, out)

        write(None, None)
        with nc.Block() as block:
            @block.tensor
            def _(eng):
                write("pe", eng)

            @block.vector
            def _(eng):
                write("dve", eng)

            @block.scalar
            def _(eng):
                write("act", eng)

            @block.gpsimd
            def _(eng):
                write("pool", eng)

            @block.sync
            def _(eng):
                write("sp", eng)


def describe(engines, sb, psum, ins, out):
    pe, dve, act, pool, sp = engines
    ps = psum("ps", [P, 8, 512])
    bank = lambda i: ps[:, i, :]
    pair = lambda i: ps[:, i:i + 2, :].rearrange("p a n -> p (a n)")
    free = [None] * 8

    def barrier():
        for e in engines:
            e.pending = [o.last for o in engines if o is not e and o.last] + e.pending

    xres = sb("xres", [P, NT, D])
    xnT = sb("xnT", [P, B, T + KW - 1])
    cst_np, cst0_np, at, _ = constants()
    cst = sb("cst", [P, cst_np.shape[1]])
    w_gu = sb("w_gu", [P, 2, IW])
    w_dn = sb("w_dn", [P, IT, D])
    cst0 = w_gu[:, 1, 0:cst0_np.shape[1]]

    def C(k):
        z, n, m = at[k]
        return (cst, cst0)[z][:, n:n + m]
    w_q, w_k, w_v = (sb(f"w_{c}", [P, H1 * DK]) for c in "qkv")
    w_au = sb("w_au", [R1 + 1, H1 * DK])
    w_o = sb("w_o", [P, HP, D])
    b_q, b_k, b_v = (sb(f"b_{c}", [P, H1 * DK]) for c in "qkv")
    small = sb("small", [P, 640])
    own = sb("own", [E1 + NS1, 2, 512])
    WORK = 24120
    work = sb("work", [P, WORK])
    used = [0, 0]

    def take(pool_i, *shape):
        buf, size = ((work, WORK), (small, 640))[pool_i]
        n = int(np.prod(shape))
        v = buf[:, used[pool_i]:used[pool_i] + n]
        used[pool_i] += n
        assert used[pool_i] <= size, (pool_i, used)
        if len(shape) > 1:
            names = "abcdef"[:len(shape)]
            v = v.rearrange(f"p ({' '.join(names)}) -> p {' '.join(names)}", **dict(zip(names, shape)))
        return v

    def load(dst, src, name, eng=sp):
        return eng.do(lambda e: e.dma_start(dst, src), sig=f"ld_{name}", inc=16)

    load(cst, ins["cst"], "cst")
    ld_c = load(cst0, ins["cst0"], "cst")
    ld_x = [load(xres[:, b * TT:(b + 1) * TT, :], ins["x"][:, b * TT:(b + 1) * TT, :], f"x{b}") for b in range(B)]
    b0 = take(1, 3)
    pw = take(1, 2, D)
    wr = take(1, E0)
    brb = take(1, E0)
    bvb = take(1, D)
    pbb = take(1, D)
    wqkv0 = w_gu[:, 0, 0:3 * D]
    ld_s = None
    for dst, key in ((wqkv0, "wqkv0"), (b0, "b0"), (wr, "wr")):
        ld_s = load(dst, ins[key], "s0")
    ld_s = load(pw[0:64, :, :], ins["pw0"], "s0")
    for dst, key in ((brb, "br"), (bvb, "bv0"), (pbb, "pb0")):
        ld_s = load(dst, ins[key].partition_broadcast(P)[:, 0, :], "s0")
    ident = C("ident")

    nwt = sb("nwt", [P, 2, H1])

    def rsqrt(x, y, ok):
        n = x.shape[1]
        u, w = nwt[:, 0, 0:n], nwt[:, 1, 0:n]
        a = act.do(lambda e: e.activation(u, x, ACT.Ln), ok, dve.last)
        a = act.do(lambda e: e.activation(y, u, ACT.Exp, scale=-0.5), a)
        a = dve.do(lambda e: e.tensor_tensor(w, y, y, ALU.mult), a)
        a = dve.do(lambda e: e.tensor_tensor(w, w, x, ALU.mult), a)
        a = dve.do(lambda e: e.tensor_scalar(w, w, -0.5, 1.5, ALU.mult, ALU.add), a)
        return dve.do(lambda e: e.tensor_tensor(y, y, w, ALU.mult), a)

    st = take(1, TT, 6)
    mv = take(1, TT, 2)
    rs = take(1, TT)
    ve = take(1, TT)
    z_pad = pool.do(lambda e: e.memset(xnT[:, :, 0:KW - 1], 0.0))

    def norm(b, xn, ready, banks, xn_free):
        for t in range(TT):
            x = xres[:, b * TT + t, :]
            a = dve.do(lambda e: e.bn_stats(st[:, t, :], x), *ready)
        for t in range(TT):
            a2 = dve.do(lambda e: e.bn_aggr(mv[:, t, :], st[:, t, :]), a)
        a = dve.do(lambda e: e.tensor_scalar(ve, mv[:, :, 1], EPS_LN, None, ALU.add), a2)
        a = rsqrt(ve, rs, a)
        for t in range(TT):
            x = xres[:, b * TT + t, :]
            a = dve.do(lambda e: e.tensor_scalar(xn[:, t, :], x, mv[:, t, 0:1], rs[:, t:t + 1],
                                                           ALU.subtract, ALU.mult), a, *xn_free)
        for g in range(TT // 4):
            k = banks[g % len(banks)]
            for q in range(4):
                t = 4 * g + q
                m = pe.do(lambda e: e.transpose(bank(k)[:, q * P:(q + 1) * P], xn[:, t, :], ident),
                          a, ld_c, free[k], sig="nT" if q == 3 else None)
            free[k] = act.do(lambda e: e.copy(xnT[:, b, KW - 1 + g * 512:KW - 1 + (g + 1) * 512],
                                                            bank(k)), m, sig="xnT")
        return free[k]

    xn = take(0, TT, D)
    xnT_ok = []
    xn_free = ()
    for b in range(B):
        tok = norm(b, xn, (ld_x[b],), (0, 1), xn_free)
        xn_free = (pe.last,)
        xnT_ok.append(tok)
    used[0] = 0
    KT = take(0, B, T)
    Vbd = take(0, TT, HP, 2, 18)
    Qbd = take(0, H0, BLK)
    pT = take(0, TT, H0 * BLK)
    Oall = take(0, B, HP, 16, 9)
    w12 = KT.rearrange("p b t -> p (b t)")[:, 0:2 * 1028].rearrange("p (s n) -> p s n", s=2)
    small_q = take(0, BLK)
    mx = take(0, 2, HP, 16)
    em = take(0, B, HP, 16)
    barrier()
    xT = lambda b, lo, n: xnT[:, b, KW - 1 + lo:KW - 1 + lo + n]

    for b in range(B):
        for g in range(2):
            k = (2 * b + g) % 4
            m = pe.do(lambda e: e.matmul(bank(k), wqkv0[:, D:2 * D], xT(b, g * 512, 512), start=True, stop=True),
                      free[k], ld_s, xnT_ok[b])
            kT_ok = free[k] = act.do(lambda e: e.activation(KT[:, b, g * 512:(g + 1) * 512], bank(k), ACT.Identity,
                                                                           bias=b0[:, 1:2]), m, ld_s)
    nmT = take(0, H0 * BLK)[0:16, :]
    Vs = take(0, TT, D)
    z1 = pool.do(lambda e: e.memset(Vbd, 0.0))
    V5 = Vbd.rearrange("p t h k (s x) -> p t h k s x", s=2)
    for kb in range(2):
        ones_ok = pool.do(lambda e: e.memset(V5[kb * 64:(kb + 1) * 64, :, :, kb, :, 8:9].rearrange("p t h s x -> p (t h) s x"), 1.0), z1)
    attn_tail = None
    for b in range(B):
        m = pe.do(lambda e: e.matmul(bank(0)[:, 0:BLK], wqkv0[:, 0:D], xT(b, T - BLK, BLK), start=True, stop=True), free[0], kT_ok)
        a = act.do(lambda e: e.activation(small_q, bank(0)[:, 0:BLK], ACT.Identity, bias=b0[:, 0:1]), m, dve.last)
        free[0] = a
        q_ok = dve.do(lambda e: e.tensor_tensor(Qbd, bc(small_q, 1, H0), bc(C("head_of"), 2, BLK), ALU.mult), a, pe.last)
        for g in range(2):
            for q in range(4):
                t = 4 * g + q
                m = pe.do(lambda e: e.matmul(bank(1 + g)[:, q * D:(q + 1) * D], xT(b, t * P, P), wqkv0[:, 2 * D:3 * D],
                                                                 start=True, stop=True), free[1 + g], sig="v0" if q == 3 else None)
            a = dve.do(lambda e: e.tensor_tensor(Vs[:, 4 * g:4 * g + 4, :], bank(1 + g).rearrange("p (q d) -> p q d", d=D),
                                                      bc(bvb, 1, 4), ALU.add), m, pe.last, pool.last)
            free[1 + g] = a
        for kb in range(2):
            rows = slice(kb * 64, (kb + 1) * 64)
            for s in range(2):
                v_ok = pool.do(lambda e: e.tensor_copy(
                    V5[rows, :, :, kb, s, 0:8], Vs[rows, :, :].rearrange("p t (h s x) -> p t h s x", s=2, x=8)[:, :, :, s, :]), a, ones_ok, pe.last)
        for hp in range(HP):
            for g in range(2):
                k = 4 + (2 * hp + g) % 4
                m = pe.do(lambda e: e.matmul(bank(k), Qbd[:, 2 * hp:2 * hp + 2, :], KT[:, b, g * 512:(g + 1) * 512],
                                                                   start=True, stop=True), free[k], q_ok)
                if g == 1:
                    m = pe.do(lambda e: e.matmul(bank(k)[:, 448:512], C("two_eyes")[0:64, :], C("causal_q")[0:64, :],
                                                      start=False, stop=True, skip_group_check=True))
                a = dve.do(lambda e: e.tensor_reduce(mx[:, 0, hp, 8 * g:8 * g + 8], bank(k).rearrange("p (j n) -> p j n", n=BLK), AX, ALU.max), m)
                free[k] = a
        src = 0
        for s in (1, 2, 4, 8):
            x, y = mx[:, src], mx[:, 1 - src]
            a1 = dve.do(lambda e: e.tensor_tensor(y[:, :, s:16], x[:, :, s:16], x[:, :, 0:16 - s], ALU.max), a, pe.last)
            a = dve.do(lambda e: e.tensor_copy(y[:, :, 0:s], x[:, :, 0:s]), a1)
            src = 1 - src
        mrun, tmp = mx[:, src], mx[:, 1 - src]
        a1 = dve.do(lambda e: e.tensor_tensor(tmp[:, :, 1:16], mrun[:, :, 0:15], mrun[:, :, 1:16], ALU.subtract), a)
        act.do(lambda e: e.activation(em[:, b, :, 1:16], tmp[:, :, 1:16], ACT.Exp, scale=D0 ** -0.5), a1)
        for hp in range(HP):
            k = hp // 4
            m = pe.do(lambda e: e.transpose(bank(k)[0:16, (hp % 4) * P:(hp % 4 + 1) * P], mrun[:, hp, :], ident), a, free[k], sig="mT" if hp % 4 == 3 else None)
        nm_ok = act.do(lambda e: e.mul(nmT, pair(0)[0:16, :], -1.0), m)
        free[0] = free[1] = nm_ok
        for kt in range(TT):
            k = 4 + 2 * (kt % 2)
            for g in range(2):
                kk = k + g
                pe.do(lambda e: e.matmul(bank(kk), KT[:, b, kt * P:(kt + 1) * P], Qbd[:, 8 * g:8 * g + 8, :], start=True, stop=False), free[kk], sig=None)
                m = pe.do(lambda e: e.matmul(bank(kk), C("blk_of")[0:16, kt * P:(kt + 1) * P], nmT[:, g * 512:(g + 1) * 512], start=False, stop=(kt < TT - 1)), nm_ok)
                if kt == TT - 1:
                    m = pe.do(lambda e: e.matmul(bank(kk), C("eye_hi")[0:64, :], bc(C("causal_k")[0:64, :], 1, 8), start=False, stop=True))
            e_ok = act.do(lambda e: e.activation(pT[:, kt, :], pair(k), ACT.Exp, scale=D0 ** -0.5), m)
            free[k] = free[k + 1] = e_ok
        for hp in range(HP):
            k = hp % 4
            for kt in range(TT):
                m = pe.do(lambda e: e.matmul(bank(k)[:, kt * 36:(kt + 1) * 36], pT[:, kt, hp * P:(hp + 1) * P], Vbd[:, kt, hp, :, :].rearrange("p k x -> p (k x)"),
                                                                start=True, stop=True), free[k], e_ok, v_ok, sig="pv" if kt == TT - 1 else None)
            for s in range(2):
                rows = slice(64 * s, 64 * s + 64)
                free[k] = o_ok = dve.do(lambda e: e.tensor_copy(
                    Oall[rows, b, hp, :, :], bank(k)[rows, 0:288].rearrange("p (j s x) -> p j s x", s=2, x=9)[:, :, s, :]), m)
    flat = pT.rearrange("p t n -> p (t n)")
    lsum, rr = (flat[:, o:o + 512].rearrange("p (b h j) -> p b h j", b=B, h=HP) for o in (2048, 2560))
    acc, df = (flat[:, o:o + 256].rearrange("p (b h x) -> p b h x", b=B, h=HP) for o in (3072, 3328))
    a = dve.do(lambda e: e.tensor_copy(lsum[:, :, :, 0], Oall[:, :, :, 0, 8]), o_ok, act.last, pe.last)
    for j in range(1, 16):
        a = dve.do(lambda e: e.tensor_tensor(lsum[:, :, :, j], lsum[:, :, :, j - 1], em[:, :, :, j], ALU.mult), a)
        a = dve.do(lambda e: e.tensor_tensor(lsum[:, :, :, j], lsum[:, :, :, j], Oall[:, :, :, j, 8], ALU.add), a)
    a = dve.do(lambda e: e.reciprocal(rr, lsum), a)
    rl = flat[:, 3584:3616].rearrange("p (b h) -> p b h", b=B)
    a2 = dve.do(lambda e: e.tensor_copy(rl, rr[:, :, :, 15]), a)
    a = dve.do(lambda e: e.tensor_tensor(rr[:, :, :, 1:16], lsum[:, :, :, 0:15], rr[:, :, :, 1:16], ALU.mult), a2)
    a = dve.do(lambda e: e.memset(acc, 0.0), a)
    for j in range(1, 16):
        a = dve.do(lambda e: e.tensor_tensor(df, Oall[:, :, :, j, 0:8], acc, ALU.subtract), a)
        a = dve.do(lambda e: e.tensor_tensor(df, df, bc(rr[:, :, :, j], 3, D0), ALU.mult), a)
        a = dve.do(lambda e: e.tensor_tensor(acc, acc, df, ALU.add), a)
    fin_ok = dve.do(lambda e: e.tensor_tensor(acc, acc, bc(rl, 3, D0), ALU.mult), a)
    for b in range(B):
        xb_ok = dve.do(lambda e: e.tensor_tensor(xres[:, b * TT:(b + 1) * TT, :], xres[:, b * TT:(b + 1) * TT, :], bc(pbb, 1, TT), ALU.add), ld_s, fin_ok)
    oT = Vs
    for b in range(B):
        m = pe.do(lambda e: e.transpose(bank(0)[0:64, 0:P], acc[:, b, :, :].rearrange("p h x -> p (h x)"), ident), fin_ok, free[0])
        a = act.do(lambda e: e.copy(oT[0:64, b, :], bank(0)[0:64, 0:P]), m)
        free[0] = a
        for s in range(2):
            m = pe.do(lambda e: e.matmul(bank(1)[64:128, 0:D], oT[0:64, b, 64 * s:64 * s + 64], pw[0:64, s, :], start=(s == 0), stop=(s == 1)), a, free[1])
        row = xres[64:128, b * TT + TT - 1, :]
        free[1] = dve.do(lambda e: e.tensor_tensor(row, row, bank(1)[64:128, 0:D], ALU.add), m, xb_ok)

    meanT = take(0, B)
    mrep = take(0, P)
    sc = take(0, B, E0)
    eq = take(0, B, E0)
    top = take(0, B)
    idxf = take(0, 2, B)
    idx = take(0, 2, B).bitcast(U32)
    b2r = take(0, B, D)
    hT = pT[:, 0:2, :].rearrange("p a (f n) -> p (a f) n", n=512)
    barrier()
    for b in range(B):
        a = dve.do(lambda e: e.tensor_reduce(meanT[:, b:b + 1], xT(b, 0, T), AX, ALU.add))
    a = dve.do(lambda e: e.tensor_scalar(meanT, meanT, 1.0 / T, None, ALU.mult), a)
    for b in range(B):
        a1 = dve.do(lambda e: e.tensor_copy(mrep, meanT[:, b:b + 1].broadcast_to([P, P])), a, pe.last)
        m = pe.do(lambda e: e.matmul(bank(0)[:, 8 * b:8 * b + 8], mrep, wr, start=True, stop=True), a1, free[0])
    a = dve.do(lambda e: e.tensor_tensor(sc, bank(0)[:, 0:32].rearrange("p (b e) -> p b e", e=E0), bc(brb, 1, B), ALU.add), m)
    free[0] = a
    a = dve.do(lambda e: e.tensor_reduce(top, sc, AX, ALU.max), a)
    a = dve.do(lambda e: e.tensor_tensor(eq, sc, bc(top, 2, E0), ALU.is_equal), a)
    a = dve.do(lambda e: e.tensor_scalar(eq, eq, -100.0, 100.0, ALU.mult, ALU.add), a)
    a = dve.do(lambda e: e.tensor_tensor(eq, eq, bc(C("iota8"), 1, B), ALU.add), a)
    a = dve.do(lambda e: e.tensor_reduce(idxf[:, 1, :], eq, AX, ALU.min), a)
    a = dve.do(lambda e: e.tensor_scalar(idxf[:, 0, :], idxf[:, 1, :], float(P), C("rowid"), ALU.mult, ALU.add), a)
    idx_ok = dve.do(lambda e: e.tensor_copy(idx, idxf), a)
    for b in range(B):
        b2_ok = pool.do(lambda e: e.indirect_dma_start(b2r[:, b, :], None, ins["b2"], bass.IndirectOffsetOnAxis(ap=idx[:, 1, b:b + 1], axis=0)),
                        idx_ok, sig="b2", inc=16)
    w_free = [None, None]
    x2_ok = []
    for b in range(B):
        w = w12[:, b % 2, :]
        w_ok = pool.do(lambda e: e.indirect_dma_start(w, None, ins["w12"], bass.IndirectOffsetOnAxis(ap=idx[:, 0, b:b + 1], axis=0)),
                       w_free[b % 2], sig=f"w12{b % 2}", inc=16)
        for g in range(2):
            for f in range(4):
                k = f
                m = pe.do(lambda e: e.matmul(bank(k), w[:, f * P:(f + 1) * P], xT(b, g * 512, 512), start=True, stop=True), w_ok, free[k])
                h_ok = free[k] = act.do(lambda e: e.activation(hT[:, f, :], bank(k), ACT.Relu, bias=w[:, 1024 + f:1025 + f]), m, pe.last)
            k = 4 + g
            for t in range(4):
                for f in range(4):
                    m = pe.do(lambda e: e.matmul(bank(k)[:, t * D:(t + 1) * D], hT[:, f, t * P:(t + 1) * P], w[:, 512 + f * D:512 + (f + 1) * D],
                                                                     start=(f == 0), stop=(f == 3)), h_ok, free[k], sig="y0" if f == 3 else None)
            xs = xres[:, b * TT + 4 * g:b * TT + 4 * g + 4, :]
            a = dve.do(lambda e: e.tensor_tensor(xs, xs, bank(k).rearrange("p (t d) -> p t d", d=D), ALU.add), m)
            free[k] = a
            a = dve.do(lambda e: e.tensor_tensor(xs, xs, bc(b2r[:, b, :], 1, 4), ALU.add), a, b2_ok)
        w_free[b % 2] = pe.last
        x2_ok.append(a)

    barrier()
    used[0] = 0
    used[1] = 0
    st = take(1, TT, 6)
    mv = take(1, TT, 2)
    rs = take(1, TT)
    ve = take(1, TT)
    xn = take(0, TT, D)
    ld1 = None
    for dst, key in ((w_gu, "w_gu"), (w_dn, "w_dn"), (w_q, "w_q"), (w_k, "w_k"), (w_v, "w_v"), (w_au, "w_au"), (w_o, "w_o")):
        ld1 = load(dst, ins[key], "l1")
    for dst, key in ((b_q, "b_q"), (b_k, "b_k"), (b_v, "b_v")):
        ld1 = load(dst, ins[key].partition_broadcast(P)[:, 0, :], "l1")
    smalls = take(1, ins["small1"].shape[1])
    ld1 = load(smalls, ins["small1"], "l1")
    so = [0]

    def sm(n):
        v = smalls[:, so[0]:so[0] + n]
        so[0] += n
        return v
    convw = sm(15).rearrange("p (c k) -> p c k", k=5)
    rmsw = sm(HP)
    w_ad, w_gd = sm(R1), sm(R1)
    b_ad, b_gd = sm(1), sm(1)
    w_be, w_gate, w_gu16 = sm(H1), sm(E1), sm(H1)
    small_b = take(1, 2 * 16 + D)
    bb, gb = small_b[:, 0:16], small_b[:, 16:32]
    bo_b = small_b[:, 32:32 + D]
    ld1 = load(small_b, ins["smallb"].partition_broadcast(P)[:, 0, :], "l1")
    xn_free = ()
    x1T_ok = []
    for b in range(B):
        x1T_ok.append(norm(b, xn, (), (0, 1), xn_free))
        xn_free = (pe.last,)
    a = None
    for hp in range(HP):
        a = wo_ok = dve.do(lambda e: e.tensor_scalar(w_o[:, hp, :], w_o[:, hp, :], rmsw[:, hp:hp + 1], None, ALU.mult), ld1)
    for b in range(B):
        a = dve.do(lambda e: e.tensor_tensor(xres[:, b * TT:(b + 1) * TT, :], xres[:, b * TT:(b + 1) * TT, :], bc(bo_b, 1, TT), ALU.add), ld1)

    used[0] = 0
    barrier()
    NTE = (NT, E1)
    scores = take(0, *NTE)
    sfc = take(0, *NTE)
    ra = take(0, *NTE)
    rb = take(0, *NTE)
    gs = take(0, NT, 4)
    g2 = take(0, NT, 4)
    gm = take(0, NT, 4)
    cmp16 = take(0, NT, E1, E1)
    cmb = take(0, *NTE)
    cwT = take(0, NT * P)[0:32, :]
    for n in range(NT):
        m = pe.do(lambda e: e.matmul(bank(0)[:, n * 16:(n + 1) * 16], xT(n // TT, (n % TT) * P, P), w_gate, start=True, stop=True), x1T_ok[n // TT], ld1, free[0],
                  sig="lg" if n == NT - 1 else None)
    fl = lambda v: v.rearrange("p n e -> p (n e)")
    a = act.do(lambda e: e.activation(fl(scores), bank(0), ACT.Sigmoid), m)
    free[0] = a
    a = dve.do(lambda e: e.tensor_tensor(sfc, scores, bc(gb, 1, NT), ALU.add), a, ld1)
    grp = sfc.rearrange("p n (g k) -> p n g k", k=4)
    first = True
    for i in range(4):
        for j in range(i + 1, 4):
            dst = gs if first else g2
            a = dve.do(lambda e: e.tensor_tensor(dst, grp[:, :, :, i], grp[:, :, :, j], ALU.add), a)
            if not first:
                a = dve.do(lambda e: e.tensor_tensor(gs, gs, g2, ALU.max), a)
            first = False

    def rank_below(dst, val, before, n, keep, a):
        c4 = cmp16.rearrange("p t a b -> p t (a b)")[:, :, 0:n * n].rearrange("p t (a b) -> p t a b", b=n)
        eqm = before.rearrange("p (a b) -> p a b", b=n)
        mine, other = bc(val, 3, n), bc(val, 2, n)
        a = dve.do(lambda e: e.tensor_tensor(c4, other, mine, ALU.is_equal), a)
        a = dve.do(lambda e: e.tensor_tensor(c4, c4, bc(eqm, 1, NT), ALU.mult), a)
        a = dve.do(lambda e: e.tensor_reduce(rank_a[:, :, 0:n], c4, AX, ALU.add), a)
        a = dve.do(lambda e: e.tensor_tensor(c4, other, mine, ALU.is_gt), a)
        a = dve.do(lambda e: e.tensor_reduce(dst, c4, AX, ALU.add), a)
        a = dve.do(lambda e: e.tensor_tensor(dst, dst, rank_a[:, :, 0:n], ALU.add), a)
        return dve.do(lambda e: e.tensor_scalar(dst, dst, keep - 0.5, None, ALU.is_lt), a)

    rank_a = take(0, NT, E1)
    a = rank_below(gm, gs, C("before4"), 4, 2, a)
    ra4 = ra.rearrange("p n (g k) -> p n g k", k=4)
    a = dve.do(lambda e: e.tensor_tensor(ra4, grp, bc(gm, 3, 4), ALU.mult), a)
    a = rank_below(rb, ra, C("before16"), 16, K1, a)
    a = dve.do(lambda e: e.tensor_tensor(cmb, scores, rb, ALU.mult), a)
    a = dve.do(lambda e: e.tensor_reduce(gs[:, :, 0], cmb, AX, ALU.add), a)
    a = dve.do(lambda e: e.tensor_scalar(gs[:, :, 0], gs[:, :, 0], 1e-20, None, ALU.add), a)
    a = dve.do(lambda e: e.reciprocal(gs[:, :, 1], gs[:, :, 0]), a)
    cmb_ok = dve.do(lambda e: e.tensor_tensor(cmb, cmb, bc(gs[:, :, 1], 2, E1), ALU.mult), a)
    ones_ok = pool.do(lambda e: e.memset(cwT, 1.0))
    for g in range(NT // 4):
        k = g % 2
        for q in range(4):
            m = pe.do(lambda e: e.transpose(bank(k)[0:16, q * P:(q + 1) * P], cmb[:, 4 * g + q, :], ident), cmb_ok, free[k], sig="cwT" if q == 3 else None)
        cw_ok = free[k] = act.do(lambda e: e.copy(cwT[0:16, g * 512:(g + 1) * 512], bank(k)[0:16, :]), m, ones_ok)
    cw_st = sp.do(lambda e: e.dma_start(ins["cw_park"], cwT[0:E1 + NS1, :]), cw_ok, sig="cwst", inc=16)
    sp.do(lambda e: e.dma_start(own[:, 0, :], ins["cw_park"][:, 0:512]), cw_st, sig="cwld", inc=16)

    barrier()
    used[0] = 0
    touched = {}
    outs_ok = []

    def add_out(n0, cnt, src, wait):
        xs = xres[:, n0:n0 + cnt, :]
        a = dve.do(lambda e: e.tensor_tensor(xs, xs, src, ALU.add), wait, *[touched.get(n) for n in range(n0, n0 + cnt)])
        for n in range(n0, n0 + cnt):
            if n in touched:
                outs_ok.append(sp.do(lambda e: e.dma_start(out[:, n, :], xres[:, n, :]), a, sig="out", inc=16))
            touched[n] = a
        return a

    s_g, t_u, acts, yT = take(0, 512), take(0, 512), take(0, 2, 512), take(0, 512)
    own_w = take(0, 2, P)

    def mixture():
        GA, UB, CWB, YB = 4, 5, 6, 7
        own_free = [None, None]
        ow_free = [None, None]
        act_free = [None, None]
        own_ld = {0: ("sp_cwld", 16)}
        ownw_free = None
        s_free = t_free = yT_free = None
        for g in range(NT // 4):
            b, lo = g // 2, (g % 2) * 512
            if g + 1 < NT // 4:
                own_ld[g + 1] = sp.do(lambda e: e.dma_start(own[:, (g + 1) % 2, :], ins["cw_park"][:, (g + 1) * 512:(g + 2) * 512]),
                                      own_free[(g + 1) % 2], sig=f"cw{g % 2}", inc=16)
            prev = None
            for it in range(IT + 1):
                if it < IT:
                    ld = sp.do(lambda e: e.dma_start(own_w[0:E1 + NS1, it % 2, :], ins["own"][:, it * P:(it + 1) * P]),
                               ow_free[it % 2], sig=f"ow{it % 2}", inc=16)
                    m = pe.do(lambda e: e.matmul(bank(GA), w_gu[:, 0, it * P:(it + 1) * P], xT(b, lo, 512), start=True, stop=True), free[GA], ld1, x1T_ok[b])
                    a_s = act.do(lambda e: e.activation(s_g, bank(GA), ACT.Silu), m, s_free)
                    free[GA] = a_s
                    m = pe.do(lambda e: e.matmul(bank(UB), w_gu[:, 1, it * P:(it + 1) * P], xT(b, lo, 512), start=True, stop=True), free[UB])
                    a_t = dve.do(lambda e: e.tensor_tensor(t_u, bank(UB), s_g, ALU.mult), m, a_s, t_free)
                    free[UB] = s_free = a_t
                    m = pe.do(lambda e: e.matmul(bank(CWB), own_w[0:E1 + NS1, it % 2, :], own[:, g % 2, :], start=True, stop=True), free[CWB], ld, own_ld[g])
                    ow_free[it % 2] = m
                    own_free[g % 2] = m
                    ac = acts[:, it % 2, :]
                    a = dve.do(lambda e: e.tensor_tensor(ac, bank(CWB), t_u, ALU.mult), m, a_t, act_free[it % 2])
                    free[CWB] = t_free = a
                if prev is not None:
                    pit, pa = prev
                    m = pe.do(lambda e: e.matmul(bank(YB), w_dn[:, pit, :], acts[:, pit % 2, :], start=(pit == 0), stop=(pit == IT - 1)), pa, free[YB])
                    act_free[pit % 2] = m
                if it < IT:
                    prev = (it, a)
                yield
            a = act.do(lambda e: e.copy(yT, bank(YB)), m, yT_free)
            free[YB] = a
            for q in range(4):
                m = pe.do(lambda e: e.transpose(bank(YB)[:, q * P:(q + 1) * P], yT[:, q * P:(q + 1) * P], ident), a, sig="yt" if q == 3 else None)
            yT_free = m
            free[YB] = add_out(4 * g, 4, bank(YB).rearrange("p (t d) -> p t d", d=D), m)
            yield

    G4 = 2
    KH = H1 * DK
    GT = G4 * P
    lg = take(0, G4, KH)
    cs = take(0, 3, GT)
    ctmp = take(0, GT)
    adT, gdT = take(0, GT), take(0, GT)
    Ex = take(0, 4, KH)
    Qr, Kr, Vr, Kb, Qd, sq = (take(0, KH) for _ in range(6))
    DT = take(0, 4, HP, P)
    AT, LT = take(0, H1, BLK), take(0, H1, BLK)
    beta, gate = take(0, G4, H1), take(0, G4, H1)
    stat = take(0, 6, H1)
    gE = take(0, HP, 2)
    S = take(0, HP, DK)
    Tm = DT[:, 0].rearrange("p a n -> p (a n)").rearrange("p (h d) -> p h d", d=DK)
    Um = Qr.rearrange("p (h d) -> p h d", d=DK)
    h16 = lambda v: v.rearrange("p (h d) -> p h d", d=DK) if len(v.shape) == 2 else v

    def delta():
        S0, S1 = 0, 2
        SB = {0: (0, 1), 2: (2, 3)}

        def fr(s):
            return [free[k] for k in SB[s]]

        def setf(s, tok):
            for k in SB[s]:
                free[k] = tok
        zt = pool.do(lambda e: e.memset(AT, 0.0))
        zt = pool.do(lambda e: e.memset(LT, 0.0))
        ones_row = pool.do(lambda e: e.memset(adT[64:65, :], 1.0))
        ones_row = pool.do(lambda e: e.memset(gdT[64:65, :], 1.0))
        for b in range(B):
            st_ok = dve.do(lambda e: e.memset(S, 0.0), pe.last)
            for half in range(TT // G4):
                lo = half * GT
                for c in range(3):
                    dst = [ctmp, cs[:, c, :]]
                    a = dve.do(lambda e: e.tensor_scalar(dst[0], xnT[:, b, lo:lo + GT], convw[:, c, 0:1], convw[:, c, 4:5], ALU.mult, ALU.add), act.last, pe.last, x1T_ok[b], ld1, z_pad)
                    for k in range(1, KW):
                        a = dve.do(lambda e: e.scalar_tensor_tensor(dst[k % 2], xnT[:, b, lo + k:lo + k + GT], convw[:, c, k:k + 1], dst[(k + 1) % 2], ALU.mult, ALU.add), a)
                    cs_ok = act.do(lambda e: e.activation(cs[:, c, :], cs[:, c, :], ACT.Silu), a)
                yield
                for dst, w_, b_, k in ((adT, w_ad, b_ad, 0), (gdT, w_gd, b_gd, 1)):
                    m = pe.do(lambda e: e.matmul(bank(k)[0:R1, 0:GT], w_, xT(b, lo, GT), start=True, stop=True), free[k])
                    free[k] = lr_ok = act.do(lambda e: e.activation(dst[0:R1, :], bank(k)[0:R1, 0:GT], ACT.Silu, bias=b_[0:R1, :]), m, pe.last)
                for t in range(G4):
                    pe.do(lambda e: e.matmul(bank(2)[:, t * 16:t * 16 + 16], xT(b, lo + t * P, P), w_be, start=True, stop=True), free[2], sig=None)
                    m = pe.do(lambda e: e.matmul(bank(2)[:, 64 + t * 16:64 + t * 16 + 16], gdT[0:R1 + 1, t * P:(t + 1) * P], w_gu16[0:R1 + 1, :], start=True, stop=True), lr_ok, ones_row)
                G16 = G4 * H1
                a = dve.do(lambda e: e.tensor_tensor(beta, bank(2)[:, 0:G16].rearrange("p (t h) -> p t h", h=H1), bc(bb, 1, G4), ALU.add), m)
                act.do(lambda e: e.activation(gate.rearrange("p t h -> p (t h)"), bank(2)[:, 64:64 + G16], ACT.Sigmoid), m, a)
                free[2] = bg_ok = act.do(lambda e: e.activation(beta, beta, ACT.Sigmoid), a)
                bg_ok = dve.do(lambda e: e.tensor_scalar(beta, beta, 1.0, None, ALU.min), bg_ok)
                yield
                for t in range(G4):
                    s = (S0, S1)[t % 2]
                    for g in range(2):
                        m = pe.do(lambda e: e.matmul(bank(s + g), adT[0:R1 + 1, t * P:(t + 1) * P], w_au[:, g * 512:(g + 1) * 512], start=True, stop=True), *fr(s))
                    a = act.do(lambda e: e.activation(lg[:, t, :], pair(s), ACT.Sigmoid), m, pe.last)
                    setf(s, a)
                    lg_ok = dve.do(lambda e: e.tensor_scalar(lg[:, t, :], lg[:, t, :], 0.1, 1.0, ALU.max, ALU.min), a)
                    yield
                lg_ok = act.do(lambda e: e.activation(lg.rearrange("p t n -> p (t n)"), lg.rearrange("p t n -> p (t n)"), ACT.Ln), lg_ok)
                for t in range(G4):
                    n = b * TT + half * G4 + t
                    tok = slice(t * P, (t + 1) * P)
                    for c, dst, w_, bias, s in ((1, Kr, w_k, b_k, S0), (0, Qr, w_q, b_q, S1), (2, Vr, w_v, b_v, S0)):
                        for g in range(2):
                            m = pe.do(lambda e: e.matmul(bank(s + g), cs[:, c, tok], w_[:, g * 512:(g + 1) * 512], start=True, stop=True), cs_ok, *fr(s))
                        a = dve.do(lambda e: e.tensor_tensor(dst, pair(s), bias, ALU.add), m, pe.last, pool.last, act.last)
                        setf(s, a)
                        if c < 2:
                            i = 0 if c == 1 else 1
                            a = pool.do(lambda e: e.tensor_tensor(sq, dst, dst, ALU.mult), a, dve.last, pe.last)
                            a = dve.do(lambda e: e.tensor_reduce(stat[:, i, :], h16(sq), AX, ALU.add), a)
                            a = dve.do(lambda e: e.tensor_scalar(stat[:, 4, :], stat[:, i, :], EPS1, None, ALU.max), a)
                            a = rsqrt(stat[:, 4, :], stat[:, i, :], a)
                    a = dve.do(lambda e: e.tensor_tensor(stat[:, 2, :], stat[:, 0, :], beta[:, t, :], ALU.mult), a, bg_ok)
                    yield
                    for j, (mat, s) in enumerate((("cum_mid", S0), ("cum_end", S1), ("cum", S0))):
                        for g in range(2):
                            m = pe.do(lambda e: e.matmul(bank(s + g), C(mat), lg[:, t, g * 512:(g + 1) * 512], start=True, stop=True), lg_ok, *fr(s))
                        if j == 0:
                            act.do(lambda e: e.activation(Ex[:, 0, :], pair(s), ACT.Exp), m, pe.last, dve.last, pool.last)
                            x_ok = act.do(lambda e: e.activation(Ex[:, 1, :], pair(s), ACT.Exp, scale=-1.0), m)
                        else:
                            x_ok = act.do(lambda e: e.activation(Ex[:, j + 1, :], pair(s), ACT.Exp), m)
                        setf(s, x_ok)
                    for hp in range(HP):
                        m = pe.do(lambda e: e.matmul(bank(S1)[:, 2 * hp:2 * hp + 2], lg[:, t, hp * P:(hp + 1) * P], C("chunk_of"), start=True, stop=True), *fr(S1), sig="ge" if hp == 7 else None)
                    ge_ok = act.do(lambda e: e.activation(gE.rearrange("p a b -> p (a b)"), bank(S1)[:, 0:16], ACT.Exp), m, dve.last)
                    setf(S1, ge_ok)
                    yield
                    mul = lambda E, dst, x, y, *w: E.do(lambda e: e.tensor_tensor(dst, x, y, ALU.mult), *w)
                    sc_ = lambda i: bc(stat[:, i, :], 2, DK)
                    kb_ok = mul(pool, h16(Kb), h16(Kr), sc_(2), a, dve.last)
                    qn_ok = mul(dve, h16(Qr), h16(Qr), sc_(1), a)
                    kn_ok = mul(dve, h16(Kr), h16(Kr), sc_(0), kb_ok)
                    qd_ok = mul(dve, Qd, Qr, Ex[:, 0, :], qn_ok, x_ok)
                    kt_ok = mul(pool, Ex[:, 3, :], Ex[:, 3, :], Kr, kn_ok, x_ok)
                    k2_ok = mul(dve, Ex[:, 0, :], Ex[:, 0, :], Kr, qd_ok, kn_ok)
                    kd_ok = mul(pool, Ex[:, 1, :], Ex[:, 1, :], Kb, kb_ok)
                    ke_ok = mul(pool, Ex[:, 2, :], Ex[:, 2, :], Kb)
                    yield
                    for j, (src, ok, s) in enumerate(((Qd, qd_ok, S0), (Ex[:, 0, :], k2_ok, S1), (Qr, qn_ok, S0), (Ex[:, 1, :], kd_ok, S1))):
                        for hp in range(HP):
                            m = pe.do(lambda e: e.transpose(pair(s)[:, hp * P:(hp + 1) * P], src[:, hp * P:(hp + 1) * P], ident), ok, *fr(s), sig="tr" if hp == 7 else None)
                        tr_ok = act.do(lambda e: e.copy(DT[:, j, :, :], pair(s).rearrange("p (h n) -> p h n", n=P)), m)
                        setf(s, tr_ok)
                    yield
                    for hp in range(HP):
                        for s2 in range(2):
                            for c in range(2):
                                r = slice(64 * s2, 64 * s2 + 64)
                                q = slice(64 * c, 64 * c + 64)
                                m = pe.do(lambda e: e.matmul(pair(2 * s2)[q, hp * P:(hp + 1) * P], DT[r, 3, hp, q], DT[r, 0:2, hp, q], start=True, stop=True),
                                          tr_ok, *fr(S0), *fr(S1), sig="la" if hp == 7 and c == 1 else None)
                    for s2 in range(2):
                        v = pair(2 * s2).rearrange("p (h k i) -> p h k i", k=2, i=BLK)
                        for k, (dst, mask) in enumerate(((AT, "mask_a"), (LT, "mask_l"))):
                            a = dve.do(lambda e: e.copy_predicated(dst.rearrange("p (h s) i -> p h s i", s=2)[:, :, s2, :],
                                       bc(C(mask).bitcast(U32), 1, HP), v[:, :, k, :]), m, zt, pool.last)
                        setf(2 * s2, a)
                    la_ok = a
                    yield
                    eye = bc(C("eye_chunk"), 1, H1)
                    Cm, Pm = h16(Qd), h16(sq)

                    def each(s, lhs, rhs, *w):
                        for h in range(H1):
                            for c in range(2):
                                q = slice(64 * c, 64 * c + 64)
                                m = pe.do(lambda e: e.matmul(pair(s)[q, h * 64:(h + 1) * 64], lhs(h)[q], rhs(h)[q], start=True, stop=True), *w, *fr(s),
                                          sig="inv" if h == H1 - 1 and c == 1 else None)
                        return m
                    a = pool.do(lambda e: e.tensor_tensor(Cm, LT, bc(C("lev2"), 1, H1), ALU.mult), la_ok, pe.last)
                    m = each(S0, lambda h: Cm[:, h, :], lambda h: C("eye_chunk"), a)
                    u_ok = dve.do(lambda e: e.tensor_tensor(Um, eye, Cm, ALU.subtract), a, pe.last)
                    t_ok = dve.do(lambda e: e.tensor_tensor(Tm, eye, h16(pair(S0)), ALU.subtract), m)
                    setf(S0, t_ok)
                    for lev in (4, 8, 16, 32, 64):
                        a = pool.do(lambda e: e.tensor_tensor(Cm, LT, bc(C(f"lev{lev}"), 1, H1), ALU.mult), pe.last, dve.last)
                        m = each(S1, lambda h: Cm[:, h, :], lambda h: Tm[:, h, :], a, t_ok)
                        p_ok = act.do(lambda e: e.copy(Pm, h16(pair(S1))), m)
                        setf(S1, p_ok)
                        if lev < 64:
                            m1 = each(S0, lambda h: Um[:, h, :], lambda h: Pm[:, h, :], p_ok, u_ok)
                        m2 = each(S1, lambda h: Pm[:, h, :], lambda h: Um[:, h, :], p_ok, u_ok)
                        if lev < 64:
                            t_ok = dve.do(lambda e: e.tensor_tensor(Tm, Tm, h16(pair(S0)), ALU.subtract), m1, m2)
                            setf(S0, t_ok)
                        u_ok = dve.do(lambda e: e.tensor_tensor(Um, Um, h16(pair(S1)), ALU.subtract), m2)
                        setf(S1, u_ok)
                        yield
                    TKT, TV, W, O = Ex[:, 0, :], h16(Ex[:, 1, :]), h16(Kb), h16(Kr)
                    for h in range(H1):
                        for c in range(2):
                            q, r = slice(64 * c, 64 * c + 64), slice(64 * (h % 2), 64 * (h % 2) + 64)
                            m = pe.do(lambda e: e.matmul(bank(c)[r, (h // 2) * 64:(h // 2) * 64 + 64], h16(Ex[:, 3, :])[q, h, :], Um[q, h, :], start=True, stop=True),
                                      kt_ok, u_ok, *fr(S0), sig="tk" if h == H1 - 1 else None)
                    tk_ok = act.do(lambda e: e.copy(TKT, pair(S0)), m)
                    setf(S0, tk_ok)
                    m = each(S1, lambda h: Um[:, h, :], lambda h: h16(Vr)[:, h, :])
                    tv_ok = act.do(lambda e: e.copy(TV, h16(pair(S1))), m)
                    setf(S1, tv_ok)
                    m = each(S0, lambda h: AT[:, h, :], lambda h: h16(Vr)[:, h, :])
                    av_ok = act.do(lambda e: e.copy(O, h16(pair(S0))), m)
                    setf(S0, av_ok)
                    yield
                    for c in range(2):
                        q = slice(64 * c, 64 * c + 64)
                        for s, lhs in ((S0, lambda r, h: TKT[r, c * 512 + (h // 2) * 64:c * 512 + (h // 2) * 64 + 64]), (S1, lambda r, h: DT[r, 2, h // 2, q])):
                            for h in range(H1):
                                r = slice(64 * (h % 2), 64 * (h % 2) + 64)
                                m = pe.do(lambda e: e.matmul(bank(s + h % 2)[q, (h // 2) * 64:(h // 2) * 64 + 64], lhs(r, h), S[r, h // 2, :], start=True, stop=True),
                                          tk_ok, st_ok, *fr(s), sig="ws" if h >= H1 - 2 else None)
                            v = pair(s)[q].rearrange("p (s h e) -> p h s e", s=2, e=DK)
                            if s == S0:
                                w_ok = dve.do(lambda e: e.tensor_tensor(W[q].rearrange("p (h s) e -> p h s e", s=2), TV[q].rearrange("p (h s) e -> p h s e", s=2), v, ALU.subtract), m, tv_ok)
                                setf(s, w_ok)
                            else:
                                o_ok = dve.do(lambda e: e.tensor_tensor(O[q].rearrange("p (h s) e -> p h s e", s=2), O[q].rearrange("p (h s) e -> p h s e", s=2), v, ALU.add), m, av_ok)
                                setf(s, o_ok)
                        for h in range(H1):
                            r = slice(64 * (h % 2), 64 * (h % 2) + 64)
                            m = pe.do(lambda e: e.matmul(bank(0)[r, (h // 2) * 64:(h // 2) * 64 + 64], h16(Ex[:, 2, :])[q, h, :], W[q, h, :], start=True, stop=True),
                                      ke_ok, w_ok, sig="su" if h == H1 - 1 else None)
                        a = dve.do(lambda e: e.tensor_tensor(S, S, bc(gE[:, :, c], 2, DK), ALU.mult), m, ge_ok)
                        st_ok = dve.do(lambda e: e.tensor_tensor(S, S, bank(0).rearrange("p (h e) -> p h e", e=DK), ALU.add), a)
                        setf(S0, st_ok)
                        yield
                    Of = O.rearrange("p h d -> p (h d)")
                    a = pool.do(lambda e: e.tensor_tensor(sq, Of, Of, ALU.mult), o_ok, pe.last)
                    a = dve.do(lambda e: e.tensor_reduce(stat[:, 3, :], h16(sq), AX, ALU.add), a)
                    a = dve.do(lambda e: e.tensor_scalar(stat[:, 4, :], stat[:, 3, :], 1.0 / DK, EPS1, ALU.mult, ALU.add), a)
                    a = rsqrt(stat[:, 4, :], stat[:, 3, :], a)
                    a = dve.do(lambda e: e.tensor_tensor(stat[:, 3, :], stat[:, 3, :], gate[:, t, :], ALU.mult), a)
                    a = dve.do(lambda e: e.tensor_tensor(O, O, bc(stat[:, 3, :], 2, DK), ALU.mult), a)
                    for hp in range(HP):
                        m = pe.do(lambda e: e.transpose(pair(S0)[:, hp * P:(hp + 1) * P], Of[:, hp * P:(hp + 1) * P], ident), a, *fr(S0), sig="ot" if hp == 7 else None)
                    ot_ok = act.do(lambda e: e.copy(Qr, pair(S0)), m)
                    setf(S0, ot_ok)
                    for hp in range(HP):
                        m = pe.do(lambda e: e.matmul(bank(S1)[:, 0:D], Qr[:, hp * P:(hp + 1) * P], w_o[:, hp, :], start=(hp == 0), stop=(hp == HP - 1)), ot_ok, wo_ok, *fr(S1), sig="op" if hp == 7 else None)
                    setf(S1, add_out(n, 1, bank(S1)[:, 0:D].unsqueeze(1), m))
                    yield

    streams = [(delta(), 2), (mixture(), 1)]
    while streams:
        for g, k in list(streams):
            for _ in range(k):
                try:
                    next(g)
                except StopIteration:
                    streams.remove((g, k))
                    break
    sp.do(lambda e: e.drain(), outs_ok[-1], sig=None)


def layout(v):
    f = lambda a: np.ascontiguousarray(a)
    A = {}
    A["cst"], A["cst0"], _, own = constants()
    A["own"] = f(own[0:E1 + NS1])
    A["x"] = f(v["L0_attn_x"].reshape(NT, P, D).transpose(1, 0, 2))
    A["wqkv0"] = f(v["L0_attn_qkv_w"].T)
    A["b0"] = f(v["L0_attn_qkv_b"].reshape(3, D).T)
    A["bv0"] = f(v["L0_attn_qkv_b"][2 * D:].reshape(1, D))
    A["pb0"] = f(v["L0_attn_proj_b"].reshape(1, D))
    A["pw0"] = f(v["L0_attn_proj_w"].T.reshape(HP, 2, D0, D).transpose(0, 2, 1, 3).reshape(64, 2, D))
    A["wr"], A["br"] = f(v["L0_ffn_Wr"]), f(v["L0_ffn_br"].reshape(1, E0))
    w1 = v["L0_ffn_W1"].reshape(E0 * P, F0)
    w2 = v["L0_ffn_W2"].reshape(E0, 4, P, D).transpose(0, 2, 1, 3).reshape(E0 * P, 4 * D)
    b1 = v["L0_ffn_b1"].reshape(E0, 4, P).transpose(0, 2, 1).reshape(E0 * P, 4)
    A["w12"] = f(np.concatenate([w1, w2, b1], 1))
    A["b2"] = f(v["L0_ffn_b2"])
    pad = lambda a: np.concatenate([a, np.zeros((IW - a.shape[0],) + a.shape[1:], a.dtype)], 0)
    gp = np.concatenate([v["L1_ffn_gate_proj"].reshape(-1, D), v["L1_ffn_shared_gate_w"]], 0)
    up = np.concatenate([v["L1_ffn_up_proj"].reshape(-1, D), v["L1_ffn_shared_up_w"]], 0)
    dn = np.concatenate([v["L1_ffn_down_proj"].transpose(0, 2, 1).reshape(-1, D), v["L1_ffn_shared_down_w"].T], 0)
    A["w_gu"] = f(np.stack([pad(gp).T, pad(up).T], 1))
    A["w_dn"] = f(pad(dn).reshape(IT, P, D).transpose(1, 0, 2))
    for c in "qkv":
        A[f"w_{c}"] = f(v[f"L1_attn_W{c}"].T)
        A[f"b_{c}"] = f(v[f"L1_attn_b{c}"].reshape(1, -1))
    A["w_au"] = f(np.concatenate([v["L1_attn_Wau"].T, v["L1_attn_bau"].reshape(1, -1)], 0))
    A["w_o"] = f(v["L1_attn_Wo"].T.reshape(HP, P, D).transpose(1, 0, 2))
    rows = lambda a: np.concatenate([a, np.zeros((P - a.shape[0],) + a.shape[1:], a.dtype)], 0)
    conv = [np.concatenate([v[f"L1_attn_w{c}_conv"][:, 0, :], v[f"L1_attn_b{c}_conv"][:, None]], 1) for c in "qkv"]
    A["small1"] = f(np.concatenate(conv + [
        v["L1_attn_rms_w"].reshape(HP, P).T, v["L1_attn_Wad"].T, v["L1_attn_Wgd"].T,
        rows(v["L1_attn_bad"][:, None]), rows(v["L1_attn_bgd"][:, None]),
        v["L1_attn_Wbeta"].T, v["L1_ffn_gate_w"].T, rows(np.concatenate([v["L1_attn_Wgu"].T, v["L1_attn_bgu"].reshape(1, -1)], 0))], 1))
    A["smallb"] = f(np.concatenate([v["L1_attn_bbeta"], v["L1_ffn_gate_bias"], v["L1_attn_bo"]]).reshape(1, -1))
    return A


def kernel(**inputs):
    import concourse.bacc as bacc
    from concourse.bass_utils import run_bass_kernel_spmd

    arrays = layout({k: np.asarray(a) for k, a in inputs.items()})
    nc = bacc.Bacc("TRN2", target_bir_lowering=False, num_devices=1)
    feed, ins = {}, {}
    for name, a in arrays.items():
        feed[f"in_{name}"] = a
        ins[name] = nc.dram_tensor(f"in_{name}", a.shape, mybir.dt.from_np(a.dtype), kind="ExternalInput").ap()
    ins["cw_park"] = nc.dram_tensor("cw_park", (E1 + NS1, NT * P), F32).ap()
    out = nc.dram_tensor("out_x", (P, NT, D), F32, kind="ExternalOutput").ap()
    program(nc, ins, out)
    r = run_bass_kernel_spmd(nc, [feed], core_ids=[0])
    y = r.results[0]["out_x"]
    return np.ascontiguousarray(np.asarray(y).reshape(P, NT, D).transpose(1, 0, 2)).reshape(B, T, D)
```

```python
from contextlib import ExitStack

import numpy as np

import concourse.bass as bass
from concourse import mybir

F32 = mybir.dt.float32
BF16 = mybir.dt.bfloat16
U16 = mybir.dt.uint16
I32 = mybir.dt.int32
U32 = mybir.dt.uint32
ALU = mybir.AluOpType
ACT = mybir.ActivationFunctionType
AX = mybir.AxisListType.X

P = 128
B, T, D = 4, 1024, 128
TT = T // P
NT = B * TT
BLK = 64
H0, D0 = 16, 8
HP = 8
F0, E0 = 512, 8
H1, DK = 16, 64
R1 = 64
E1, I1, NS1, K1 = 16, 176, 2, 4
IT = -(-(E1 + NS1) * I1 // P)
IW = IT * P
EPS_LN, EPS1 = 1e-05, 1e-06
NEG = -1e30
KW = 4


def constants():
    i = np.arange(P)
    parts = {}
    parts["ident"] = np.eye(P)
    c, r = i // BLK, i % BLK
    same = (c[:, None] == c[None, :])
    upto = same & (r[:, None] <= r[None, :])
    tomid = same & (r[:, None] < BLK // 2)
    parts["cum_mid"] = tomid - upto.astype(float)
    parts["cum_end"] = -1.0 * (same & (r[:, None] > r[None, :]))
    parts["cum"] = -1.0 * upto
    parts["chunk_of"] = -1.0 * (c[:, None] == np.arange(2)[None, :])
    parts["one"] = np.ones((P, 1))
    ii = np.arange(BLK)[None, :]
    parts["mask_a"] = (r[:, None] <= ii)
    parts["mask_l"] = (r[:, None] < ii)
    for s in (32, 64):
        parts[f"lev{s}"] = (r[:, None] // s == ii // s) & (r[:, None] % s < s // 2) & (ii % s >= s // 2)
    parts["sub_eye"] = (np.arange(16)[None, :, None] == (4 * (i % 32 // 8)[:, None, None] + np.arange(4)[None, None, :])).reshape(P, 64)
    parts["sixteen_of"] = (r[:, None] // 16 == np.arange(4)[None, :])
    parts["head_of"] = (i[:, None] // D0 == np.arange(H0)[None, :])
    parts["causal_q"] = np.where(r[:, None] < ii, NEG, 0.0)
    parts["causal_k"] = np.where(ii < r[:, None], NEG, 0.0)
    parts["two_eyes"] = (i[:, None] == np.arange(P)[None, :] % BLK) & (i[:, None] < BLK)
    parts["eye_hi"] = (i[:, None] + BLK == np.arange(P)[None, :])
    blk = np.arange(T) // BLK
    parts["blk_of"] = (i[:, None] == blk[None, :])
    parts["iota8"] = np.broadcast_to(np.arange(E0), (P, E0))
    parts["rowid"] = i[:, None]
    e = np.arange(E1)
    parts["before16"] = np.broadcast_to((e[None, :] < e[:, None]).reshape(1, -1), (P, 256))
    g = np.arange(4)
    parts["before4"] = np.broadcast_to((g[None, :] < g[:, None]).reshape(1, -1), (P, 16))
    only0 = ("head_of", "causal_q", "causal_k", "two_eyes", "eye_hi", "blk_of", "iota8", "rowid")
    at, cols, n = {}, ([], []), [0, 0]
    for k, v in parts.items():
        v = np.asarray(v, np.float32)
        z = int(k in only0)
        at[k] = (z, n[z], v.shape[1])
        n[z] += v.shape[1]
        cols[z].append(v)
    own = np.zeros((96, IW), np.uint16)
    for x in range(E1 + NS1):
        own[x::32, x * I1:(x + 1) * I1] = 0x3F80
    return np.concatenate(cols[0], 1), np.concatenate(cols[1], 1), at, own


class Engine:

    def __init__(self, name, eng, semaphore):
        self.name, self.eng, self.semaphore = name, eng, semaphore
        self.counts, self.waited, self.pending, self.last = {}, {}, [], None

    def do(self, issue, *waits, sig="done", inc=1):
        own = [self.last] if self.name in ("dve", "act", "pool") else []
        for w in list(waits) + self.pending + own:
            if w and self.waited.get(w[0], 0) < w[1]:
                self.waited[w[0]] = w[1]
                if self.eng is not None:
                    self.eng.wait_ge(self.semaphore(w[0]), w[1])
        self.pending = []
        ins = issue(self.eng) if self.eng is not None else None
        if not sig:
            return None
        key = f"{self.name}_{sig}"
        self.counts[key] = self.counts.get(key, 0) + inc
        self.last = (key, self.counts[key])
        if ins is not None:
            ins.then_inc(self.semaphore(key), inc)
        else:
            self.semaphore(key)
        return self.last


def bc(ap, axis, n):
    a = ap.unsqueeze(axis)
    shape = list(a.shape)
    shape[axis] = n
    return a.broadcast_to(shape)


def program(nc, ins, out):
    with ExitStack() as ctx:
        made = {}

        def sbuf(name, shape):
            if name not in made:
                made[name] = ctx.enter_context(nc.sbuf_tensor(name, shape, F32))
            return made[name][:]

        def psum(name, shape):
            if name not in made:
                made[name] = ctx.enter_context(nc.psum_tensor(name, shape, F32))
            return made[name][:]

        def semaphore(name):
            if name not in made:
                made[name] = ctx.enter_context(nc.semaphore(name))
            return made[name]

        def write(name, eng):
            engines = [Engine(n, eng if n == name else None, semaphore) for n in ("pe", "dve", "act", "pool", "sp")]
            describe(engines, sbuf, psum, ins, out)

        write(None, None)
        with nc.Block() as block:
            @block.tensor
            def _(eng):
                write("pe", eng)

            @block.vector
            def _(eng):
                write("dve", eng)

            @block.scalar
            def _(eng):
                write("act", eng)

            @block.gpsimd
            def _(eng):
                write("pool", eng)

            @block.sync
            def _(eng):
                write("sp", eng)


def describe(engines, sb, psum, ins, out):
    pe, dve, act, pool, sp = engines
    ps = psum("ps", [P, 8, 512])
    bank = lambda i: ps[:, i, :]
    pair = lambda i: ps[:, i:i + 2, :].rearrange("p a n -> p (a n)")
    free = [None] * 8

    def barrier():
        for e in engines:
            e.pending = [o.last for o in engines if o is not e and o.last] + e.pending

    xres = sb("xres", [P, NT, D])
    xnT = sb("xnT", [P, B, T + KW - 1])
    cst_np, cst0_np, at, _ = constants()
    cst = sb("cst", [P, cst_np.shape[1]])
    w_gu = sb("w_gu", [P, 2, IW])
    w_dn = sb("w_dn", [P, IT, D])
    cst0 = w_gu[:, 1, 0:cst0_np.shape[1]]

    def C(k):
        z, n, m = at[k]
        return (cst, cst0)[z][:, n:n + m]
    w_q, w_k, w_v = (sb(f"w_{c}", [P, H1 * DK]) for c in "qkv")
    w_au = sb("w_au", [R1 + 1, H1 * DK])
    w_o = sb("w_o", [P, HP, D])
    b_qk = sb("b_qk", [P, 2, H1 * DK])
    b_v = sb("b_v", [P, H1 * DK])
    small = sb("small", [P, 640])
    own = sb("own", [96, 2, 256]).bitcast(BF16)
    WORK = 24600
    work = sb("work", [P, WORK])
    used = [0, 0]

    def take(pool_i, *shape):
        buf, size = ((work, WORK), (small, 640))[pool_i]
        n = int(np.prod(shape))
        v = buf[:, used[pool_i]:used[pool_i] + n]
        used[pool_i] += n
        assert used[pool_i] <= size, (pool_i, used)
        if len(shape) > 1:
            names = "abcdef"[:len(shape)]
            v = v.rearrange(f"p ({' '.join(names)}) -> p {' '.join(names)}", **dict(zip(names, shape)))
        return v

    act.do(lambda e: e.preload_act_table_set("natural_log_exp_and_others"), sig=None)

    def load(dst, src, name, eng=sp):
        return eng.do(lambda e: e.dma_start(dst, src), sig=f"ld_{name}", inc=16)

    load(cst, ins["cst"], "cst")
    ld_c = load(cst0, ins["cst0"], "cst")
    ld_x = [load(xres[:, b * TT:(b + 1) * TT, :], ins["x"][:, b * TT:(b + 1) * TT, :], f"x{b}") for b in range(B)]
    b0 = take(1, 3)
    pw = take(1, 2, D)
    wr = take(1, E0)
    brb = take(1, E0)
    bvb = take(1, D)
    pbb = take(1, D)
    wqkv0 = w_gu[:, 0, 0:3 * D]
    ld_s = None
    for dst, key in ((wqkv0, "wqkv0"), (b0, "b0"), (wr, "wr")):
        ld_s = load(dst, ins[key], "s0")
    ld_s = load(pw[0:64, :, :], ins["pw0"], "s0")
    for dst, key in ((brb, "br"), (bvb, "bv0"), (pbb, "pb0")):
        ld_s = load(dst, ins[key].partition_broadcast(P)[:, 0, :], "s0")
    ident = C("ident")

    nwt = sb("nwt", [P, 3, 2, H1])

    def rsqrt_steps(x, y, ok, z=0):
        n = x.shape[1]
        u, w = nwt[:, z, 0, 0:n], nwt[:, z, 1, 0:n]
        a = act.do(lambda e: e.activation(u, x, ACT.Ln), ok)
        a = act.do(lambda e: e.activation(y, u, ACT.Exp, scale=-0.5), a)
        yield
        a = dve.do(lambda e: e.tensor_tensor(w, y, y, ALU.mult), a)
        a = dve.do(lambda e: e.tensor_tensor(w, w, x, ALU.mult), a)
        a = dve.do(lambda e: e.tensor_scalar(w, w, -0.5, 1.5, ALU.mult, ALU.add), a)
        return dve.do(lambda e: e.tensor_tensor(y, y, w, ALU.mult), a)

    def at_once(steps):
        while True:
            try:
                next(steps)
            except StopIteration as end:
                return end.value

    def sigmoid(dst, z, *ok, scale=-1.0):
        a = act.do(lambda e: e.activation(dst, z, ACT.Exp, scale=scale), *ok)
        a = act.do(lambda e: e.activation(dst, dst, ACT.Ln, bias=C("one")[0:dst.shape[0], :]), a, ld_c)
        return act.do(lambda e: e.activation(dst, dst, ACT.Exp, scale=-1.0), a)

    st = take(1, TT, 6)
    mv = take(1, TT, 2)
    rs = take(1, TT)
    ve = take(1, TT)
    z_pad = pool.do(lambda e: e.memset(xnT[:, :, 0:KW - 1], 0.0))

    def norm(b, xn, ready, banks, xn_free):
        for t in range(TT):
            x = xres[:, b * TT + t, :]
            a = dve.do(lambda e: e.bn_stats(st[:, t, :], x), *ready)
        for t in range(TT):
            a2 = dve.do(lambda e: e.bn_aggr(mv[:, t, :], st[:, t, :]), a)
        a = dve.do(lambda e: e.tensor_scalar(ve, mv[:, :, 1], EPS_LN, None, ALU.add), a2)
        a = at_once(rsqrt_steps(ve, rs, a))
        for t in range(TT):
            x = xres[:, b * TT + t, :]
            a = dve.do(lambda e: e.tensor_scalar(xn[:, t, :], x, mv[:, t, 0:1], rs[:, t:t + 1],
                                                           ALU.subtract, ALU.mult), a, *xn_free)
        for g in range(TT // 4):
            k = banks[g % len(banks)]
            for q in range(4):
                t = 4 * g + q
                m = pe.do(lambda e: e.transpose(bank(k)[:, q * P:(q + 1) * P], xn[:, t, :], ident),
                          a, ld_c, free[k], sig="nT" if q == 3 else None)
            free[k] = act.do(lambda e: e.copy(xnT[:, b, KW - 1 + g * 512:KW - 1 + (g + 1) * 512],
                                                            bank(k)), m, sig="xnT")
        return free[k]

    xn = take(0, TT, D)
    xnT_ok = []
    xn_free = ()
    for b in range(B):
        tok = norm(b, xn, (ld_x[b],), (0, 1), xn_free)
        xn_free = (pe.last,)
        xnT_ok.append(tok)
    used[0] = 0
    KT = take(0, B, T)
    Vbd = take(0, TT, HP, 2, 18)
    Qbd = take(0, H0, BLK)
    pT = take(0, TT, H0 * BLK)
    Oall = take(0, B, HP, 16, 9)
    w12 = KT.rearrange("p b t -> p (b t)")[:, 0:2 * 1028].rearrange("p (s n) -> p s n", s=2)
    small_q = take(0, BLK)
    mx = take(0, 2, HP, 16)
    em = take(0, B, HP, 16)
    barrier()
    xT = lambda b, lo, n: xnT[:, b, KW - 1 + lo:KW - 1 + lo + n]

    for b in range(B):
        for g in range(2):
            k = (2 * b + g) % 4
            m = pe.do(lambda e: e.matmul(bank(k), wqkv0[:, D:2 * D], xT(b, g * 512, 512), start=True, stop=True),
                      free[k], ld_s, xnT_ok[b])
            kT_ok = free[k] = act.do(lambda e: e.activation(KT[:, b, g * 512:(g + 1) * 512], bank(k), ACT.Identity,
                                                                           bias=b0[:, 1:2]), m, ld_s)
    nmT = take(0, H0 * BLK)[0:16, :]
    Vs = take(0, TT, D)
    z1 = pool.do(lambda e: e.memset(Vbd, 0.0))
    V5 = Vbd.rearrange("p t h k (s x) -> p t h k s x", s=2)
    for kb in range(2):
        ones_ok = pool.do(lambda e: e.memset(V5[kb * 64:(kb + 1) * 64, :, :, kb, :, 8:9].rearrange("p t h s x -> p (t h) s x"), 1.0), z1)
    attn_tail = None
    for b in range(B):
        m = pe.do(lambda e: e.matmul(bank(0)[:, 0:BLK], wqkv0[:, 0:D], xT(b, T - BLK, BLK), start=True, stop=True), free[0], kT_ok)
        a = act.do(lambda e: e.activation(small_q, bank(0)[:, 0:BLK], ACT.Identity, bias=b0[:, 0:1]), m, dve.last)
        free[0] = a
        q_ok = dve.do(lambda e: e.tensor_tensor(Qbd, bc(small_q, 1, H0), bc(C("head_of"), 2, BLK), ALU.mult), a, pe.last)
        for g in range(2):
            for q in range(4):
                t = 4 * g + q
                m = pe.do(lambda e: e.matmul(bank(1 + g)[:, q * D:(q + 1) * D], xT(b, t * P, P), wqkv0[:, 2 * D:3 * D],
                                                                 start=True, stop=True), free[1 + g], sig="v0" if q == 3 else None)
            a = dve.do(lambda e: e.tensor_tensor(Vs[:, 4 * g:4 * g + 4, :], bank(1 + g).rearrange("p (q d) -> p q d", d=D),
                                                      bc(bvb, 1, 4), ALU.add), m, pe.last, pool.last)
            free[1 + g] = a
        for kb in range(2):
            rows = slice(kb * 64, (kb + 1) * 64)
            for s in range(2):
                v_ok = pool.do(lambda e: e.tensor_copy(
                    V5[rows, :, :, kb, s, 0:8], Vs[rows, :, :].rearrange("p t (h s x) -> p t h s x", s=2, x=8)[:, :, :, s, :]), a, ones_ok, pe.last)
        for hp in range(HP):
            for g in range(2):
                k = 4 + (2 * hp + g) % 4
                m = pe.do(lambda e: e.matmul(bank(k), Qbd[:, 2 * hp:2 * hp + 2, :], KT[:, b, g * 512:(g + 1) * 512],
                                                                   start=True, stop=True), free[k], q_ok)
                if g == 1:
                    m = pe.do(lambda e: e.matmul(bank(k)[:, 448:512], C("two_eyes")[0:64, :], C("causal_q")[0:64, :],
                                                      start=False, stop=True, skip_group_check=True))
                a = dve.do(lambda e: e.tensor_reduce(mx[:, 0, hp, 8 * g:8 * g + 8], bank(k).rearrange("p (j n) -> p j n", n=BLK), AX, ALU.max), m)
                free[k] = a
        src = 0
        for s in (1, 2, 4, 8):
            x, y = mx[:, src], mx[:, 1 - src]
            a1 = dve.do(lambda e: e.tensor_tensor(y[:, :, s:16], x[:, :, s:16], x[:, :, 0:16 - s], ALU.max), a, pe.last)
            a = dve.do(lambda e: e.tensor_copy(y[:, :, 0:s], x[:, :, 0:s]), a1)
            src = 1 - src
        mrun, tmp = mx[:, src], mx[:, 1 - src]
        a1 = dve.do(lambda e: e.tensor_tensor(tmp[:, :, 1:16], mrun[:, :, 0:15], mrun[:, :, 1:16], ALU.subtract), a)
        act.do(lambda e: e.activation(em[:, b, :, 1:16], tmp[:, :, 1:16], ACT.Exp, scale=D0 ** -0.5), a1)
        for hp in range(HP):
            k = hp // 4
            m = pe.do(lambda e: e.transpose(bank(k)[0:16, (hp % 4) * P:(hp % 4 + 1) * P], mrun[:, hp, :], ident), a, free[k], sig="mT" if hp % 4 == 3 else None)
        nm_ok = act.do(lambda e: e.mul(nmT, pair(0)[0:16, :], -1.0), m)
        free[0] = free[1] = nm_ok
        for kt in range(TT):
            k = 4 + 2 * (kt % 2)
            for g in range(2):
                kk = k + g
                pe.do(lambda e: e.matmul(bank(kk), KT[:, b, kt * P:(kt + 1) * P], Qbd[:, 8 * g:8 * g + 8, :], start=True, stop=False), free[kk], sig=None)
                m = pe.do(lambda e: e.matmul(bank(kk), C("blk_of")[0:16, kt * P:(kt + 1) * P], nmT[:, g * 512:(g + 1) * 512], start=False, stop=(kt < TT - 1)), nm_ok)
                if kt == TT - 1:
                    m = pe.do(lambda e: e.matmul(bank(kk), C("eye_hi")[0:64, :], bc(C("causal_k")[0:64, :], 1, 8), start=False, stop=True))
            e_ok = act.do(lambda e: e.activation(pT[:, kt, :], pair(k), ACT.Exp, scale=D0 ** -0.5), m)
            free[k] = free[k + 1] = e_ok
        for hp in range(HP):
            k = hp % 4
            for kt in range(TT):
                m = pe.do(lambda e: e.matmul(bank(k)[:, kt * 36:(kt + 1) * 36], pT[:, kt, hp * P:(hp + 1) * P], Vbd[:, kt, hp, :, :].rearrange("p k x -> p (k x)"),
                                                                start=True, stop=True), free[k], e_ok, v_ok, sig="pv" if kt == TT - 1 else None)
            for s in range(2):
                rows = slice(64 * s, 64 * s + 64)
                free[k] = o_ok = dve.do(lambda e: e.tensor_copy(
                    Oall[rows, b, hp, :, :], bank(k)[rows, 0:288].rearrange("p (j s x) -> p j s x", s=2, x=9)[:, :, s, :]), m)
    flat = pT.rearrange("p t n -> p (t n)")
    lsum, rr = (flat[:, o:o + 512].rearrange("p (b h j) -> p b h j", b=B, h=HP) for o in (2048, 2560))
    acc, df = (flat[:, o:o + 256].rearrange("p (b h x) -> p b h x", b=B, h=HP) for o in (3072, 3328))
    a = dve.do(lambda e: e.tensor_copy(lsum[:, :, :, 0], Oall[:, :, :, 0, 8]), o_ok, act.last, pe.last)
    for j in range(1, 16):
        a = dve.do(lambda e: e.tensor_tensor(lsum[:, :, :, j], lsum[:, :, :, j - 1], em[:, :, :, j], ALU.mult), a)
        a = dve.do(lambda e: e.tensor_tensor(lsum[:, :, :, j], lsum[:, :, :, j], Oall[:, :, :, j, 8], ALU.add), a)
    a = dve.do(lambda e: e.reciprocal(rr, lsum), a)
    rl = flat[:, 3584:3616].rearrange("p (b h) -> p b h", b=B)
    a2 = dve.do(lambda e: e.tensor_copy(rl, rr[:, :, :, 15]), a)
    a = dve.do(lambda e: e.tensor_tensor(rr[:, :, :, 1:16], lsum[:, :, :, 0:15], rr[:, :, :, 1:16], ALU.mult), a2)
    a = dve.do(lambda e: e.memset(acc, 0.0), a)
    for j in range(1, 16):
        a = dve.do(lambda e: e.tensor_tensor(df, Oall[:, :, :, j, 0:8], acc, ALU.subtract), a)
        a = dve.do(lambda e: e.tensor_tensor(df, df, bc(rr[:, :, :, j], 3, D0), ALU.mult), a)
        a = dve.do(lambda e: e.tensor_tensor(acc, acc, df, ALU.add), a)
    fin_ok = dve.do(lambda e: e.tensor_tensor(acc, acc, bc(rl, 3, D0), ALU.mult), a)
    for b in range(B):
        xb_ok = dve.do(lambda e: e.tensor_tensor(xres[:, b * TT:(b + 1) * TT, :], xres[:, b * TT:(b + 1) * TT, :], bc(pbb, 1, TT), ALU.add), ld_s, fin_ok)
    oT = Vs
    for b in range(B):
        m = pe.do(lambda e: e.transpose(bank(0)[0:64, 0:P], acc[:, b, :, :].rearrange("p h x -> p (h x)"), ident), fin_ok, free[0])
        a = act.do(lambda e: e.copy(oT[0:64, b, :], bank(0)[0:64, 0:P]), m)
        free[0] = a
        for s in range(2):
            m = pe.do(lambda e: e.matmul(bank(1)[64:128, 0:D], oT[0:64, b, 64 * s:64 * s + 64], pw[0:64, s, :], start=(s == 0), stop=(s == 1)), a, free[1])
        row = xres[64:128, b * TT + TT - 1, :]
        free[1] = dve.do(lambda e: e.tensor_tensor(row, row, bank(1)[64:128, 0:D], ALU.add), m, xb_ok)

    meanT = take(0, B)
    mrep = take(0, P)
    sc = take(0, B, E0)
    eq = take(0, B, E0)
    top = take(0, B)
    idxf = take(0, 2, B)
    idx = take(0, 2, B).bitcast(U32)
    b2r = take(0, B, D)
    hT = pT[:, 0:2, :].rearrange("p a (f n) -> p (a f) n", n=512)
    barrier()
    for b in range(B):
        a = dve.do(lambda e: e.tensor_reduce(meanT[:, b:b + 1], xT(b, 0, T), AX, ALU.add))
    a = dve.do(lambda e: e.tensor_scalar(meanT, meanT, 1.0 / T, None, ALU.mult), a)
    for b in range(B):
        a1 = dve.do(lambda e: e.tensor_copy(mrep, meanT[:, b:b + 1].broadcast_to([P, P])), a, pe.last)
        m = pe.do(lambda e: e.matmul(bank(0)[:, 8 * b:8 * b + 8], mrep, wr, start=True, stop=True), a1, free[0])
    a = dve.do(lambda e: e.tensor_tensor(sc, bank(0)[:, 0:32].rearrange("p (b e) -> p b e", e=E0), bc(brb, 1, B), ALU.add), m)
    free[0] = a
    a = dve.do(lambda e: e.tensor_reduce(top, sc, AX, ALU.max), a)
    a = dve.do(lambda e: e.tensor_tensor(eq, sc, bc(top, 2, E0), ALU.is_equal), a)
    a = dve.do(lambda e: e.tensor_scalar(eq, eq, -100.0, 100.0, ALU.mult, ALU.add), a)
    a = dve.do(lambda e: e.tensor_tensor(eq, eq, bc(C("iota8"), 1, B), ALU.add), a)
    a = dve.do(lambda e: e.tensor_reduce(idxf[:, 1, :], eq, AX, ALU.min), a)
    a = dve.do(lambda e: e.tensor_scalar(idxf[:, 0, :], idxf[:, 1, :], float(P), C("rowid"), ALU.mult, ALU.add), a)
    idx_ok = dve.do(lambda e: e.tensor_copy(idx, idxf), a)
    for b in range(B):
        b2_ok = pool.do(lambda e: e.indirect_dma_start(b2r[:, b, :], None, ins["b2"], bass.IndirectOffsetOnAxis(ap=idx[:, 1, b:b + 1], axis=0)),
                        idx_ok, sig="b2", inc=16)
    w_free = [None, None]
    x2_ok = []
    for b in range(B):
        w = w12[:, b % 2, :]
        w_ok = pool.do(lambda e: e.indirect_dma_start(w, None, ins["w12"], bass.IndirectOffsetOnAxis(ap=idx[:, 0, b:b + 1], axis=0)),
                       w_free[b % 2], sig=f"w12{b % 2}", inc=16)
        for g in range(2):
            for f in range(4):
                k = f
                m = pe.do(lambda e: e.matmul(bank(k), w[:, f * P:(f + 1) * P], xT(b, g * 512, 512), start=True, stop=True), w_ok, free[k])
                h_ok = free[k] = act.do(lambda e: e.activation(hT[:, f, :], bank(k), ACT.Relu, bias=w[:, 1024 + f:1025 + f]), m, pe.last)
            k = 4 + g
            for t in range(4):
                for f in range(4):
                    m = pe.do(lambda e: e.matmul(bank(k)[:, t * D:(t + 1) * D], hT[:, f, t * P:(t + 1) * P], w[:, 512 + f * D:512 + (f + 1) * D],
                                                                     start=(f == 0), stop=(f == 3)), h_ok, free[k], sig="y0" if f == 3 else None)
            xs = xres[:, b * TT + 4 * g:b * TT + 4 * g + 4, :]
            a = dve.do(lambda e: e.tensor_tensor(xs, xs, bank(k).rearrange("p (t d) -> p t d", d=D), ALU.add), m)
            free[k] = a
            a = dve.do(lambda e: e.tensor_tensor(xs, xs, bc(b2r[:, b, :], 1, 4), ALU.add), a, b2_ok)
        w_free[b % 2] = pe.last
        x2_ok.append(a)

    barrier()
    used[0] = 0
    used[1] = 0
    st = take(1, TT, 6)
    mv = take(1, TT, 2)
    rs = take(1, TT)
    ve = take(1, TT)
    xn = take(0, TT, D)
    ld1 = None
    for dst, key in ((w_gu, "w_gu"), (w_dn, "w_dn"), (w_q, "w_q"), (w_k, "w_k"), (w_v, "w_v"), (w_au, "w_au"), (w_o, "w_o")):
        ld1 = load(dst, ins[key], "l1")
    for dst, key in ((b_qk[:, 0, :], "b_q"), (b_qk[:, 1, :], "b_k"), (b_v, "b_v")):
        ld1 = load(dst, ins[key].partition_broadcast(P)[:, 0, :], "l1")
    smalls = take(1, ins["small1"].shape[1])
    ld1 = load(smalls, ins["small1"], "l1")
    so = [0]

    def sm(n):
        v = smalls[:, so[0]:so[0] + n]
        so[0] += n
        return v
    convw = sm(15).rearrange("p (c k) -> p c k", k=5)
    rmsw = sm(HP)
    w_ad, w_gd = sm(R1), sm(R1)
    b_ad, b_gd = sm(1), sm(1)
    w_be, w_gate, w_gu16 = sm(H1), sm(E1), sm(H1)
    small_b = take(1, 2 * 16 + D)
    bb, gb = small_b[:, 0:16], small_b[:, 16:32]
    bo_b = small_b[:, 32:32 + D]
    ld1 = load(small_b, ins["smallb"].partition_broadcast(P)[:, 0, :], "l1")
    xn_free = ()
    x1T_ok = []
    for b in range(B):
        x1T_ok.append(norm(b, xn, (), (0, 1), xn_free))
        xn_free = (pe.last,)
    a = None
    for hp in range(HP):
        a = wo_ok = dve.do(lambda e: e.tensor_scalar(w_o[:, hp, :], w_o[:, hp, :], rmsw[:, hp:hp + 1], None, ALU.mult), ld1)
    for b in range(B):
        a = dve.do(lambda e: e.tensor_tensor(xres[:, b * TT:(b + 1) * TT, :], xres[:, b * TT:(b + 1) * TT, :], bc(bo_b, 1, TT), ALU.add), ld1)

    used[0] = 0
    barrier()
    NTE = (NT, E1)
    scores = take(0, *NTE)
    sfc = take(0, *NTE)
    ra = take(0, *NTE)
    rb = take(0, *NTE)
    gs = take(0, NT, 4)
    g2 = take(0, NT, 4)
    gm = take(0, NT, 4)
    cmp16 = take(0, NT, E1, E1)
    cmb = take(0, *NTE)
    cwT = take(0, NT * P)[0:32, :]
    for n in range(NT):
        m = pe.do(lambda e: e.matmul(bank(0)[:, n * 16:(n + 1) * 16], xT(n // TT, (n % TT) * P, P), w_gate, start=True, stop=True), x1T_ok[n // TT], ld1, free[0],
                  sig="lg" if n == NT - 1 else None)
    fl = lambda v: v.rearrange("p n e -> p (n e)")
    free[0] = a = act.do(lambda e: e.activation(fl(scores), bank(0), ACT.Exp, scale=-1.0), m)
    a = dve.do(lambda e: e.tensor_scalar(scores, scores, 1.0, None, ALU.add), a)
    a = dve.do(lambda e: e.reciprocal(scores, scores), a)
    a = dve.do(lambda e: e.tensor_tensor(sfc, scores, bc(gb, 1, NT), ALU.add), a, ld1)
    grp = sfc.rearrange("p n (g k) -> p n g k", k=4)
    first = True
    for i in range(4):
        for j in range(i + 1, 4):
            dst = gs if first else g2
            a = dve.do(lambda e: e.tensor_tensor(dst, grp[:, :, :, i], grp[:, :, :, j], ALU.add), a)
            if not first:
                a = dve.do(lambda e: e.tensor_tensor(gs, gs, g2, ALU.max), a)
            first = False

    def rank_below(dst, val, before, n, keep, a):
        c4 = cmp16.rearrange("p t a b -> p t (a b)")[:, :, 0:n * n].rearrange("p t (a b) -> p t a b", b=n)
        eqm = before.rearrange("p (a b) -> p a b", b=n)
        mine, other = bc(val, 3, n), bc(val, 2, n)
        a = dve.do(lambda e: e.tensor_tensor(c4, other, mine, ALU.is_equal), a)
        a = dve.do(lambda e: e.tensor_tensor(c4, c4, bc(eqm, 1, NT), ALU.mult), a)
        a = dve.do(lambda e: e.tensor_reduce(rank_a[:, :, 0:n], c4, AX, ALU.add), a)
        a = dve.do(lambda e: e.tensor_tensor(c4, other, mine, ALU.is_gt), a)
        a = dve.do(lambda e: e.tensor_reduce(dst, c4, AX, ALU.add), a)
        a = dve.do(lambda e: e.tensor_tensor(dst, dst, rank_a[:, :, 0:n], ALU.add), a)
        return dve.do(lambda e: e.tensor_scalar(dst, dst, keep - 0.5, None, ALU.is_lt), a)

    rank_a = take(0, NT, E1)
    a = rank_below(gm, gs, C("before4"), 4, 2, a)
    ra4 = ra.rearrange("p n (g k) -> p n g k", k=4)
    a = dve.do(lambda e: e.tensor_tensor(ra4, grp, bc(gm, 3, 4), ALU.mult), a)
    a = rank_below(rb, ra, C("before16"), 16, K1, a)
    a = dve.do(lambda e: e.tensor_tensor(cmb, scores, rb, ALU.mult), a)
    a = dve.do(lambda e: e.tensor_reduce(gs[:, :, 0], cmb, AX, ALU.add), a)
    a = dve.do(lambda e: e.tensor_scalar(gs[:, :, 0], gs[:, :, 0], 1e-20, None, ALU.add), a)
    a = dve.do(lambda e: e.reciprocal(gs[:, :, 1], gs[:, :, 0]), a)
    cmb_ok = dve.do(lambda e: e.tensor_tensor(cmb, cmb, bc(gs[:, :, 1], 2, E1), ALU.mult), a)
    ones_ok = pool.do(lambda e: e.memset(cwT, 1.0))
    for g in range(NT // 4):
        k = g % 2
        for q in range(4):
            m = pe.do(lambda e: e.transpose(bank(k)[0:16, q * P:(q + 1) * P], cmb[:, 4 * g + q, :], ident), cmb_ok, free[k], sig="cwT" if q == 3 else None)
        cw_ok = free[k] = act.do(lambda e: e.copy(cwT[0:16, g * 512:(g + 1) * 512], bank(k)[0:16, :]), m, ones_ok)
    cw3 = take(0, NT * P // 2).bitcast(BF16)
    for i in range(3):
        a = act.do(lambda e: e.copy(cw3[32 * i:32 * i + 32, :], cwT), cw_ok)
        if i < 2:
            part = cw3[0:32, :] if i == 0 else cw3[96:128, :]
            if i == 1:
                a = act.do(lambda e: e.copy(part, cwT), a)
            cw_ok = dve.do(lambda e: e.tensor_tensor(cwT, cwT, part, ALU.subtract), a)
    cw_ok = a
    cw_st = sp.do(lambda e: e.dma_start(ins["cw_park"], cw3[0:96, :].bitcast(U16)), cw_ok, sig="cwst", inc=16)
    sp.do(lambda e: e.dma_start(own[:, 0, :].bitcast(U16), ins["cw_park"][:, 0:512]), cw_st, sig="cwld", inc=16)

    barrier()
    used[0] = 0
    touched, shares = {}, {}
    outs_ok = []

    def add_out(n0, cnt, src, wait):
        xs = xres[:, n0:n0 + cnt, :]
        a = dve.do(lambda e: e.tensor_tensor(xs, xs, src, ALU.add), wait, *[touched.get(n) for n in range(n0, n0 + cnt)])
        for n in range(n0, n0 + cnt):
            shares[n] = shares.get(n, 0) + 1
            if shares[n] == 3:
                outs_ok.append(sp.do(lambda e: e.dma_start(out[:, n, :], xres[:, n, :]), a, sig="out", inc=16))
            touched[n] = a
        return a

    s_g, t_u, acts, yT = take(0, 512), take(0, 512), take(0, 2, 512), take(0, 512)
    own_w = take(0, P).bitcast(BF16).rearrange("p (s n) -> p s n", s=2)

    def mixture():
        GA, UB, CWB, YB = 4, 5, 6, 7
        own_free = [None, None]
        ow_free = [None, None]
        act_free = [None, None]
        own_ld = {0: ("sp_cwld", 16)}
        s_free = yT_free = None
        for g in range(NT // 4):
            b, lo = g // 2, (g % 2) * 512
            if g + 1 < NT // 4:
                own_ld[g + 1] = sp.do(lambda e: e.dma_start(own[:, (g + 1) % 2, :].bitcast(U16), ins["cw_park"][:, (g + 1) * 512:(g + 2) * 512]),
                                      own_free[(g + 1) % 2], sig=f"cw{g % 2}", inc=16)
            prev = None
            for it in range(IT + 1):
                if it < IT:
                    ld = sp.do(lambda e: e.dma_start(own_w[0:96, it % 2, :].bitcast(U16), ins["own"][:, it * P:(it + 1) * P]),
                               ow_free[it % 2], sig=f"ow{it % 2}", inc=16)
                    sg = s_g
                    m = pe.do(lambda e: e.matmul(bank(GA), w_gu[:, 0, it * P:(it + 1) * P], xT(b, lo, 512), start=True, stop=True), free[GA], ld1, x1T_ok[b])
                    a_s = sigmoid(sg, bank(GA), m, s_free)
                    mu = pe.do(lambda e: e.matmul(bank(UB), w_gu[:, 1, it * P:(it + 1) * P], xT(b, lo, 512), start=True, stop=True), free[UB])
                    mc = pe.do(lambda e: e.matmul(bank(CWB), own_w[0:96, it % 2, :], own[:, g % 2, :], start=True, stop=True), free[CWB], ld, own_ld[g])
                    ow_free[it % 2] = own_free[g % 2] = mc
                if prev is not None:
                    pit, pa = prev
                    m = pe.do(lambda e: e.matmul(bank(YB), w_dn[:, pit, :], acts[:, pit % 2, :], start=(pit == 0), stop=(pit == IT - 1)), pa, free[YB])
                    act_free[pit % 2] = m
                if it == IT:
                    break
                yield
                free[GA] = a = dve.do(lambda e: e.tensor_tensor(t_u, bank(GA), sg, ALU.mult), a_s)
                s_free = a
                free[UB] = a = dve.do(lambda e: e.tensor_tensor(t_u, bank(UB), t_u, ALU.mult), mu, a)
                ac = acts[:, it % 2, :]
                free[CWB] = a = dve.do(lambda e: e.tensor_tensor(ac, bank(CWB), t_u, ALU.mult), mc, a, act_free[it % 2])
                prev = (it, a)
                yield
            a = act.do(lambda e: e.copy(yT, bank(YB)), m, yT_free)
            free[YB] = a
            yield
            for q in range(4):
                m = pe.do(lambda e: e.transpose(bank(YB)[:, q * P:(q + 1) * P], yT[:, q * P:(q + 1) * P], ident), a, sig="yt" if q == 3 else None)
            yT_free = m
            free[YB] = add_out(4 * g, 4, bank(YB).rearrange("p (t d) -> p t d", d=D), m)
            yield

    G4 = 2
    GT = G4 * P
    NG = NT // G4
    HH = H1 // 2
    HPH = HH // 2
    KH = HH * DK
    h8 = lambda v: v.rearrange("p (h d) -> p h d", d=DK)
    cs = take(0, 3, GT)
    csig = take(0, 3, GT)
    ctmp = csig[:, 0, :]
    low = take(0, 2, GT)
    adT, gdT = low[:, 0, :], low[:, 1, :]
    betagate = take(0, 2, 2, G4, H1)
    shared = {"made": 0, "used": [0, 0], "in_ok": None, "b_ok": [None, None], "reads": [None, None], "gate_reads": [[None, None], [None, None]]}

    def prelude():
        ones_row = pool.do(lambda e: e.memset(low[R1:R1 + 1, :, :], 1.0))
        mm = None
        for g in range(NG):
            b, lo = g * G4 // TT, (g * G4 % TT) * P
            while min(shared["used"]) < g:
                yield
            reads = shared["reads"]
            for c in range(3):
                dst = [ctmp, cs[:, c, :]]
                a = dve.do(lambda e: e.tensor_scalar(dst[0], xnT[:, b, lo:lo + GT], convw[:, c, 0:1], convw[:, c, 4:5], ALU.mult, ALU.add), *reads, x1T_ok[b], ld1, z_pad)
                for k in range(1, KW):
                    a = dve.do(lambda e: e.scalar_tensor_tensor(dst[k % 2], xnT[:, b, lo + k:lo + k + GT], convw[:, c, k:k + 1], dst[(k + 1) % 2], ALU.mult, ALU.add), a)
                yield
            s = sigmoid(csig, cs, a)
            yield
            shared["in_ok"] = dve.do(lambda e: e.tensor_tensor(cs, cs, csig, ALU.mult), s)
            pre = csig[0:R1, 0:2, :]
            for i, (w_, b_) in enumerate(((w_ad, b_ad), (w_gd, b_gd))):
                m = pe.do(lambda e: e.matmul(bank(0)[0:R1, i * GT:(i + 1) * GT], w_, xT(b, lo, GT), start=True, stop=True), free[0], x1T_ok[b])
            for i, b_ in enumerate((b_ad, b_gd)):
                a = act.do(lambda e: e.activation(low[0:R1, i, :], bank(0)[0:R1, i * GT:(i + 1) * GT], ACT.Identity, bias=b_[0:R1, :]), m, *reads, mm, ones_row)
            free[0] = a
            s = sigmoid(pre, low[0:R1, :, :], a, shared["in_ok"])
            yield
            shared["ad_ok"] = dve.do(lambda e: e.tensor_tensor(low[0:R1, :, :], low[0:R1, :, :], pre, ALU.mult), s)
            yield
            for t in range(G4):
                pe.do(lambda e: e.matmul(bank(2)[:, t * 16:t * 16 + 16], xT(b, lo + t * P, P), w_be, start=True, stop=True), free[2], sig=None)
                mm = pe.do(lambda e: e.matmul(bank(2)[:, 64 + t * 16:64 + t * 16 + 16], gdT[0:R1 + 1, t * P:(t + 1) * P], w_gu16[0:R1 + 1, :], start=True, stop=True), shared["ad_ok"], ones_row)
            G16 = G4 * H1
            bg = betagate[:, g % 2]
            old = shared["gate_reads"][g % 2]
            a = dve.do(lambda e: e.tensor_tensor(bg[:, 0], bank(2)[:, 0:G16].rearrange("p (t h) -> p t h", h=H1), bc(bb, 1, G4), ALU.add), mm, *old)
            free[2] = a = dve.do(lambda e: e.tensor_copy(bg[:, 1], bank(2)[:, 64:64 + G16].rearrange("p (t h) -> p t h", h=H1)), a)
            yield
            a = sigmoid(bg, bg, a)
            yield
            shared["b_ok"][g % 2] = dve.do(lambda e: e.tensor_scalar(bg[:, 0], bg[:, 0], 1.0, None, ALU.min), a)
            shared["made"] = g + 1
            yield

    def delta(x):
        lg = take(0, G4, KH)
        E01 = take(0, 2 * KH + 32)
        E23 = take(0, 2 * KH)
        Ex = [E01[:, 0:KH], E01[:, KH:2 * KH], E23[:, 0:KH], E23[:, KH:2 * KH]]
        QK = take(0, 2, KH)
        Qr, Kr = QK[:, 0, :], QK[:, 1, :]
        Vr, Kb = take(0, KH), take(0, KH)
        sq2 = take(0, 2, KH)
        Qd, sq = sq2[:, 0, :], sq2[:, 1, :]
        DT = take(0, 4, HPH, P)
        AT, LT = take(0, HH, BLK), take(0, HH, BLK)
        stat = take(0, 6, HH)
        gE = take(0, HPH, 2)
        S = take(0, HPH, DK)
        Tm = DT[:, 0].rearrange("p a n -> p (a n)").rearrange("p (h d) -> p h d", d=DK)
        Um = h8(Qr)
        TR = E01[:, 0:1056]
        X16 = sq[:, 0:128].rearrange("p (b i c) -> p b i c", b=2, i=16)
        prod = sq[:, 128:256].rearrange("p (b i c) -> p b i c", b=2, i=16)
        Y16 = sq[:, 256:384].rearrange("p (c x h) -> p c x h", c=4, x=4)
        Cm, Pm = {32: h8(Qd), 64: h8(Ex[0])}, h8(sq)
        A, Bk = 2 * x, 2 * x + 1
        two = pair(A)
        F0 = x * KH
        L = {"pe": None, "dve": None, "act": None, "pool": None}

        def doer(name, eng):
            def do(issue, *w, sig="done"):
                tok = eng.do(issue, *w, sig=sig)
                L[name] = tok or L[name]
                return tok
            return do

        PE, V, Sc, G = doer("pe", pe), doer("dve", dve), doer("act", act), doer("pool", pool)

        def both(tok):
            free[A] = free[Bk] = tok

        def each(k, lhs, rhs, *w):
            for h in range(HH):
                for c in range(2):
                    q = slice(64 * c, 64 * c + 64)
                    m = PE(lambda e: e.matmul(bank(k)[q, h * 64:(h + 1) * 64], lhs(h)[q], rhs(h)[q], start=True, stop=True), *w, free[k],
                           sig="inv" if h == HH - 1 and c == 1 else None)
            return m

        ps8 = lambda k: bank(k).rearrange("p (h i) -> p h i", i=BLK)
        G(lambda e: e.memset(AT, 0.0))
        zt = G(lambda e: e.memset(LT, 0.0))
        st_ok = None
        for g in range(NG):
            b = g * G4 // TT
            if g * G4 % TT == 0:
                st_ok = V(lambda e: e.memset(S, 0.0), L["pe"])
            while shared["made"] <= g:
                yield
            for t in range(G4):
                k = (A, Bk)[t % 2]
                m = shared["reads"][x] = PE(lambda e: e.matmul(bank(k), adT[0:R1 + 1, t * P:(t + 1) * P], w_au[:, F0:F0 + KH], start=True, stop=True), free[k], shared["ad_ok"], ld1)
                free[k] = a = Sc(lambda e: e.activation(lg[:, t, :], bank(k), ACT.Exp, scale=-1.0), m, L["pe"])
            a = Sc(lambda e: e.activation(lg, lg, ACT.Ln, bias=C("one")), a)
            yield
            lg_ok = V(lambda e: e.tensor_scalar(lg, lg, float(-np.log(0.1)), 0.0, ALU.min, ALU.max), a)
            for t in range(G4):
                n = g * G4 + t
                tok = slice(t * P, (t + 1) * P)
                be, ga = (betagate[:, g % 2, z, t, x * HH:(x + 1) * HH] for z in range(2))
                for c, w_, k in ((0, w_q, A), (1, w_k, Bk)):
                    m = shared["reads"][x] = PE(lambda e: e.matmul(bank(k), cs[:, c, tok], w_[:, F0:F0 + KH], start=True, stop=True), shared["in_ok"], free[k])
                a = V(lambda e: e.tensor_tensor(QK, ps[:, A:A + 2, :], b_qk[:, :, F0:F0 + KH], ALU.add), m, L["pe"], L["pool"], L["act"])
                both(a)
                yield
                a = Sc(lambda e: e.activation(sq2, QK, ACT.Square), a, L["dve"], L["pe"], L["pool"])
                m = shared["reads"][x] = PE(lambda e: e.matmul(bank(A), cs[:, 2, tok], w_v[:, F0:F0 + KH], start=True, stop=True), free[A])
                yield
                a = V(lambda e: e.tensor_reduce(stat[:, 0:2, :].rearrange("p a h -> p (a h)"), sq2.rearrange("p a (h d) -> p (a h) d", d=DK), AX, ALU.add), a)
                a = V(lambda e: e.tensor_scalar(stat[:, 4:6, :], stat[:, 0:2, :], EPS1, None, ALU.max), a)
                free[A] = V(lambda e: e.tensor_tensor(Vr, bank(A), b_v[:, F0:F0 + KH], ALU.add), m)
                yield
                n_ok = yield from rsqrt_steps(stat[:, 4:6, :].rearrange("p a h -> p (a h)"), stat[:, 0:2, :].rearrange("p a h -> p (a h)"), a, 1 + x)
                nb_ok = V(lambda e: e.tensor_tensor(stat[:, 2, :], stat[:, 1, :], be, ALU.mult), n_ok, shared["b_ok"][g % 2])
                if t == G4 - 1:
                    shared["used"][x] = g + 1
                yield
                for j, (mat, k) in enumerate((("cum_mid", Bk), ("cum_end", A), ("cum", Bk))):
                    m = PE(lambda e: e.matmul(bank(k), C(mat), lg[:, t, :], start=True, stop=True), lg_ok, free[k])
                    if j == 0:
                        Sc(lambda e: e.activation(Ex[0], bank(k), ACT.Exp), m, L["pe"], L["dve"], L["pool"])
                        x_ok = Sc(lambda e: e.activation(Ex[1], bank(k), ACT.Exp, scale=-1.0), m)
                    else:
                        x_ok = Sc(lambda e: e.activation(Ex[j + 1], bank(k), ACT.Exp), m)
                    free[k] = x_ok
                for hp in range(HPH):
                    m = PE(lambda e: e.matmul(bank(A)[:, 2 * hp:2 * hp + 2], lg[:, t, hp * P:(hp + 1) * P], C("chunk_of"), start=True, stop=True), free[A], sig="ge" if hp == HPH - 1 else None)
                free[A] = ge_ok = Sc(lambda e: e.activation(gE.rearrange("p a b -> p (a b)"), bank(A)[:, 0:2 * HPH], ACT.Exp), m, L["dve"])
                yield
                mul = lambda E, dst, u, w, *ok: E(lambda e: e.tensor_tensor(dst, u, w, ALU.mult), *ok)
                sc_ = lambda i: bc(stat[:, i, :], 2, DK)
                kb_ok = mul(G, h8(Kb), h8(Kr), sc_(2), nb_ok)
                qn_ok = mul(V, h8(Qr), h8(Qr), sc_(0), n_ok)
                qd_ok = mul(V, Qd, Qr, Ex[0], qn_ok, x_ok)
                yield
                kn_ok = mul(V, h8(Kr), h8(Kr), sc_(1), kb_ok)
                k2_ok = mul(V, Ex[0], Ex[0], Kr, qd_ok, kn_ok)
                kd_ok = mul(G, Ex[1], Ex[1], Kb, kb_ok, x_ok)
                kt_ok = mul(G, Ex[3], Ex[3], Kr, kn_ok, x_ok)
                ke_ok = mul(G, Ex[2], Ex[2], Kb)
                yield
                for j, src, ok, k in ((2, Qr, qn_ok, Bk), (0, Qd, qd_ok, A), (1, Ex[0], k2_ok, Bk), (3, Ex[1], kd_ok, A)):
                    for hp in range(HPH):
                        m = PE(lambda e: e.transpose(bank(k)[:, hp * P:(hp + 1) * P], src[:, hp * P:(hp + 1) * P], ident), ok, free[k], sig="tr" if hp == HPH - 1 else None)
                    free[k] = tr_ok = Sc(lambda e: e.copy(DT[:, j, :, :], bank(k).rearrange("p (h n) -> p h n", n=P)), m)
                zu = G(lambda e: e.memset(Um, 0.0), tr_ok, L["pe"])
                yield
                for hp in range(HPH):
                    for s2 in range(2):
                        r = slice(64 * s2, 64 * s2 + 64)
                        for c in range(2):
                            q = slice(64 * c, 64 * c + 64)
                            m = PE(lambda e: e.matmul(bank(A + s2)[q, hp * P:(hp + 1) * P], DT[r, 3, hp, q], DT[r, 0:2, hp, q], start=True, stop=True),
                                   tr_ok, free[A], free[Bk], sig="la" if hp == HPH - 1 and c == 1 else None)
                for k, dst, mask in ((1, LT, "mask_l"), (0, AT, "mask_a")):
                    for s2 in range(2):
                        a = V(lambda e: e.copy_predicated(dst.rearrange("p (h s) i -> p h s i", s=2)[:, :, s2, :], bc(C(mask).bitcast(U32), 1, HPH),
                                                          bank(A + s2).rearrange("p (h k i) -> p h k i", k=2, i=BLK)[:, :, k, :]), m, zt, L["pool"])
                        free[A + s2] = a
                la_ok = a
                cm_ok = {32: G(lambda e: e.tensor_tensor(Cm[32], LT, bc(C("lev32"), 1, HH), ALU.mult), la_ok)}
                yield
                for q in range(4):
                    r, w = slice(32 * q, 32 * q + 32), slice(32 * (q % 2), 32 * (q % 2) + 32)
                    a = V(lambda e: e.transpose(TR[r, 0:1024].rearrange("p (i n) -> p i n", n=32),
                                                bc(LT[r, :, w].rearrange("p h i -> p i h"), 2, 4)), la_ok, L["pe"])
                Lsub = TR.rearrange("p (b n) -> p b n", b=2)[:, :, 0:512].rearrange("p b (i n) -> p b i n", n=32)
                a = V(lambda e: e.tensor_copy(X16, bc(C("sub_eye").rearrange("p (i c) -> p i c", c=4), 1, 2)), a)
                for j in range(15):
                    nr = 15 - j
                    a = V(lambda e: e.tensor_tensor(prod[:, :, 0:nr, :], bc(Lsub[:, :, j + 1:16, j], 3, 4), bc(X16[:, :, j, :], 2, nr), ALU.mult), a)
                    a = V(lambda e: e.tensor_tensor(X16[:, :, j + 1:16, :], X16[:, :, j + 1:16, :], prod[:, :, 0:nr, :], ALU.subtract), a)
                    if j % 4 == 3:
                        yield
                cm_ok[64] = G(lambda e: e.tensor_tensor(Cm[64], LT, bc(C("lev64"), 1, HH), ALU.mult), a, la_ok)
                a = V(lambda e: e.transpose(Y16.rearrange("p c x h -> p c (x h)"), X16.rearrange("p b i c -> p c b i")), a)
                for s4 in range(4):
                    a = V(lambda e: e.tensor_scalar(Tm[:, :, 16 * s4:16 * s4 + 16].rearrange("p h (x c) -> p h x c", x=4), Y16.rearrange("p c x h -> p h x c"),
                                                    C("sixteen_of")[:, s4:s4 + 1], None, ALU.mult), a)
                t_ok = a
                for q in range(4):
                    r, w = slice(32 * q, 32 * q + 32), slice(32 * (q % 2), 32 * (q % 2) + 32)
                    u_ok = V(lambda e: e.transpose(Um[r, :, w], Tm[r, :, w]), t_ok, zu)
                yield
                for lev in (32, 64):
                    m = each(A, lambda h: Cm[lev][:, h, :], lambda h: Tm[:, h, :], cm_ok[lev], t_ok)
                    free[A] = p_ok = Sc(lambda e: e.copy(Pm, ps8(A)), m, L["dve"])
                    yield
                    m2 = each(Bk, lambda h: Pm[:, h, :], lambda h: Um[:, h, :], p_ok, u_ok)
                    if lev < 64:
                        m1 = each(A, lambda h: Um[:, h, :], lambda h: Pm[:, h, :])
                        free[A] = t_ok = V(lambda e: e.tensor_tensor(Tm, Tm, ps8(A), ALU.subtract), m1)
                        yield
                    free[Bk] = u_ok = V(lambda e: e.tensor_tensor(Um, Um, ps8(Bk), ALU.subtract), m2, L["pe"])
                    yield
                TKT, TV, W, O = E01[:, 0:KH], h8(Ex[1]), h8(Kb), h8(Kr)
                for h in range(HH):
                    for c in range(2):
                        q, r = slice(64 * c, 64 * c + 64), slice(64 * (h % 2), 64 * (h % 2) + 64)
                        m = PE(lambda e: e.matmul(bank(A + c)[r, (h // 2) * 64:(h // 2) * 64 + 64], h8(Ex[3])[q, h, :], Um[q, h, :], start=True, stop=True),
                               kt_ok, u_ok, free[A], free[Bk], sig="tk" if h == HH - 1 else None)
                yield
                tk_ok = Sc(lambda e: e.copy(TKT.rearrange("p (c n) -> p c n", c=2), ps[:, A:A + 2, 0:256]), m, L["dve"])
                both(tk_ok)
                m = each(A, lambda h: Um[:, h, :], lambda h: h8(Vr)[:, h, :])
                free[A] = tv_ok = Sc(lambda e: e.copy(TV, ps8(A)), m)
                m = each(Bk, lambda h: AT[:, h, :], lambda h: h8(Vr)[:, h, :])
                free[Bk] = av_ok = Sc(lambda e: e.copy(O, ps8(Bk)), m, L["pool"])
                yield
                for c in range(2):
                    q = slice(64 * c, 64 * c + 64)
                    for what, lhs in (("w", lambda r, h: TKT[r, c * 256 + (h // 2) * 64:c * 256 + (h // 2) * 64 + 64]), ("o", lambda r, h: DT[r, 2, h // 2, q])):
                        for h in range(HH):
                            r = slice(64 * (h % 2), 64 * (h % 2) + 64)
                            m = PE(lambda e: e.matmul(bank(A + h % 2)[q, (h // 2) * 64:(h // 2) * 64 + 64], lhs(r, h), S[r, h // 2, :], start=True, stop=True),
                                   tk_ok, st_ok, free[A], free[Bk], sig="ws" if h >= HH - 2 else None)
                        yield
                        v = ps[q, A:A + 2, 0:256].rearrange("p s (h e) -> p h s e", e=DK)
                        four = lambda z: z[q].rearrange("p (h s) e -> p h s e", s=2)
                        if what == "w":
                            w_ok = V(lambda e: e.tensor_tensor(four(W), four(TV), v, ALU.subtract), m, tv_ok, L["pool"])
                            both(w_ok)
                        else:
                            o_ok = V(lambda e: e.tensor_tensor(four(O), four(O), v, ALU.add), m, av_ok)
                            both(o_ok)
                        yield
                    for h in range(HH):
                        r = slice(64 * (h % 2), 64 * (h % 2) + 64)
                        m = PE(lambda e: e.matmul(bank(A)[r, (h // 2) * 64:(h // 2) * 64 + 64], h8(Ex[2])[q, h, :], W[q, h, :], start=True, stop=True),
                               ke_ok, w_ok, free[A], sig="su" if h == HH - 1 else None)
                    a = V(lambda e: e.tensor_tensor(S, S, bc(gE[:, :, c], 2, DK), ALU.mult), m, ge_ok)
                    free[A] = st_ok = V(lambda e: e.tensor_tensor(S, S, bank(A)[:, 0:256].rearrange("p (h e) -> p h e", e=DK), ALU.add), a)
                    yield
                Of = Kr
                a = Sc(lambda e: e.activation(sq, Of, ACT.Square), o_ok, L["pe"])
                yield
                a = V(lambda e: e.tensor_reduce(stat[:, 3, :], h8(sq), AX, ALU.add), a)
                a = V(lambda e: e.tensor_scalar(stat[:, 4, :], stat[:, 3, :], 1.0 / DK, EPS1, ALU.mult, ALU.add), a)
                yield
                a = yield from rsqrt_steps(stat[:, 4, :], stat[:, 3, :], a, 1 + x)
                a = shared["gate_reads"][g % 2][x] = V(lambda e: e.tensor_tensor(stat[:, 3, :], stat[:, 3, :], ga, ALU.mult), a, shared["b_ok"][g % 2])
                a = V(lambda e: e.tensor_tensor(O, O, bc(stat[:, 3, :], 2, DK), ALU.mult), a)
                yield
                for hp in range(HPH):
                    m = PE(lambda e: e.transpose(bank(A)[:, hp * P:(hp + 1) * P], Of[:, hp * P:(hp + 1) * P], ident), a, free[A], sig="ot" if hp == HPH - 1 else None)
                free[A] = ot_ok = Sc(lambda e: e.copy(Qr, bank(A)), m)
                yield
                for hp in range(HPH):
                    m = PE(lambda e: e.matmul(bank(Bk)[:, 0:D], Qr[:, hp * P:(hp + 1) * P], w_o[:, x * HPH + hp, :], start=(hp == 0), stop=(hp == HPH - 1)), ot_ok, wo_ok, free[Bk], sig="op" if hp == HPH - 1 else None)
                yield
                free[Bk] = add_out(n, 1, bank(Bk)[:, 0:D].unsqueeze(1), m)
                yield

    STEPS, AHEAD = 35, 18
    streams = [delta(0), delta(1), prelude()]
    mix, credit = mixture(), 0.0
    for _ in range(AHEAD):
        for s in (streams[2], streams[0]):
            next(s)
    while streams or mix:
        for s in list(streams):
            if next(s, "end") == "end":
                streams.remove(s)
        credit += (2 * IT + 3) * (NT // 4) / (NT * STEPS)
        while mix and (credit >= 1 or not streams):
            credit -= 1
            if next(mix, "end") == "end":
                mix = None
    sp.do(lambda e: e.drain(), outs_ok[-1], sig=None)


def layout(v):
    f = lambda a: np.ascontiguousarray(a)
    A = {}
    A["cst"], A["cst0"], _, own = constants()
    A["own"] = own
    A["x"] = f(v["L0_attn_x"].reshape(NT, P, D).transpose(1, 0, 2))
    A["wqkv0"] = f(v["L0_attn_qkv_w"].T)
    A["b0"] = f(v["L0_attn_qkv_b"].reshape(3, D).T)
    A["bv0"] = f(v["L0_attn_qkv_b"][2 * D:].reshape(1, D))
    A["pb0"] = f(v["L0_attn_proj_b"].reshape(1, D))
    A["pw0"] = f(v["L0_attn_proj_w"].T.reshape(HP, 2, D0, D).transpose(0, 2, 1, 3).reshape(64, 2, D))
    A["wr"], A["br"] = f(v["L0_ffn_Wr"]), f(v["L0_ffn_br"].reshape(1, E0))
    w1 = v["L0_ffn_W1"].reshape(E0 * P, F0)
    w2 = v["L0_ffn_W2"].reshape(E0, 4, P, D).transpose(0, 2, 1, 3).reshape(E0 * P, 4 * D)
    b1 = v["L0_ffn_b1"].reshape(E0, 4, P).transpose(0, 2, 1).reshape(E0 * P, 4)
    A["w12"] = f(np.concatenate([w1, w2, b1], 1))
    A["b2"] = f(v["L0_ffn_b2"])
    pad = lambda a: np.concatenate([a, np.zeros((IW - a.shape[0],) + a.shape[1:], a.dtype)], 0)
    gp = np.concatenate([v["L1_ffn_gate_proj"].reshape(-1, D), v["L1_ffn_shared_gate_w"]], 0)
    up = np.concatenate([v["L1_ffn_up_proj"].reshape(-1, D), v["L1_ffn_shared_up_w"]], 0)
    dn = np.concatenate([v["L1_ffn_down_proj"].transpose(0, 2, 1).reshape(-1, D), v["L1_ffn_shared_down_w"].T], 0)
    A["w_gu"] = f(np.stack([pad(gp).T, pad(up).T], 1))
    A["w_dn"] = f(pad(dn).reshape(IT, P, D).transpose(1, 0, 2))
    for c in "qkv":
        A[f"w_{c}"] = f(v[f"L1_attn_W{c}"].T)
        A[f"b_{c}"] = f(v[f"L1_attn_b{c}"].reshape(1, -1))
    A["w_au"] = f(np.concatenate([v["L1_attn_Wau"].T, v["L1_attn_bau"].reshape(1, -1)], 0))
    A["w_o"] = f(v["L1_attn_Wo"].T.reshape(HP, P, D).transpose(1, 0, 2))
    rows = lambda a: np.concatenate([a, np.zeros((P - a.shape[0],) + a.shape[1:], a.dtype)], 0)
    conv = [np.concatenate([v[f"L1_attn_w{c}_conv"][:, 0, :], v[f"L1_attn_b{c}_conv"][:, None]], 1) for c in "qkv"]
    A["small1"] = f(np.concatenate(conv + [
        v["L1_attn_rms_w"].reshape(HP, P).T, v["L1_attn_Wad"].T, v["L1_attn_Wgd"].T,
        rows(v["L1_attn_bad"][:, None]), rows(v["L1_attn_bgd"][:, None]),
        v["L1_attn_Wbeta"].T, v["L1_ffn_gate_w"].T, rows(np.concatenate([v["L1_attn_Wgu"].T, v["L1_attn_bgu"].reshape(1, -1)], 0))], 1))
    A["smallb"] = f(np.concatenate([v["L1_attn_bbeta"], v["L1_ffn_gate_bias"], v["L1_attn_bo"]]).reshape(1, -1))
    return A


def kernel(**inputs):
    import concourse.bacc as bacc
    from concourse.bass_utils import run_bass_kernel_spmd

    arrays = layout({k: np.asarray(a) for k, a in inputs.items()})
    nc = bacc.Bacc("TRN2", target_bir_lowering=False, num_devices=1)
    feed, ins = {}, {}
    for name, a in arrays.items():
        feed[f"in_{name}"] = a
        ins[name] = nc.dram_tensor(f"in_{name}", a.shape, mybir.dt.from_np(a.dtype), kind="ExternalInput").ap()
    ins["cw_park"] = nc.dram_tensor("cw_park", (96, NT * P), U16).ap()
    out = nc.dram_tensor("out_x", (P, NT, D), F32, kind="ExternalOutput").ap()
    program(nc, ins, out)
    r = run_bass_kernel_spmd(nc, [feed], core_ids=[0])
    y = r.results[0]["out_x"]
    return np.ascontiguousarray(np.asarray(y).reshape(P, NT, D).transpose(1, 0, 2)).reshape(B, T, D)
```

```python
from contextlib import ExitStack

import numpy as np

import concourse.bass as bass
from concourse import mybir

F32 = mybir.dt.float32
BF16 = mybir.dt.bfloat16
U16 = mybir.dt.uint16
I32 = mybir.dt.int32
U32 = mybir.dt.uint32
ALU = mybir.AluOpType
ACT = mybir.ActivationFunctionType
AX = mybir.AxisListType.X

P = 128
B, T, D = 4, 1024, 128
TT = T // P
NT = B * TT
BLK = 64
H0, D0 = 16, 8
HP = 8
F0, E0 = 512, 8
H1, DK = 16, 64
R1 = 64
E1, I1, NS1, K1 = 16, 176, 2, 4
IT = -(-(E1 + NS1) * I1 // P)
IW = IT * P
EPS_LN, EPS1 = 1e-05, 1e-06
NEG = -1e30
KW = 4


def constants():
    i = np.arange(P)
    parts = {}
    parts["ident"] = np.eye(P)
    c, r = i // BLK, i % BLK
    same = (c[:, None] == c[None, :])
    upto = same & (r[:, None] <= r[None, :])
    tomid = same & (r[:, None] < BLK // 2)
    parts["cum_mid"] = tomid - upto.astype(float)
    parts["cum_end"] = -1.0 * (same & (r[:, None] > r[None, :]))
    of = c[:, None] == np.arange(2)[None, :]
    parts["chunk_of"] = -1.0 * np.concatenate([of, of & (r[:, None] < BLK // 2)], 1)
    parts["one"] = np.ones((P, 1))
    ii = np.arange(BLK)[None, :]
    parts["mask_a"] = (r[:, None] <= ii)
    parts["mask_l"] = (r[:, None] < ii)
    for s in (32, 64):
        parts[f"lev{s}"] = (r[:, None] // s == ii // s) & (r[:, None] % s < s // 2) & (ii % s >= s // 2)
    parts["sub_eye"] = (np.arange(16)[None, :, None] == (4 * (i % 32 // 8)[:, None, None] + np.arange(4)[None, None, :])).reshape(P, 64)
    parts["sixteen_of"] = (r[:, None] // 16 % 2 == np.arange(2)[None, :])
    parts["half_of"] = (r[:, None] // 32 == np.arange(2)[None, :])
    parts["head_of"] = (i[:, None] // D0 == np.arange(H0)[None, :])
    parts["causal_q"] = np.where(r[:, None] < ii, NEG, 0.0)
    parts["causal_k"] = np.where(ii < r[:, None], NEG, 0.0)
    parts["two_eyes"] = (i[:, None] == np.arange(P)[None, :] % BLK) & (i[:, None] < BLK)
    parts["eye_hi"] = (i[:, None] + BLK == np.arange(P)[None, :])
    blk = np.arange(T) // BLK
    parts["blk_of"] = (i[:, None] == blk[None, :])
    parts["iota8"] = np.broadcast_to(np.arange(E0), (P, E0))
    parts["rowid"] = i[:, None]
    e = np.arange(E1)
    parts["before16"] = np.broadcast_to((e[None, :] < e[:, None]).reshape(1, -1), (P, 256))
    g = np.arange(4)
    parts["before4"] = np.broadcast_to((g[None, :] < g[:, None]).reshape(1, -1), (P, 16))
    only0 = ("head_of", "causal_q", "causal_k", "two_eyes", "eye_hi", "blk_of", "iota8", "rowid")
    at, cols, n = {}, ([], []), [0, 0]
    for k, v in parts.items():
        v = np.asarray(v, np.float32)
        z = int(k in only0)
        at[k] = (z, n[z], v.shape[1])
        n[z] += v.shape[1]
        cols[z].append(v)
    own = np.zeros((96, IW), np.uint16)
    for x in range(E1 + NS1):
        own[x::32, x * I1:(x + 1) * I1] = 0x3F80
    return np.concatenate(cols[0], 1), np.concatenate(cols[1], 1), at, own


class Engine:

    LENGTH = {"pe": 160, "dve": 600, "act": 480, "pool": 1100, "sp": 2000}

    def __init__(self, name, eng, semaphore, plan):
        self.name, self.eng, self.semaphore = name, eng, semaphore
        self.plan, self.time = plan, 0
        self.counts, self.waited, self.pending, self.last = {}, {}, [], None

    def do(self, issue, *waits, sig="done", inc=1, length=None):
        own = [self.last] if self.name in ("dve", "act", "pool") else []
        for w in list(waits) + self.pending + own:
            if w and self.waited.get(w[0], 0) < w[1]:
                self.waited[w[0]] = w[1]
                if self.eng is not None:
                    self.eng.wait_ge(self.semaphore(w[0]), w[1])
        start = max([self.time] + [self.plan.get(w, 0) for w in list(waits) + self.pending + own if w])
        self.time = start + (length or self.LENGTH[self.name])
        self.plan["segment"] = max(self.plan.get("segment", 0), self.time + 100)
        self.pending = []
        ins = issue(self.eng) if self.eng is not None else None
        if not sig:
            return None
        key = f"{self.name}_{sig}"
        self.counts[key] = self.counts.get(key, 0) + inc
        self.last = (key, self.counts[key])
        self.plan[self.last] = self.time + 100
        if ins is not None:
            ins.then_inc(self.semaphore(key), inc)
        else:
            self.semaphore(key)
        return self.last


def bc(ap, axis, n):
    a = ap.unsqueeze(axis)
    shape = list(a.shape)
    shape[axis] = n
    return a.broadcast_to(shape)


def program(nc, ins, out):
    with ExitStack() as ctx:
        made = {}

        def sbuf(name, shape):
            if name not in made:
                made[name] = ctx.enter_context(nc.sbuf_tensor(name, shape, F32))
            return made[name][:]

        def psum(name, shape):
            if name not in made:
                made[name] = ctx.enter_context(nc.psum_tensor(name, shape, F32))
            return made[name][:]

        def semaphore(name):
            if name not in made:
                made[name] = ctx.enter_context(nc.semaphore(name))
            return made[name]

        def write(name, eng):
            plan = {}
            engines = [Engine(n, eng if n == name else None, semaphore, plan) for n in ("pe", "dve", "act", "pool", "sp")]
            describe(engines, sbuf, psum, ins, out)

        write(None, None)
        with nc.Block() as block:
            @block.tensor
            def _(eng):
                write("pe", eng)

            @block.vector
            def _(eng):
                write("dve", eng)

            @block.scalar
            def _(eng):
                write("act", eng)

            @block.gpsimd
            def _(eng):
                write("pool", eng)

            @block.sync
            def _(eng):
                write("sp", eng)


def describe(engines, sb, psum, ins, out):
    pe, dve, act, pool, sp = engines
    ps = psum("ps", [P, 8, 512])
    bank = lambda i: ps[:, i, :]
    pair = lambda i: ps[:, i:i + 2, :].rearrange("p a n -> p (a n)")
    free = [None] * 8

    def barrier():
        for e in engines:
            e.pending = [o.last for o in engines if o is not e and o.last] + e.pending

    xres = sb("xres", [P, NT, D])
    xnT = sb("xnT", [P, B, T + KW - 1])
    cst_np, cst0_np, at, _ = constants()
    cst = sb("cst", [P, cst_np.shape[1]])
    w_gu = sb("w_gu", [P, 2, IW])
    w_dn = sb("w_dn", [P, IT, D])
    cst0 = w_gu[:, 1, 0:cst0_np.shape[1]]

    def C(k):
        z, n, m = at[k]
        return (cst, cst0)[z][:, n:n + m]
    w_q, w_k, w_v = (sb(f"w_{c}", [P, H1 * DK]) for c in "qkv")
    w_au = sb("w_au", [R1 + 1, H1 * DK])
    w_o = sb("w_o", [P, HP, D])
    b_qk = sb("b_qk", [P, 2, H1 * DK])
    b_v = sb("b_v", [P, H1 * DK])
    small = sb("small", [P, 640])
    own = sb("own", [96, 2, 256]).bitcast(BF16)
    WORK = 24600
    work = sb("work", [P, WORK])
    used = [0, 0]

    def take(pool_i, *shape):
        buf, size = ((work, WORK), (small, 640))[pool_i]
        n = int(np.prod(shape))
        v = buf[:, used[pool_i]:used[pool_i] + n]
        used[pool_i] += n
        assert used[pool_i] <= size, (pool_i, used)
        if len(shape) > 1:
            names = "abcdef"[:len(shape)]
            v = v.rearrange(f"p ({' '.join(names)}) -> p {' '.join(names)}", **dict(zip(names, shape)))
        return v

    act.do(lambda e: e.preload_act_table_set("natural_log_exp_and_others"), sig=None)

    def load(dst, src, name, eng=sp):
        return eng.do(lambda e: e.dma_start(dst, src), sig=f"ld_{name}", inc=16)

    load(cst, ins["cst"], "cst")
    ld_c = load(cst0, ins["cst0"], "cst")
    ld_x = [load(xres[:, b * TT:(b + 1) * TT, :], ins["x"][:, b * TT:(b + 1) * TT, :], f"x{b}") for b in range(B)]
    b0 = take(1, 3)
    pw = take(1, 2, D)
    wr = take(1, E0)
    brb = take(1, E0)
    bvb = take(1, D)
    pbb = take(1, D)
    wqkv0 = w_gu[:, 0, 0:3 * D]
    ld_s = None
    for dst, key in ((wqkv0, "wqkv0"), (b0, "b0"), (wr, "wr")):
        ld_s = load(dst, ins[key], "s0")
    ld_s = load(pw[0:64, :, :], ins["pw0"], "s0")
    for dst, key in ((brb, "br"), (bvb, "bv0"), (pbb, "pb0")):
        ld_s = load(dst, ins[key].partition_broadcast(P)[:, 0, :], "s0")
    ident = C("ident")

    nwt = sb("nwt", [P, 3, 2, H1])

    def rsqrt_steps(x, y, ok, z=0):
        n = x.shape[1]
        u, w = nwt[:, z, 0, 0:n], nwt[:, z, 1, 0:n]
        a = act.do(lambda e: e.activation(u, x, ACT.Ln), ok, length=100)
        a = act.do(lambda e: e.activation(y, u, ACT.Exp, scale=-0.5), a, length=100)
        yield
        a = dve.do(lambda e: e.tensor_tensor(w, y, y, ALU.mult), a, length=90)
        a = dve.do(lambda e: e.tensor_tensor(w, w, x, ALU.mult), a, length=90)
        a = dve.do(lambda e: e.tensor_scalar(w, w, -0.5, 1.5, ALU.mult, ALU.add), a, length=90)
        return dve.do(lambda e: e.tensor_tensor(y, y, w, ALU.mult), a, length=90)

    def at_once(steps):
        while True:
            try:
                next(steps)
            except StopIteration as end:
                return end.value

    def sigmoid(dst, z, *ok, scale=-1.0):
        a = act.do(lambda e: e.activation(dst, z, ACT.Exp, scale=scale), *ok)
        a = act.do(lambda e: e.activation(dst, dst, ACT.Ln, bias=C("one")[0:dst.shape[0], :]), a, ld_c)
        return act.do(lambda e: e.activation(dst, dst, ACT.Exp, scale=-1.0), a)

    st = take(1, TT, 6)
    mv = take(1, TT, 2)
    rs = take(1, TT)
    ve = take(1, TT)
    z_pad = pool.do(lambda e: e.memset(xnT[:, :, 0:KW - 1], 0.0))

    def norm(b, xn, ready, banks, xn_free):
        for t in range(TT):
            x = xres[:, b * TT + t, :]
            a = dve.do(lambda e: e.bn_stats(st[:, t, :], x), *ready)
        for t in range(TT):
            a2 = dve.do(lambda e: e.bn_aggr(mv[:, t, :], st[:, t, :]), a)
        a = dve.do(lambda e: e.tensor_scalar(ve, mv[:, :, 1], EPS_LN, None, ALU.add), a2)
        a = at_once(rsqrt_steps(ve, rs, a))
        for t in range(TT):
            x = xres[:, b * TT + t, :]
            a = dve.do(lambda e: e.tensor_scalar(xn[:, t, :], x, mv[:, t, 0:1], rs[:, t:t + 1],
                                                           ALU.subtract, ALU.mult), a, *xn_free)
        for g in range(TT // 4):
            k = banks[g % len(banks)]
            for q in range(4):
                t = 4 * g + q
                m = pe.do(lambda e: e.transpose(bank(k)[:, q * P:(q + 1) * P], xn[:, t, :], ident),
                          a, ld_c, free[k], sig="nT" if q == 3 else None)
            free[k] = act.do(lambda e: e.copy(xnT[:, b, KW - 1 + g * 512:KW - 1 + (g + 1) * 512],
                                                            bank(k)), m, sig="xnT")
        return free[k]

    xn = take(0, TT, D)
    xnT_ok = []
    xn_free = ()
    for b in range(B):
        tok = norm(b, xn, (ld_x[b],), (0, 1), xn_free)
        xn_free = (pe.last,)
        xnT_ok.append(tok)
    used[0] = 0
    KT = take(0, B, T)
    Vbd = take(0, TT, HP, 2, 18)
    Qbd = take(0, H0, BLK)
    pT = take(0, TT, H0 * BLK)
    Oall = take(0, B, HP, 16, 9)
    w12 = KT.rearrange("p b t -> p (b t)")[:, 0:2 * 1028].rearrange("p (s n) -> p s n", s=2)
    small_q = take(0, BLK)
    mx = take(0, 2, HP, 16)
    em = take(0, B, HP, 16)
    barrier()
    xT = lambda b, lo, n: xnT[:, b, KW - 1 + lo:KW - 1 + lo + n]

    for b in range(B):
        for g in range(2):
            k = (2 * b + g) % 4
            m = pe.do(lambda e: e.matmul(bank(k), wqkv0[:, D:2 * D], xT(b, g * 512, 512), start=True, stop=True),
                      free[k], ld_s, xnT_ok[b])
            kT_ok = free[k] = act.do(lambda e: e.activation(KT[:, b, g * 512:(g + 1) * 512], bank(k), ACT.Identity,
                                                                           bias=b0[:, 1:2]), m, ld_s)
    nmT = take(0, H0 * BLK)[0:16, :]
    Vs = take(0, TT, D)
    z1 = pool.do(lambda e: e.memset(Vbd, 0.0))
    V5 = Vbd.rearrange("p t h k (s x) -> p t h k s x", s=2)
    for kb in range(2):
        ones_ok = pool.do(lambda e: e.memset(V5[kb * 64:(kb + 1) * 64, :, :, kb, :, 8:9].rearrange("p t h s x -> p (t h) s x"), 1.0), z1)
    attn_tail = None
    for b in range(B):
        m = pe.do(lambda e: e.matmul(bank(0)[:, 0:BLK], wqkv0[:, 0:D], xT(b, T - BLK, BLK), start=True, stop=True), free[0], kT_ok)
        a = act.do(lambda e: e.activation(small_q, bank(0)[:, 0:BLK], ACT.Identity, bias=b0[:, 0:1]), m, dve.last)
        free[0] = a
        q_ok = dve.do(lambda e: e.tensor_tensor(Qbd, bc(small_q, 1, H0), bc(C("head_of"), 2, BLK), ALU.mult), a, pe.last)
        for g in range(2):
            for q in range(4):
                t = 4 * g + q
                m = pe.do(lambda e: e.matmul(bank(1 + g)[:, q * D:(q + 1) * D], xT(b, t * P, P), wqkv0[:, 2 * D:3 * D],
                                                                 start=True, stop=True), free[1 + g], sig="v0" if q == 3 else None)
            a = dve.do(lambda e: e.tensor_tensor(Vs[:, 4 * g:4 * g + 4, :], bank(1 + g).rearrange("p (q d) -> p q d", d=D),
                                                      bc(bvb, 1, 4), ALU.add), m, pe.last, pool.last)
            free[1 + g] = a
        for kb in range(2):
            rows = slice(kb * 64, (kb + 1) * 64)
            for s in range(2):
                v_ok = pool.do(lambda e: e.tensor_copy(
                    V5[rows, :, :, kb, s, 0:8], Vs[rows, :, :].rearrange("p t (h s x) -> p t h s x", s=2, x=8)[:, :, :, s, :]), a, ones_ok, pe.last)
        for hp in range(HP):
            for g in range(2):
                k = 4 + (2 * hp + g) % 4
                m = pe.do(lambda e: e.matmul(bank(k), Qbd[:, 2 * hp:2 * hp + 2, :], KT[:, b, g * 512:(g + 1) * 512],
                                                                   start=True, stop=True), free[k], q_ok)
                if g == 1:
                    m = pe.do(lambda e: e.matmul(bank(k)[:, 448:512], C("two_eyes")[0:64, :], C("causal_q")[0:64, :],
                                                      start=False, stop=True, skip_group_check=True))
                a = dve.do(lambda e: e.tensor_reduce(mx[:, 0, hp, 8 * g:8 * g + 8], bank(k).rearrange("p (j n) -> p j n", n=BLK), AX, ALU.max), m)
                free[k] = a
        src = 0
        for s in (1, 2, 4, 8):
            x, y = mx[:, src], mx[:, 1 - src]
            a1 = dve.do(lambda e: e.tensor_tensor(y[:, :, s:16], x[:, :, s:16], x[:, :, 0:16 - s], ALU.max), a, pe.last)
            a = dve.do(lambda e: e.tensor_copy(y[:, :, 0:s], x[:, :, 0:s]), a1)
            src = 1 - src
        mrun, tmp = mx[:, src], mx[:, 1 - src]
        a1 = dve.do(lambda e: e.tensor_tensor(tmp[:, :, 1:16], mrun[:, :, 0:15], mrun[:, :, 1:16], ALU.subtract), a)
        act.do(lambda e: e.activation(em[:, b, :, 1:16], tmp[:, :, 1:16], ACT.Exp, scale=D0 ** -0.5), a1)
        for hp in range(HP):
            k = hp // 4
            m = pe.do(lambda e: e.transpose(bank(k)[0:16, (hp % 4) * P:(hp % 4 + 1) * P], mrun[:, hp, :], ident), a, free[k], sig="mT" if hp % 4 == 3 else None)
        nm_ok = act.do(lambda e: e.mul(nmT, pair(0)[0:16, :], -1.0), m)
        free[0] = free[1] = nm_ok
        for kt in range(TT):
            k = 4 + 2 * (kt % 2)
            for g in range(2):
                kk = k + g
                pe.do(lambda e: e.matmul(bank(kk), KT[:, b, kt * P:(kt + 1) * P], Qbd[:, 8 * g:8 * g + 8, :], start=True, stop=False), free[kk], sig=None)
                m = pe.do(lambda e: e.matmul(bank(kk), C("blk_of")[0:16, kt * P:(kt + 1) * P], nmT[:, g * 512:(g + 1) * 512], start=False, stop=(kt < TT - 1)), nm_ok)
                if kt == TT - 1:
                    m = pe.do(lambda e: e.matmul(bank(kk), C("eye_hi")[0:64, :], bc(C("causal_k")[0:64, :], 1, 8), start=False, stop=True))
            e_ok = act.do(lambda e: e.activation(pT[:, kt, :], pair(k), ACT.Exp, scale=D0 ** -0.5), m)
            free[k] = free[k + 1] = e_ok
        for hp in range(HP):
            k = hp % 4
            for kt in range(TT):
                m = pe.do(lambda e: e.matmul(bank(k)[:, kt * 36:(kt + 1) * 36], pT[:, kt, hp * P:(hp + 1) * P], Vbd[:, kt, hp, :, :].rearrange("p k x -> p (k x)"),
                                                                start=True, stop=True), free[k], e_ok, v_ok, sig="pv" if kt == TT - 1 else None)
            for s in range(2):
                rows = slice(64 * s, 64 * s + 64)
                free[k] = o_ok = dve.do(lambda e: e.tensor_copy(
                    Oall[rows, b, hp, :, :], bank(k)[rows, 0:288].rearrange("p (j s x) -> p j s x", s=2, x=9)[:, :, s, :]), m)
    flat = pT.rearrange("p t n -> p (t n)")
    lsum, rr = (flat[:, o:o + 512].rearrange("p (b h j) -> p b h j", b=B, h=HP) for o in (2048, 2560))
    acc, df = (flat[:, o:o + 256].rearrange("p (b h x) -> p b h x", b=B, h=HP) for o in (3072, 3328))
    a = dve.do(lambda e: e.tensor_copy(lsum[:, :, :, 0], Oall[:, :, :, 0, 8]), o_ok, act.last, pe.last)
    for j in range(1, 16):
        a = dve.do(lambda e: e.tensor_tensor(lsum[:, :, :, j], lsum[:, :, :, j - 1], em[:, :, :, j], ALU.mult), a)
        a = dve.do(lambda e: e.tensor_tensor(lsum[:, :, :, j], lsum[:, :, :, j], Oall[:, :, :, j, 8], ALU.add), a)
    a = dve.do(lambda e: e.reciprocal(rr, lsum), a)
    rl = flat[:, 3584:3616].rearrange("p (b h) -> p b h", b=B)
    a2 = dve.do(lambda e: e.tensor_copy(rl, rr[:, :, :, 15]), a)
    a = dve.do(lambda e: e.tensor_tensor(rr[:, :, :, 1:16], lsum[:, :, :, 0:15], rr[:, :, :, 1:16], ALU.mult), a2)
    a = dve.do(lambda e: e.memset(acc, 0.0), a)
    for j in range(1, 16):
        a = dve.do(lambda e: e.tensor_tensor(df, Oall[:, :, :, j, 0:8], acc, ALU.subtract), a)
        a = dve.do(lambda e: e.tensor_tensor(df, df, bc(rr[:, :, :, j], 3, D0), ALU.mult), a)
        a = dve.do(lambda e: e.tensor_tensor(acc, acc, df, ALU.add), a)
    fin_ok = dve.do(lambda e: e.tensor_tensor(acc, acc, bc(rl, 3, D0), ALU.mult), a)
    for b in range(B):
        xb_ok = dve.do(lambda e: e.tensor_tensor(xres[:, b * TT:(b + 1) * TT, :], xres[:, b * TT:(b + 1) * TT, :], bc(pbb, 1, TT), ALU.add), ld_s, fin_ok)
    oT = Vs
    for b in range(B):
        m = pe.do(lambda e: e.transpose(bank(0)[0:64, 0:P], acc[:, b, :, :].rearrange("p h x -> p (h x)"), ident), fin_ok, free[0])
        a = act.do(lambda e: e.copy(oT[0:64, b, :], bank(0)[0:64, 0:P]), m)
        free[0] = a
        for s in range(2):
            m = pe.do(lambda e: e.matmul(bank(1)[64:128, 0:D], oT[0:64, b, 64 * s:64 * s + 64], pw[0:64, s, :], start=(s == 0), stop=(s == 1)), a, free[1])
        row = xres[64:128, b * TT + TT - 1, :]
        free[1] = dve.do(lambda e: e.tensor_tensor(row, row, bank(1)[64:128, 0:D], ALU.add), m, xb_ok)

    meanT = take(0, B)
    mrep = take(0, P)
    sc = take(0, B, E0)
    eq = take(0, B, E0)
    top = take(0, B)
    idxf = take(0, 2, B)
    idx = take(0, 2, B).bitcast(U32)
    b2r = take(0, B, D)
    hT = pT[:, 0:2, :].rearrange("p a (f n) -> p (a f) n", n=512)
    barrier()
    for b in range(B):
        a = dve.do(lambda e: e.tensor_reduce(meanT[:, b:b + 1], xT(b, 0, T), AX, ALU.add))
    a = dve.do(lambda e: e.tensor_scalar(meanT, meanT, 1.0 / T, None, ALU.mult), a)
    for b in range(B):
        a1 = dve.do(lambda e: e.tensor_copy(mrep, meanT[:, b:b + 1].broadcast_to([P, P])), a, pe.last)
        m = pe.do(lambda e: e.matmul(bank(0)[:, 8 * b:8 * b + 8], mrep, wr, start=True, stop=True), a1, free[0])
    a = dve.do(lambda e: e.tensor_tensor(sc, bank(0)[:, 0:32].rearrange("p (b e) -> p b e", e=E0), bc(brb, 1, B), ALU.add), m)
    free[0] = a
    a = dve.do(lambda e: e.tensor_reduce(top, sc, AX, ALU.max), a)
    a = dve.do(lambda e: e.tensor_tensor(eq, sc, bc(top, 2, E0), ALU.is_equal), a)
    a = dve.do(lambda e: e.tensor_scalar(eq, eq, -100.0, 100.0, ALU.mult, ALU.add), a)
    a = dve.do(lambda e: e.tensor_tensor(eq, eq, bc(C("iota8"), 1, B), ALU.add), a)
    a = dve.do(lambda e: e.tensor_reduce(idxf[:, 1, :], eq, AX, ALU.min), a)
    a = dve.do(lambda e: e.tensor_scalar(idxf[:, 0, :], idxf[:, 1, :], float(P), C("rowid"), ALU.mult, ALU.add), a)
    idx_ok = dve.do(lambda e: e.tensor_copy(idx, idxf), a)
    for b in range(B):
        b2_ok = pool.do(lambda e: e.indirect_dma_start(b2r[:, b, :], None, ins["b2"], bass.IndirectOffsetOnAxis(ap=idx[:, 1, b:b + 1], axis=0)),
                        idx_ok, sig="b2", inc=16)
    w_free = [None, None]
    x2_ok = []
    for b in range(B):
        w = w12[:, b % 2, :]
        w_ok = pool.do(lambda e: e.indirect_dma_start(w, None, ins["w12"], bass.IndirectOffsetOnAxis(ap=idx[:, 0, b:b + 1], axis=0)),
                       w_free[b % 2], sig=f"w12{b % 2}", inc=16)
        for g in range(2):
            for f in range(4):
                k = f
                m = pe.do(lambda e: e.matmul(bank(k), w[:, f * P:(f + 1) * P], xT(b, g * 512, 512), start=True, stop=True), w_ok, free[k])
                h_ok = free[k] = act.do(lambda e: e.activation(hT[:, f, :], bank(k), ACT.Relu, bias=w[:, 1024 + f:1025 + f]), m, pe.last)
            k = 4 + g
            for t in range(4):
                for f in range(4):
                    m = pe.do(lambda e: e.matmul(bank(k)[:, t * D:(t + 1) * D], hT[:, f, t * P:(t + 1) * P], w[:, 512 + f * D:512 + (f + 1) * D],
                                                                     start=(f == 0), stop=(f == 3)), h_ok, free[k], sig="y0" if f == 3 else None)
            xs = xres[:, b * TT + 4 * g:b * TT + 4 * g + 4, :]
            a = dve.do(lambda e: e.tensor_tensor(xs, xs, bank(k).rearrange("p (t d) -> p t d", d=D), ALU.add), m)
            free[k] = a
            a = dve.do(lambda e: e.tensor_tensor(xs, xs, bc(b2r[:, b, :], 1, 4), ALU.add), a, b2_ok)
        w_free[b % 2] = pe.last
        x2_ok.append(a)

    barrier()
    used[0] = 0
    used[1] = 0
    st = take(1, TT, 6)
    mv = take(1, TT, 2)
    rs = take(1, TT)
    ve = take(1, TT)
    xn = take(0, TT, D)
    ld1 = None
    for dst, key in ((w_gu, "w_gu"), (w_dn, "w_dn"), (w_q, "w_q"), (w_k, "w_k"), (w_v, "w_v"), (w_au, "w_au"), (w_o, "w_o")):
        ld1 = load(dst, ins[key], "l1")
    for dst, key in ((b_qk[:, 0, :], "b_q"), (b_qk[:, 1, :], "b_k"), (b_v, "b_v")):
        ld1 = load(dst, ins[key].partition_broadcast(P)[:, 0, :], "l1")
    smalls = take(1, ins["small1"].shape[1])
    ld1 = load(smalls, ins["small1"], "l1")
    so = [0]

    def sm(n):
        v = smalls[:, so[0]:so[0] + n]
        so[0] += n
        return v
    convw = sm(15).rearrange("p (c k) -> p c k", k=5)
    rmsw = sm(HP)
    w_ad, w_gd = sm(R1), sm(R1)
    b_ad, b_gd = sm(1), sm(1)
    w_be, w_gate, w_gu16 = sm(H1), sm(E1), sm(H1)
    small_b = take(1, 2 * 16 + D)
    bb, gb = small_b[:, 0:16], small_b[:, 16:32]
    bo_b = small_b[:, 32:32 + D]
    ld1 = load(small_b, ins["smallb"].partition_broadcast(P)[:, 0, :], "l1")
    xn_free = ()
    x1T_ok = []
    for b in range(B):
        x1T_ok.append(norm(b, xn, (), (0, 1), xn_free))
        xn_free = (pe.last,)
    a = None
    for hp in range(HP):
        a = wo_ok = dve.do(lambda e: e.tensor_scalar(w_o[:, hp, :], w_o[:, hp, :], rmsw[:, hp:hp + 1], None, ALU.mult), ld1)
    for b in range(B):
        a = dve.do(lambda e: e.tensor_tensor(xres[:, b * TT:(b + 1) * TT, :], xres[:, b * TT:(b + 1) * TT, :], bc(bo_b, 1, TT), ALU.add), ld1)

    used[0] = 0
    barrier()
    NTE = (NT, E1)
    scores = take(0, *NTE)
    sfc = take(0, *NTE)
    ra = take(0, *NTE)
    rb = take(0, *NTE)
    gs = take(0, NT, 4)
    g2 = take(0, NT, 4)
    gm = take(0, NT, 4)
    cmp16 = take(0, NT, E1, E1)
    cmb = take(0, *NTE)
    cwT = take(0, NT * P)[0:32, :]
    for n in range(NT):
        m = pe.do(lambda e: e.matmul(bank(0)[:, n * 16:(n + 1) * 16], xT(n // TT, (n % TT) * P, P), w_gate, start=True, stop=True), x1T_ok[n // TT], ld1, free[0],
                  sig="lg" if n == NT - 1 else None)
    fl = lambda v: v.rearrange("p n e -> p (n e)")
    free[0] = a = act.do(lambda e: e.activation(fl(scores), bank(0), ACT.Exp, scale=-1.0), m)
    a = dve.do(lambda e: e.tensor_scalar(scores, scores, 1.0, None, ALU.add), a)
    a = dve.do(lambda e: e.reciprocal(scores, scores), a)
    a = dve.do(lambda e: e.tensor_tensor(sfc, scores, bc(gb, 1, NT), ALU.add), a, ld1)
    grp = sfc.rearrange("p n (g k) -> p n g k", k=4)
    first = True
    for i in range(4):
        for j in range(i + 1, 4):
            dst = gs if first else g2
            a = dve.do(lambda e: e.tensor_tensor(dst, grp[:, :, :, i], grp[:, :, :, j], ALU.add), a)
            if not first:
                a = dve.do(lambda e: e.tensor_tensor(gs, gs, g2, ALU.max), a)
            first = False

    def rank_below(dst, val, before, n, keep, a):
        c4 = cmp16.rearrange("p t a b -> p t (a b)")[:, :, 0:n * n].rearrange("p t (a b) -> p t a b", b=n)
        eqm = before.rearrange("p (a b) -> p a b", b=n)
        mine, other = bc(val, 3, n), bc(val, 2, n)
        a = dve.do(lambda e: e.tensor_tensor(c4, other, mine, ALU.is_equal), a)
        a = dve.do(lambda e: e.tensor_tensor(c4, c4, bc(eqm, 1, NT), ALU.mult), a)
        a = dve.do(lambda e: e.tensor_reduce(rank_a[:, :, 0:n], c4, AX, ALU.add), a)
        a = dve.do(lambda e: e.tensor_tensor(c4, other, mine, ALU.is_gt), a)
        a = dve.do(lambda e: e.tensor_reduce(dst, c4, AX, ALU.add), a)
        a = dve.do(lambda e: e.tensor_tensor(dst, dst, rank_a[:, :, 0:n], ALU.add), a)
        return dve.do(lambda e: e.tensor_scalar(dst, dst, keep - 0.5, None, ALU.is_lt), a)

    rank_a = take(0, NT, E1)
    a = rank_below(gm, gs, C("before4"), 4, 2, a)
    ra4 = ra.rearrange("p n (g k) -> p n g k", k=4)
    a = dve.do(lambda e: e.tensor_tensor(ra4, grp, bc(gm, 3, 4), ALU.mult), a)
    a = rank_below(rb, ra, C("before16"), 16, K1, a)
    a = dve.do(lambda e: e.tensor_tensor(cmb, scores, rb, ALU.mult), a)
    a = dve.do(lambda e: e.tensor_reduce(gs[:, :, 0], cmb, AX, ALU.add), a)
    a = dve.do(lambda e: e.tensor_scalar(gs[:, :, 0], gs[:, :, 0], 1e-20, None, ALU.add), a)
    a = dve.do(lambda e: e.reciprocal(gs[:, :, 1], gs[:, :, 0]), a)
    cmb_ok = dve.do(lambda e: e.tensor_tensor(cmb, cmb, bc(gs[:, :, 1], 2, E1), ALU.mult), a)
    ones_ok = pool.do(lambda e: e.memset(cwT, 1.0))
    for g in range(NT // 4):
        k = g % 2
        for q in range(4):
            m = pe.do(lambda e: e.transpose(bank(k)[0:16, q * P:(q + 1) * P], cmb[:, 4 * g + q, :], ident), cmb_ok, free[k], sig="cwT" if q == 3 else None)
        cw_ok = free[k] = act.do(lambda e: e.copy(cwT[0:16, g * 512:(g + 1) * 512], bank(k)[0:16, :]), m, ones_ok)
    cw3 = take(0, NT * P // 2).bitcast(BF16)
    for i in range(3):
        a = act.do(lambda e: e.copy(cw3[32 * i:32 * i + 32, :], cwT), cw_ok)
        if i < 2:
            part = cw3[0:32, :] if i == 0 else cw3[96:128, :]
            if i == 1:
                a = act.do(lambda e: e.copy(part, cwT), a)
            cw_ok = dve.do(lambda e: e.tensor_tensor(cwT, cwT, part, ALU.subtract), a)
    cw_ok = a
    cw_st = sp.do(lambda e: e.dma_start(ins["cw_park"], cw3[0:96, :].bitcast(U16)), cw_ok, sig="cwst", inc=16)
    sp.do(lambda e: e.dma_start(own[:, 0, :].bitcast(U16), ins["cw_park"][:, 0:512]), cw_st, sig="cwld", inc=16)

    barrier()
    used[0] = 0
    touched, shares = {}, {}
    outs_ok = []

    def add_out(n0, cnt, src, wait):
        xs = xres[:, n0:n0 + cnt, :]
        a = dve.do(lambda e: e.tensor_tensor(xs, xs, src, ALU.add), wait, *[touched.get(n) for n in range(n0, n0 + cnt)])
        for n in range(n0, n0 + cnt):
            shares[n] = shares.get(n, 0) + 1
            if shares[n] == 3:
                outs_ok.append(sp.do(lambda e: e.dma_start(out[:, n, :], xres[:, n, :]), a, sig="out", inc=16))
            touched[n] = a
        return a

    s_g, t_u, acts, yT = take(0, 512), take(0, 512), take(0, 2, 512), take(0, 512)
    own_w = take(0, P).bitcast(BF16).rearrange("p (s n) -> p s n", s=2)

    def mixture():
        GA, UB, CWB, YB = 4, 5, 6, 7
        own_free = [None, None]
        ow_free = [None, None]
        act_free = [None, None]
        own_ld = {0: ("sp_cwld", 16)}
        s_free = yT_free = None
        for g in range(NT // 4):
            b, lo = g // 2, (g % 2) * 512
            if g + 1 < NT // 4:
                own_ld[g + 1] = sp.do(lambda e: e.dma_start(own[:, (g + 1) % 2, :].bitcast(U16), ins["cw_park"][:, (g + 1) * 512:(g + 2) * 512]),
                                      own_free[(g + 1) % 2], sig=f"cw{g % 2}", inc=16)
            prev = None
            for it in range(IT + 1):
                if it < IT:
                    ld = sp.do(lambda e: e.dma_start(own_w[0:96, it % 2, :].bitcast(U16), ins["own"][:, it * P:(it + 1) * P]),
                               ow_free[it % 2], sig=f"ow{it % 2}", inc=16)
                    sg = s_g
                    m = pe.do(lambda e: e.matmul(bank(GA), w_gu[:, 0, it * P:(it + 1) * P], xT(b, lo, 512), start=True, stop=True), free[GA], ld1, x1T_ok[b], length=850)
                    a_s = sigmoid(sg, bank(GA), m, s_free)
                    mu = pe.do(lambda e: e.matmul(bank(UB), w_gu[:, 1, it * P:(it + 1) * P], xT(b, lo, 512), start=True, stop=True), free[UB], length=850)
                    mc = pe.do(lambda e: e.matmul(bank(CWB), own_w[0:96, it % 2, :], own[:, g % 2, :], start=True, stop=True), free[CWB], ld, own_ld[g], length=210)
                    ow_free[it % 2] = own_free[g % 2] = mc
                if prev is not None:
                    pit, pa = prev
                    m = pe.do(lambda e: e.matmul(bank(YB), w_dn[:, pit, :], acts[:, pit % 2, :], start=(pit == 0), stop=(pit == IT - 1)), pa, free[YB], length=850)
                    act_free[pit % 2] = m
                if it == IT:
                    break
                yield
                free[GA] = a = dve.do(lambda e: e.tensor_tensor(t_u, bank(GA), sg, ALU.mult), a_s)
                s_free = a
                free[UB] = a = dve.do(lambda e: e.tensor_tensor(t_u, bank(UB), t_u, ALU.mult), mu, a)
                ac = acts[:, it % 2, :]
                free[CWB] = a = dve.do(lambda e: e.tensor_tensor(ac, bank(CWB), t_u, ALU.mult), mc, a, act_free[it % 2])
                prev = (it, a)
                yield
            a = act.do(lambda e: e.copy(yT, bank(YB)), m, yT_free)
            free[YB] = a
            yield
            for q in range(4):
                m = pe.do(lambda e: e.transpose(bank(YB)[:, q * P:(q + 1) * P], yT[:, q * P:(q + 1) * P], ident), a, sig="yt" if q == 3 else None)
            yT_free = m
            free[YB] = add_out(4 * g, 4, bank(YB).rearrange("p (t d) -> p t d", d=D), m)
            yield

    SUBS = 4
    LAG, SLACK, GAP = 45000, 0.02, 1200
    G4 = 2
    GT = G4 * P
    NG = NT // G4
    HH = H1 // 2
    HPH = HH // 2
    KH = HH * DK
    h8 = lambda v: v.rearrange("p (h d) -> p h d", d=DK)
    h32 = lambda v: v.rearrange("p (h d) -> p h d", d=32)
    calm = [True, True]
    progress = [0, 0]
    cs = take(0, 3, GT)
    csig = take(0, 3, GT)
    ctmp = csig[:, 0, :]
    low = take(0, 2, GT)
    adT, gdT = low[:, 0, :], low[:, 1, :]
    betagate = take(0, 2, 2, G4, H1)
    shared = {"made": 0, "used": [0, 0], "in_ok": None, "b_ok": [None, None], "reads": [None, None], "gate_reads": [[None, None], [None, None]]}

    def prelude():
        ones_row = pool.do(lambda e: e.memset(low[R1:R1 + 1, :, :], 1.0))
        mm = None
        for g in range(NG):
            b, lo = g * G4 // TT, (g * G4 % TT) * P
            while min(shared["used"]) < g:
                yield
            reads = shared["reads"]
            for c in range(3):
                dst = [ctmp, cs[:, c, :]]
                a = dve.do(lambda e: e.tensor_scalar(dst[0], xnT[:, b, lo:lo + GT], convw[:, c, 0:1], convw[:, c, 4:5], ALU.mult, ALU.add), *reads, x1T_ok[b], ld1, z_pad)
                for k in range(1, KW):
                    a = dve.do(lambda e: e.scalar_tensor_tensor(dst[k % 2], xnT[:, b, lo + k:lo + k + GT], convw[:, c, k:k + 1], dst[(k + 1) % 2], ALU.mult, ALU.add), a)
                yield
            s = sigmoid(csig, cs, a)
            yield
            shared["in_ok"] = dve.do(lambda e: e.tensor_tensor(cs, cs, csig, ALU.mult), s)
            pre = csig[0:R1, 0:2, :]
            while not calm[0]:
                yield
            for i, (w_, b_) in enumerate(((w_ad, b_ad), (w_gd, b_gd))):
                m = pe.do(lambda e: e.matmul(bank(0)[0:R1, i * GT:(i + 1) * GT], w_, xT(b, lo, GT), start=True, stop=True), free[0], x1T_ok[b], length=430)
            for i, b_ in enumerate((b_ad, b_gd)):
                a = act.do(lambda e: e.activation(low[0:R1, i, :], bank(0)[0:R1, i * GT:(i + 1) * GT], ACT.Identity, bias=b_[0:R1, :]), m, *reads, mm, ones_row)
            free[0] = a
            s = sigmoid(pre, low[0:R1, :, :], a, shared["in_ok"])
            yield
            shared["ad_ok"] = dve.do(lambda e: e.tensor_tensor(low[0:R1, :, :], low[0:R1, :, :], pre, ALU.mult), s)
            yield
            while not calm[1]:
                yield
            for t in range(G4):
                pe.do(lambda e: e.matmul(bank(2)[:, t * 16:t * 16 + 16], xT(b, lo + t * P, P), w_be, start=True, stop=True), free[2], sig=None)
                mm = pe.do(lambda e: e.matmul(bank(2)[:, 64 + t * 16:64 + t * 16 + 16], gdT[0:R1 + 1, t * P:(t + 1) * P], w_gu16[0:R1 + 1, :], start=True, stop=True), shared["ad_ok"], ones_row)
            G16 = G4 * H1
            bg = betagate[:, g % 2]
            old = shared["gate_reads"][g % 2]
            a = dve.do(lambda e: e.tensor_tensor(bg[:, 0], bank(2)[:, 0:G16].rearrange("p (t h) -> p t h", h=H1), bc(bb, 1, G4), ALU.add), mm, *old)
            free[2] = a = dve.do(lambda e: e.tensor_copy(bg[:, 1], bank(2)[:, 64:64 + G16].rearrange("p (t h) -> p t h", h=H1)), a)
            yield
            a = sigmoid(bg, bg, a)
            yield
            shared["b_ok"][g % 2] = dve.do(lambda e: e.tensor_scalar(bg[:, 0], bg[:, 0], 1.0, None, ALU.min), a)
            shared["made"] = g + 1
            yield

    def delta(x):
        lg = take(0, G4, KH)
        E01 = take(0, 2 * KH + 32)
        Ex = [E01[:, 0:KH], E01[:, KH:2 * KH], take(0, KH)]
        QK = take(0, 2, KH)
        Qr, Kr = QK[:, 0, :], QK[:, 1, :]
        Vr, Kb = take(0, KH), take(0, KH)
        sq2 = take(0, 2, KH)
        Qd, sq = sq2[:, 0, :], sq2[:, 1, :]
        DT = take(0, 4, HPH, P)
        AT, LT = take(0, HH, BLK), take(0, HH, BLK)
        stat = take(0, 6, HH)
        gE = take(0, HPH, 4)
        S = take(0, HPH, DK)
        Sm = take(0, HPH, DK)
        Tm = DT[:, 0].rearrange("p a n -> p (a n)").rearrange("p (h d) -> p h d", d=DK)
        Um = h8(Qr)
        TR = E01[:, 0:2 * KH]
        Lsub = E01.rearrange("p (b n) -> p b n", b=2)[:, :, 0:512].rearrange("p b (i n) -> p b i n", n=32)
        Dc = h32(QK[:, 0, 0:KH // 2])
        Tc, Uc = h32(E01[:, KH:3 * KH // 2]), h32(E01[:, 3 * KH // 2:2 * KH])
        X16 = sq[:, 0:128].rearrange("p (b i c) -> p b i c", b=2, i=16)
        prod = sq[:, 128:256].rearrange("p (b i c) -> p b i c", b=2, i=16)
        Y16 = sq[:, 256:384].rearrange("p (c x h) -> p c x h", c=4, x=4)
        Cm, Pm = {32: h8(Qd), 64: h8(Ex[0])}, h8(sq)
        A, Bk = 2 * x, 2 * x + 1
        two = pair(A)
        F0 = x * KH
        L = {"pe": None, "dve": None, "act": None, "pool": None}

        def doer(name, eng):
            def do(issue, *w, sig="done", length=None):
                tok = eng.do(issue, *w, sig=sig, length=length)
                L[name] = tok or L[name]
                return tok
            return do

        PE, V, Sc, G = doer("pe", pe), doer("dve", dve), doer("act", act), doer("pool", pool)

        def both(tok):
            free[A] = free[Bk] = tok

        def each(k, lhs, rhs, *w):
            for h in range(HH):
                for c in range(2):
                    q = slice(64 * c, 64 * c + 64)
                    m = PE(lambda e: e.matmul(bank(k)[q, h * 64:(h + 1) * 64], lhs(h)[q], rhs(h)[q], start=True, stop=True), *w, free[k],
                           sig="inv" if h == HH - 1 and c == 1 else None)
            return m

        ps8 = lambda k: bank(k).rearrange("p (h i) -> p h i", i=BLK)
        G(lambda e: e.memset(AT, 0.0))
        zt = G(lambda e: e.memset(LT, 0.0))
        st_ok = None
        for g in range(NG):
            b = g * G4 // TT
            if g * G4 % TT == 0:
                st_ok = V(lambda e: e.memset(S, 0.0), L["pe"])
            calm[x] = True
            while shared["made"] <= g:
                yield
            calm[x] = False
            for t in range(G4):
                k = (A, Bk)[t % 2]
                m = shared["reads"][x] = PE(lambda e: e.matmul(bank(k), adT[0:R1 + 1, t * P:(t + 1) * P], w_au[:, F0:F0 + KH], start=True, stop=True), free[k], shared["ad_ok"], ld1, length=850)
                free[k] = a = Sc(lambda e: e.activation(lg[:, t, :], bank(k), ACT.Exp, scale=-1.0), m, L["pe"])
            a = Sc(lambda e: e.activation(lg, lg, ACT.Ln, bias=C("one")), a, length=920)
            yield
            lg_ok = V(lambda e: e.tensor_scalar(lg, lg, float(-np.log(0.1)), 0.0, ALU.min, ALU.max), a)
            for t in range(G4):
                n = g * G4 + t
                tok = slice(t * P, (t + 1) * P)
                be, ga = (betagate[:, g % 2, z, t, x * HH:(x + 1) * HH] for z in range(2))
                progress[x] = n
                for c, w_, k in ((0, w_q, A), (1, w_k, Bk)):
                    m = shared["reads"][x] = PE(lambda e: e.matmul(bank(k), cs[:, c, tok], w_[:, F0:F0 + KH], start=True, stop=True), shared["in_ok"], free[k], length=850)
                a = V(lambda e: e.tensor_tensor(QK, ps[:, A:A + 2, :], b_qk[:, :, F0:F0 + KH], ALU.add), m, L["pe"], L["pool"], L["act"], length=1140)
                both(a)
                yield
                a = Sc(lambda e: e.activation(sq2, QK, ACT.Square), a, L["dve"], L["pe"], L["pool"], length=920)
                m = shared["reads"][x] = PE(lambda e: e.matmul(bank(A), cs[:, 2, tok], w_v[:, F0:F0 + KH], start=True, stop=True), free[A], length=850)
                yield
                a = V(lambda e: e.tensor_reduce(stat[:, 0:2, :].rearrange("p a h -> p (a h)"), sq2.rearrange("p a (h d) -> p (a h) d", d=DK), AX, ALU.add), a, length=1140)
                a = V(lambda e: e.tensor_scalar(stat[:, 4:6, :], stat[:, 0:2, :], EPS1, None, ALU.max), a, length=90)
                free[A] = V(lambda e: e.tensor_tensor(Vr, bank(A), b_v[:, F0:F0 + KH], ALU.add), m)
                yield
                n_ok = yield from rsqrt_steps(stat[:, 4:6, :].rearrange("p a h -> p (a h)"), stat[:, 0:2, :].rearrange("p a h -> p (a h)"), a, 1 + x)
                nb_ok = V(lambda e: e.tensor_tensor(stat[:, 2, :], stat[:, 1, :], be, ALU.mult), n_ok, shared["b_ok"][g % 2], length=90)
                if t == G4 - 1:
                    shared["used"][x] = g + 1
                calm[x] = True
                yield
                calm[x] = False
                for j, (mat, k) in enumerate((("cum_mid", Bk), ("cum_end", A))):
                    m = PE(lambda e: e.matmul(bank(k), C(mat), lg[:, t, :], start=True, stop=True), lg_ok, free[k], length=850)
                    if j == 0:
                        Sc(lambda e: e.activation(Ex[0], bank(k), ACT.Exp), m, L["pe"], L["dve"], L["pool"])
                        x_ok = Sc(lambda e: e.activation(Ex[1], bank(k), ACT.Exp, scale=-1.0), m)
                    else:
                        x_ok = Sc(lambda e: e.activation(Ex[j + 1], bank(k), ACT.Exp), m)
                    free[k] = x_ok
                for hp in range(HPH):
                    m = PE(lambda e: e.matmul(bank(Bk)[:, 4 * hp:4 * hp + 4], lg[:, t, hp * P:(hp + 1) * P], C("chunk_of"), start=True, stop=True), free[Bk], sig="ge" if hp == HPH - 1 else None, length=320)
                free[Bk] = ge_ok = Sc(lambda e: e.activation(gE.rearrange("p a b -> p (a b)"), bank(Bk)[:, 0:4 * HPH], ACT.Exp), m, L["dve"])
                yield
                mul = lambda E, dst, u, w, *ok: E(lambda e: e.tensor_tensor(dst, u, w, ALU.mult), *ok)
                sc_ = lambda i: bc(stat[:, i, :], 2, DK)
                kb_ok = mul(G, h8(Kb), h8(Kr), sc_(2), nb_ok)
                qn_ok = mul(V, h8(Qr), h8(Qr), sc_(0), n_ok)
                qd_ok = mul(V, Qd, Qr, Ex[0], qn_ok, x_ok)
                yield
                kn_ok = mul(V, h8(Kr), h8(Kr), sc_(1), kb_ok)
                k2_ok = mul(V, Ex[0], Ex[0], Kr, qd_ok, kn_ok)
                kd_ok = mul(G, Ex[1], Ex[1], Kb, kb_ok, x_ok)
                ke_ok = mul(G, Ex[2], Ex[2], Kb)
                yield
                for j, src, ok, k in ((2, Qr, qn_ok, Bk), (0, Qd, qd_ok, A), (1, Ex[0], k2_ok, Bk), (3, Ex[1], kd_ok, A)):
                    for hp in range(HPH):
                        m = PE(lambda e: e.transpose(bank(k)[:, hp * P:(hp + 1) * P], src[:, hp * P:(hp + 1) * P], ident), ok, free[k], sig="tr" if hp == HPH - 1 else None)
                    free[k] = tr_ok = Sc(lambda e: e.copy(DT[:, j, :, :], bank(k).rearrange("p (h n) -> p h n", n=P)), m)
                yield
                for hp in range(HPH):
                    for s2 in range(2):
                        r = slice(64 * s2, 64 * s2 + 64)
                        for c in range(2):
                            q = slice(64 * c, 64 * c + 64)
                            m = PE(lambda e: e.matmul(bank(A + s2)[q, hp * P:(hp + 1) * P], DT[r, 3, hp, q], DT[r, 0:2, hp, q], start=True, stop=True),
                                   tr_ok, free[A], free[Bk], sig="la" if hp == HPH - 1 and c == 1 else None)
                tri = ps[:, A:A + 2, :].rearrange("p s (h k i) -> p s h k i", k=2, i=BLK)
                by_s = lambda z: z.rearrange("p (h s) i -> p s h i", s=2)
                d_ok = Sc(lambda e: e.copy(by_s(Dc), tri[:, :, :, 1, 0:32]), m)
                yield
                for k, dst, mask in ((1, LT, "mask_l"), (0, AT, "mask_a")):
                    for s2 in range(2):
                        la_ok = V(lambda e: e.copy_predicated(by_s(dst)[:, s2], bc(C(mask).bitcast(U32), 1, HPH), tri[:, s2, :, k, :]), d_ok, zt, L["pool"], length=330)
                for s2 in range(2):
                    a = V(lambda e: e.copy_predicated(by_s(Dc)[:, s2], bc(C("half_of")[:, 1:2].broadcast_to([P, 32]).bitcast(U32), 1, HPH), tri[:, s2, :, 1, 32:64]), d_ok)
                both(a)
                a = V(lambda e: e.transpose(TR.rearrange("p (i n) -> p i n", n=32), bc(Dc.rearrange("p h i -> p i h"), 2, 4)), a, length=1200)
                calm[x] = True
                yield
                s_ok = G(lambda e: e.tensor_copy(X16, bc(C("sub_eye").rearrange("p (i c) -> p i c", c=4), 1, 2)), L["pe"], L["dve"], length=200)
                cm_ok = {32: G(lambda e: e.tensor_tensor(Cm[32], LT, bc(C("lev32"), 1, HH), ALU.mult), la_ok)}
                for j in range(15):
                    nr = 15 - j
                    s_ok = G(lambda e: e.tensor_tensor(prod[:, :, 0:nr, :], bc(Lsub[:, :, j + 1:16, j], 3, 4), bc(X16[:, :, j, :], 2, nr), ALU.mult), a, s_ok, length=220)
                    s_ok = G(lambda e: e.tensor_tensor(X16[:, :, j + 1:16, :], X16[:, :, j + 1:16, :], prod[:, :, 0:nr, :], ALU.subtract), s_ok, length=220)
                    if j % SUBS == SUBS - 1:
                        yield
                cm_ok[64] = G(lambda e: e.tensor_tensor(Cm[64], LT, bc(C("lev64"), 1, HH), ALU.mult))
                yield
                calm[x] = False
                a = V(lambda e: e.transpose(Y16.rearrange("p c x h -> p c (x h)"), X16.rearrange("p b i c -> p c b i")), s_ok)
                for z in range(2):
                    a = V(lambda e: e.tensor_scalar(Tc[:, :, 16 * z:16 * z + 16].rearrange("p h (x c) -> p h x c", x=4), Y16.rearrange("p c x h -> p h x c"),
                                                    C("sixteen_of")[:, z:z + 1], None, ALU.mult), a)
                u_ok = V(lambda e: e.transpose(Uc, Tc), a)
                yield
                for z in range(2):
                    t_ok = Sc(lambda e: e.activation(Tm[:, :, 32 * z:32 * z + 32], Tc, ACT.Copy, scale=C("half_of")[:, z:z + 1]), a)
                for z in range(2):
                    u_ok = Sc(lambda e: e.activation(Um[:, :, 32 * z:32 * z + 32], Uc, ACT.Copy, scale=C("half_of")[:, z:z + 1]), u_ok)
                yield
                for lev in (32, 64):
                    m = each(A, lambda h: Cm[lev][:, h, :], lambda h: Tm[:, h, :], cm_ok[lev], t_ok)
                    free[A] = p_ok = Sc(lambda e: e.copy(Pm, ps8(A)), m, L["dve"])
                    yield
                    m2 = each(Bk, lambda h: Pm[:, h, :], lambda h: Um[:, h, :], p_ok, u_ok)
                    if lev < 64:
                        m1 = each(A, lambda h: Um[:, h, :], lambda h: Pm[:, h, :])
                        free[A] = t_ok = V(lambda e: e.tensor_tensor(Tm, Tm, ps8(A), ALU.subtract), m1)
                        yield
                    free[Bk] = u_ok = V(lambda e: e.tensor_tensor(Um, Um, ps8(Bk), ALU.subtract), m2, L["pe"])
                    yield
                W, O = h8(Kb), h8(Kr)
                m = each(Bk, lambda h: AT[:, h, :], lambda h: h8(Vr)[:, h, :])
                sm_ok = V(lambda e: e.tensor_tensor(Sm, S, bc(gE[:, :, 2], 2, DK), ALU.mult), st_ok, ge_ok, L["pe"], length=330)
                free[Bk] = av_ok = Sc(lambda e: e.copy(O, ps8(Bk)), m, L["pool"])
                yield
                four = lambda z: z[q].rearrange("p (h s) e -> p h s e", s=2)
                for c in range(2):
                    q = slice(64 * c, 64 * c + 64)
                    for at_, lhs, St in ((0, 1, Sm), (256, 2, S)):
                        for h in range(HH):
                            r = slice(64 * (h % 2), 64 * (h % 2) + 64)
                            m = PE(lambda e: e.matmul(bank(A + h % 2)[q, at_ + (h // 2) * 64:at_ + (h // 2) * 64 + 64], DT[r, lhs, h // 2, q], St[r, h // 2, :], start=True, stop=True),
                                   sm_ok, st_ok, free[A], free[Bk], sig="ws" if h >= HH - 2 else None)
                    yield
                    v = lambda at_: ps[q, A:A + 2, at_:at_ + 256].rearrange("p s (h e) -> p h s e", e=DK)
                    r_ok = V(lambda e: e.tensor_tensor(four(h8(Vr)), four(h8(Vr)), v(0), ALU.subtract), m)
                    o_ok = V(lambda e: e.tensor_tensor(four(O), four(O), v(256), ALU.add), m, av_ok)
                    both(o_ok)
                    yield
                    for h in range(HH):
                        m = PE(lambda e: e.matmul(bank(A)[q, h * 64:(h + 1) * 64], Um[q, h, :], h8(Vr)[q, h, :], start=True, stop=True), r_ok, u_ok, free[A], sig="tr" if h == HH - 1 else None)
                    g_ok = V(lambda e: e.tensor_tensor(S, S, bc(gE[:, :, c], 2, DK), ALU.mult), o_ok, length=330)
                    yield
                    free[A] = w_ok = Sc(lambda e: e.copy(W[q].rearrange("p h e -> p (h e)"), bank(A)[q]), m, L["pool"])
                    yield
                    for h in range(HH):
                        r = slice(64 * (h % 2), 64 * (h % 2) + 64)
                        m = PE(lambda e: e.matmul(bank(Bk)[r, (h // 2) * 64:(h // 2) * 64 + 64], h8(Ex[2])[q, h, :], W[q, h, :], start=True, stop=True),
                               ke_ok, w_ok, free[Bk], sig="su" if h == HH - 1 else None)
                    yield
                    free[Bk] = st_ok = V(lambda e: e.tensor_tensor(S, S, bank(Bk)[:, 0:256].rearrange("p (h e) -> p h e", e=DK), ALU.add), m, g_ok, length=330)
                    if c == 0:
                        sm_ok = V(lambda e: e.tensor_tensor(Sm, S, bc(gE[:, :, 3], 2, DK), ALU.mult), st_ok, length=330)
                    yield
                Of = Kr
                a = Sc(lambda e: e.activation(sq, Of, ACT.Square), o_ok, L["pe"])
                yield
                a = V(lambda e: e.tensor_reduce(stat[:, 3, :], h8(sq), AX, ALU.add), a)
                a = V(lambda e: e.tensor_scalar(stat[:, 4, :], stat[:, 3, :], 1.0 / DK, EPS1, ALU.mult, ALU.add), a, length=90)
                yield
                a = yield from rsqrt_steps(stat[:, 4, :], stat[:, 3, :], a, 1 + x)
                a = shared["gate_reads"][g % 2][x] = V(lambda e: e.tensor_tensor(stat[:, 3, :], stat[:, 3, :], ga, ALU.mult), a, shared["b_ok"][g % 2])
                a = V(lambda e: e.tensor_tensor(O, O, bc(stat[:, 3, :], 2, DK), ALU.mult), a)
                yield
                for hp in range(HPH):
                    m = PE(lambda e: e.transpose(bank(A)[:, hp * P:(hp + 1) * P], Of[:, hp * P:(hp + 1) * P], ident), a, free[A], sig="ot" if hp == HPH - 1 else None)
                free[A] = ot_ok = Sc(lambda e: e.copy(Qr, bank(A)), m)
                yield
                for hp in range(HPH):
                    m = PE(lambda e: e.matmul(bank(Bk)[:, 0:D], Qr[:, hp * P:(hp + 1) * P], w_o[:, x * HPH + hp, :], start=(hp == 0), stop=(hp == HPH - 1)), ot_ok, wo_ok, free[Bk], sig="op" if hp == HPH - 1 else None)
                yield
                free[Bk] = add_out(n, 1, bank(Bk)[:, 0:D].unsqueeze(1), m)
                yield

    plan = pe.plan
    streams = {"delta0": delta(0), "delta1": delta(1), "prelude": prelude(), "mixture": mixture()}
    now = pe.time
    ready = {"delta0": now, "delta1": now + LAG, "prelude": now, "mixture": now}
    steps, total = 0, (2 * IT + 3) * (NT // 4)
    while streams:
        others = [n for n in streams if n != "mixture"]
        name = min(others, key=lambda n: ready[n]) if others else "mixture"
        if others and "mixture" in streams:
            ahead = steps / total - (progress[0] + progress[1]) / (2 * NT)
            if ahead < -SLACK or (ahead < SLACK and ready["mixture"] <= max(ready[name], pe.time) and ready[name] > pe.time + GAP):
                name = "mixture"
        plan["segment"] = 0
        if next(streams[name], "end") == "end":
            del streams[name]
        elif plan["segment"]:
            ready[name] = plan["segment"]
        else:
            ready[name] = min([ready[n] for n in others if n != name] or [ready[name]]) + 300
        if name == "mixture":
            steps += 1
    sp.do(lambda e: e.drain(), outs_ok[-1], sig=None)


def layout(v):
    f = lambda a: np.ascontiguousarray(a)
    A = {}
    A["cst"], A["cst0"], _, own = constants()
    A["own"] = own
    A["x"] = f(v["L0_attn_x"].reshape(NT, P, D).transpose(1, 0, 2))
    A["wqkv0"] = f(v["L0_attn_qkv_w"].T)
    A["b0"] = f(v["L0_attn_qkv_b"].reshape(3, D).T)
    A["bv0"] = f(v["L0_attn_qkv_b"][2 * D:].reshape(1, D))
    A["pb0"] = f(v["L0_attn_proj_b"].reshape(1, D))
    A["pw0"] = f(v["L0_attn_proj_w"].T.reshape(HP, 2, D0, D).transpose(0, 2, 1, 3).reshape(64, 2, D))
    A["wr"], A["br"] = f(v["L0_ffn_Wr"]), f(v["L0_ffn_br"].reshape(1, E0))
    w1 = v["L0_ffn_W1"].reshape(E0 * P, F0)
    w2 = v["L0_ffn_W2"].reshape(E0, 4, P, D).transpose(0, 2, 1, 3).reshape(E0 * P, 4 * D)
    b1 = v["L0_ffn_b1"].reshape(E0, 4, P).transpose(0, 2, 1).reshape(E0 * P, 4)
    A["w12"] = f(np.concatenate([w1, w2, b1], 1))
    A["b2"] = f(v["L0_ffn_b2"])
    pad = lambda a: np.concatenate([a, np.zeros((IW - a.shape[0],) + a.shape[1:], a.dtype)], 0)
    gp = np.concatenate([v["L1_ffn_gate_proj"].reshape(-1, D), v["L1_ffn_shared_gate_w"]], 0)
    up = np.concatenate([v["L1_ffn_up_proj"].reshape(-1, D), v["L1_ffn_shared_up_w"]], 0)
    dn = np.concatenate([v["L1_ffn_down_proj"].transpose(0, 2, 1).reshape(-1, D), v["L1_ffn_shared_down_w"].T], 0)
    A["w_gu"] = f(np.stack([pad(gp).T, pad(up).T], 1))
    A["w_dn"] = f(pad(dn).reshape(IT, P, D).transpose(1, 0, 2))
    for c in "qkv":
        A[f"w_{c}"] = f(v[f"L1_attn_W{c}"].T)
        A[f"b_{c}"] = f(v[f"L1_attn_b{c}"].reshape(1, -1))
    A["w_au"] = f(np.concatenate([v["L1_attn_Wau"].T, v["L1_attn_bau"].reshape(1, -1)], 0))
    A["w_o"] = f(v["L1_attn_Wo"].T.reshape(HP, P, D).transpose(1, 0, 2))
    rows = lambda a: np.concatenate([a, np.zeros((P - a.shape[0],) + a.shape[1:], a.dtype)], 0)
    conv = [np.concatenate([v[f"L1_attn_w{c}_conv"][:, 0, :], v[f"L1_attn_b{c}_conv"][:, None]], 1) for c in "qkv"]
    A["small1"] = f(np.concatenate(conv + [
        v["L1_attn_rms_w"].reshape(HP, P).T, v["L1_attn_Wad"].T, v["L1_attn_Wgd"].T,
        rows(v["L1_attn_bad"][:, None]), rows(v["L1_attn_bgd"][:, None]),
        v["L1_attn_Wbeta"].T, v["L1_ffn_gate_w"].T, rows(np.concatenate([v["L1_attn_Wgu"].T, v["L1_attn_bgu"].reshape(1, -1)], 0))], 1))
    A["smallb"] = f(np.concatenate([v["L1_attn_bbeta"], v["L1_ffn_gate_bias"], v["L1_attn_bo"]]).reshape(1, -1))
    return A


def kernel(**inputs):
    import concourse.bacc as bacc
    from concourse.bass_utils import run_bass_kernel_spmd

    arrays = layout({k: np.asarray(a) for k, a in inputs.items()})
    nc = bacc.Bacc("TRN2", target_bir_lowering=False, num_devices=1)
    feed, ins = {}, {}
    for name, a in arrays.items():
        feed[f"in_{name}"] = a
        ins[name] = nc.dram_tensor(f"in_{name}", a.shape, mybir.dt.from_np(a.dtype), kind="ExternalInput").ap()
    ins["cw_park"] = nc.dram_tensor("cw_park", (96, NT * P), U16).ap()
    out = nc.dram_tensor("out_x", (P, NT, D), F32, kind="ExternalOutput").ap()
    program(nc, ins, out)
    r = run_bass_kernel_spmd(nc, [feed], core_ids=[0])
    y = r.results[0]["out_x"]
    return np.ascontiguousarray(np.asarray(y).reshape(P, NT, D).transpose(1, 0, 2)).reshape(B, T, D)
```
